# Optimizing a Trainium2 kernel written in Bass

```python
import numpy as np
import jax
import jax.numpy as jnp

def _softmax(x, axis=-1):
    return jax.nn.softmax(x, axis=axis)

def _gelu(x):
    return jax.nn.gelu(x, approximate=True)

def _silu(x):
    return jax.nn.silu(x)

def _sigmoid(x):
    return jax.nn.sigmoid(x)

def _layernorm(x, axis=-1, eps=1e-05):
    m = jnp.mean(x, axis=axis, keepdims=True)
    v = jnp.var(x, axis=axis, keepdims=True)
    return (x - m) / jnp.sqrt(v + eps)

def _scatter_add(tgt, idx, src, axis=0):
    return tgt.at[idx].add(src)

def _segment_sum(src, seg, n):
    return jax.ops.segment_sum(src, seg, n)
kernel_name = 'mk_recurrent_d4_jaxref_r8_984bf0'

def setup_inputs(seed: int=0):
    np.random.seed(seed)
    _w = jnp.asarray

    def _L0_attn_setup():
        import jax, jax.numpy as jnp
        import numpy as np
        N_HEAD = 16
        key = jax.random.key(seed)
        ks = jax.random.split(key, 9)
        B, T, C = (4, 256, 128)
        s = 0.02
        return {'x': jax.random.normal(ks[0], (B, T, C), dtype=jnp.float32), 'Wq': jax.random.normal(ks[1], (C, C), dtype=jnp.float32) * s, 'bq': jnp.zeros((C,), dtype=jnp.float32), 'Wk': jax.random.normal(ks[2], (C, C), dtype=jnp.float32) * s, 'bk': jnp.zeros((C,), dtype=jnp.float32), 'Wv': jax.random.normal(ks[3], (C, C), dtype=jnp.float32) * s, 'bv': jnp.zeros((C,), dtype=jnp.float32), 'Wo': jax.random.normal(ks[4], (C, C), dtype=jnp.float32) * s, 'bo': jnp.zeros((C,), dtype=jnp.float32)}
    _L0_attn_in = _L0_attn_setup()

    def _L0_ffn_setup():
        import jax, jax.numpy as jnp
        import numpy as np
        D_MODEL = 128
        key = jax.random.key(seed)
        k_x, k_w, k_a1, k_a2 = jax.random.split(key, 4)
        x = jax.random.normal(k_x, (4, 256, D_MODEL), dtype=jnp.float32)
        weight = jax.random.normal(k_w, (D_MODEL, D_MODEL), dtype=jnp.float32) * 0.02
        aux_weight1 = jax.random.normal(k_a1, (D_MODEL, D_MODEL), dtype=jnp.float32) * 0.02
        aux_weight2 = jax.random.normal(k_a2, (D_MODEL, D_MODEL), dtype=jnp.float32) * 0.02
        bias = jnp.zeros((D_MODEL,), dtype=jnp.float32)
        return {'x': x, 'weight': weight, 'aux_weight1': aux_weight1, 'aux_weight2': aux_weight2, 'bias': bias}
    _L0_ffn_in = _L0_ffn_setup()

    def _L1_attn_setup():
        import jax, jax.numpy as jnp
        import numpy as np
        B, S, D_IN, D_OUT = (4, 256, 128, 128)
        key = jax.random.key(seed)
        ks = jax.random.split(key, 7)
        return {'X': jax.random.normal(ks[0], (B, S, D_IN), dtype=jnp.float32), 'Wq': jax.random.normal(ks[1], (D_IN, D_OUT), dtype=jnp.float32) * (1.0 / np.sqrt(D_IN)), 'bq': jax.random.normal(ks[2], (D_OUT,), dtype=jnp.float32) * 0.02, 'Wk': jax.random.normal(ks[3], (D_IN, D_OUT), dtype=jnp.float32) * (1.0 / np.sqrt(D_IN)), 'bk': jax.random.normal(ks[4], (D_OUT,), dtype=jnp.float32) * 0.02, 'Wv': jax.random.normal(ks[5], (D_IN, D_OUT), dtype=jnp.float32) * (1.0 / np.sqrt(D_IN)), 'bv': jax.random.normal(ks[6], (D_OUT,), dtype=jnp.float32) * 0.02}
    _L1_attn_in = _L1_attn_setup()

    def _L1_ffn_setup():
        import jax, jax.numpy as jnp
        import numpy as np
        H = 128
        E = 32
        I = 64
        TOP_K = 6
        IS = 128
        NORM_MIN = 1e-12
        B, S = (2, 128)
        key = jax.random.key(seed)
        ks = jax.random.split(key, 8)
        sc = 0.02
        return {'hidden_states': jax.random.normal(ks[0], (B, S, H), jnp.float32), 'router_weight': jax.random.normal(ks[1], (E, H), jnp.float32) * sc, 'e_score_bias': jnp.zeros((E,), jnp.float32), 'gate_up_proj': jax.random.normal(ks[2], (E, 2 * I, H), jnp.float32) * sc, 'down_proj': jax.random.normal(ks[3], (E, H, I), jnp.float32) * sc, 'shared_gate_w': jax.random.normal(ks[4], (IS, H), jnp.float32) * sc, 'shared_up_w': jax.random.normal(ks[5], (IS, H), jnp.float32) * sc, 'shared_down_w': jax.random.normal(ks[6], (H, IS), jnp.float32) * sc}
    _L1_ffn_in = _L1_ffn_setup()

    def _L2_attn_setup():
        import jax, jax.numpy as jnp
        import numpy as np
        import math
        DIM = 128
        ATTN_DIM = 128
        B, S = (2, 512)
        key = jax.random.key(seed)
        k1, k2, k3 = jax.random.split(key, 3)
        x = jax.random.normal(k1, (B, S, DIM), dtype=jnp.float32)
        W_qkv = jax.random.normal(k2, (3 * ATTN_DIM, DIM), dtype=jnp.float32) * (1.0 / math.sqrt(DIM))
        b_qkv = jax.random.normal(k3, (3 * ATTN_DIM,), dtype=jnp.float32) * 0.01
        return {'x': x, 'W_qkv': W_qkv, 'b_qkv': b_qkv}
    _L2_attn_in = _L2_attn_setup()

    def _L2_ffn_setup():
        import math
        import jax, jax.numpy as jnp
        import numpy as np
        E = 24

        def layer_norm(x, w, b, eps=1e-06):
            m = x.mean(-1, keepdims=True)
            v = x.var(-1, keepdims=True)
            return (x - m) / jnp.sqrt(v + eps) * w + b

        def top2_dispatch(x, Wg, C):
            logits = x @ Wg
            gates = jax.nn.softmax(logits, axis=-1)
            idx1 = jnp.argmax(gates, axis=-1)
            m1 = jax.nn.one_hot(idx1, E, dtype=x.dtype)
            masked = jnp.where(m1 > 0, -jnp.inf, logits)
            idx2 = jnp.argmax(masked, axis=-1)
            m2 = jax.nn.one_hot(idx2, E, dtype=x.dtype)
            loc1 = jnp.cumsum(m1, axis=0) - m1
            loc2 = jnp.cumsum(m2, axis=0) - m2 + jnp.sum(m1, axis=0, keepdims=True)
            m1 = m1 * (loc1 < C)
            m2 = m2 * (loc2 < C)
            g1 = jnp.sum(gates * m1, axis=-1)
            g2 = jnp.sum(gates * m2, axis=-1)
            denom = jnp.maximum(g1 + g2, 1e-09)
            g1, g2 = (g1 / denom, g2 / denom)
            p1 = jnp.sum(loc1 * m1, axis=-1).astype(jnp.int32)
            p2 = jnp.sum(loc2 * m2, axis=-1).astype(jnp.int32)
            c1 = g1[:, None, None] * m1[:, :, None] * jax.nn.one_hot(p1, C, dtype=x.dtype)[:, None, :]
            c2 = g2[:, None, None] * m2[:, :, None] * jax.nn.one_hot(p2, C, dtype=x.dtype)[:, None, :]
            combine = c1 + c2
            dispatch = (combine > 0).astype(x.dtype)
            return (combine, dispatch)

        def moe_apply(x, combine, dispatch, W, b):
            disp = jnp.einsum('sec,sd->ecd', dispatch, x)
            h = jnp.einsum('ecd,edf->ecf', disp, W) + b[:, None, :]
            return jnp.einsum('sec,ecf->sf', combine, h)
        b, seq, d_in, d_hid = (4, 256, 128, 512)
        ks = jax.random.split(jax.random.key(seed), 6)
        s = 0.02
        return {'x': jax.random.normal(ks[0], (b, seq, d_in), dtype=jnp.float32), 'Wg': jax.random.normal(ks[1], (d_in, E), dtype=jnp.float32) * s, 'W1': jax.random.normal(ks[2], (E, d_in, d_hid), dtype=jnp.float32) * s, 'b1': jnp.zeros((E, d_hid), dtype=jnp.float32), 'W2': jax.random.normal(ks[3], (E, d_hid, d_in), dtype=jnp.float32) * s, 'b2': jnp.zeros((E, d_in), dtype=jnp.float32), 'ln_hid_w': jnp.ones((4, d_hid), dtype=jnp.float32), 'ln_hid_b': jnp.zeros((4, d_hid), dtype=jnp.float32), 'ln_out_w': jnp.ones((d_in,), dtype=jnp.float32), 'ln_out_b': jnp.zeros((d_in,), dtype=jnp.float32)}
    _L2_ffn_in = _L2_ffn_setup()

    def _L3_attn_setup():
        import jax, jax.numpy as jnp
        import numpy as np
        D_MODEL, N_HEADS, BATCH, SEQ = (128, 16, 2, 256)

        def get_freqs(seq, n_dim):
            inv_freq = 1.0 / 10000.0 ** (jnp.arange(0, n_dim, 2, dtype=jnp.float32) / n_dim)
            pos = jnp.arange(seq, dtype=jnp.float32)
            return pos[:, None] * inv_freq[None, :]

        def rope(x, freq):
            cos = jnp.cos(freq)[None, :, None, :]
            sin = jnp.sin(freq)[None, :, None, :]
            x1, x2 = (x[..., ::2], x[..., 1::2])
            r1 = x1 * cos - x2 * sin
            r2 = x1 * sin + x2 * cos
            return jnp.stack([r1, r2], axis=-1).reshape(x.shape)
        key = jax.random.key(seed)
        ks = jax.random.split(key, 5)
        w_scale = 0.01
        return {'x': jax.random.normal(ks[0], (BATCH, SEQ, D_MODEL), dtype=jnp.float32), 'qw': jax.random.normal(ks[1], (D_MODEL, D_MODEL), dtype=jnp.float32) * w_scale, 'kw': jax.random.normal(ks[2], (D_MODEL, D_MODEL), dtype=jnp.float32) * w_scale, 'vw': jax.random.normal(ks[3], (D_MODEL, D_MODEL), dtype=jnp.float32) * w_scale, 'ow': jax.random.normal(ks[4], (D_MODEL, D_MODEL), dtype=jnp.float32) * w_scale}
    _L3_attn_in = _L3_attn_setup()

    def _L3_ffn_setup():
        import jax, jax.numpy as jnp
        import numpy as np
        H, E, DFF = (128, 8, 512)
        key = jax.random.key(seed)
        ks = jax.random.split(key, 7)
        s = lambda *shape: 1.0 / np.sqrt(shape[-2] if len(shape) > 1 else shape[-1])
        x = jax.random.normal(ks[0], (2, 256, H), dtype=jnp.float32)
        Wr = jax.random.normal(ks[1], (H, E), dtype=jnp.float32) * (1.0 / np.sqrt(H))
        br = jnp.zeros((E,), dtype=jnp.float32)
        W1 = jax.random.normal(ks[2], (E, H, DFF), dtype=jnp.float32) * (1.0 / np.sqrt(H))
        b1 = jnp.zeros((E, DFF), dtype=jnp.float32)
        W2 = jax.random.normal(ks[3], (E, DFF, H), dtype=jnp.float32) * (1.0 / np.sqrt(DFF))
        b2 = jnp.zeros((E, H), dtype=jnp.float32)
        return {'x': x, 'Wr': Wr, 'br': br, 'W1': W1, 'b1': b1, 'W2': W2, 'b2': b2}
    _L3_ffn_in = _L3_ffn_setup()
    _d = {'L0_attn_x': _L0_attn_in['x'], 'L0_attn_Wq': _L0_attn_in['Wq'], 'L0_attn_bq': _L0_attn_in['bq'], 'L0_attn_Wk': _L0_attn_in['Wk'], 'L0_attn_bk': _L0_attn_in['bk'], 'L0_attn_Wv': _L0_attn_in['Wv'], 'L0_attn_bv': _L0_attn_in['bv'], 'L0_attn_Wo': _L0_attn_in['Wo'], 'L0_attn_bo': _L0_attn_in['bo'], 'L0_ffn_weight': _L0_ffn_in['weight'], 'L0_ffn_aux_weight1': _L0_ffn_in['aux_weight1'], 'L0_ffn_aux_weight2': _L0_ffn_in['aux_weight2'], 'L0_ffn_bias': _L0_ffn_in['bias'], 'L1_attn_Wq': _L1_attn_in['Wq'], 'L1_attn_bq': _L1_attn_in['bq'], 'L1_attn_Wk': _L1_attn_in['Wk'], 'L1_attn_bk': _L1_attn_in['bk'], 'L1_attn_Wv': _L1_attn_in['Wv'], 'L1_attn_bv': _L1_attn_in['bv'], 'L1_ffn_router_weight': _L1_ffn_in['router_weight'], 'L1_ffn_e_score_bias': _L1_ffn_in['e_score_bias'], 'L1_ffn_gate_up_proj': _L1_ffn_in['gate_up_proj'], 'L1_ffn_down_proj': _L1_ffn_in['down_proj'], 'L1_ffn_shared_gate_w': _L1_ffn_in['shared_gate_w'], 'L1_ffn_shared_up_w': _L1_ffn_in['shared_up_w'], 'L1_ffn_shared_down_w': _L1_ffn_in['shared_down_w'], 'L2_attn_W_qkv': _L2_attn_in['W_qkv'], 'L2_attn_b_qkv': _L2_attn_in['b_qkv'], 'L2_ffn_Wg': _L2_ffn_in['Wg'], 'L2_ffn_W1': _L2_ffn_in['W1'], 'L2_ffn_b1': _L2_ffn_in['b1'], 'L2_ffn_W2': _L2_ffn_in['W2'], 'L2_ffn_b2': _L2_ffn_in['b2'], 'L2_ffn_ln_hid_w': _L2_ffn_in['ln_hid_w'], 'L2_ffn_ln_hid_b': _L2_ffn_in['ln_hid_b'], 'L2_ffn_ln_out_w': _L2_ffn_in['ln_out_w'], 'L2_ffn_ln_out_b': _L2_ffn_in['ln_out_b'], 'L3_attn_qw': _L3_attn_in['qw'], 'L3_attn_kw': _L3_attn_in['kw'], 'L3_attn_vw': _L3_attn_in['vw'], 'L3_attn_ow': _L3_attn_in['ow'], 'L3_ffn_Wr': _L3_ffn_in['Wr'], 'L3_ffn_br': _L3_ffn_in['br'], 'L3_ffn_W1': _L3_ffn_in['W1'], 'L3_ffn_b1': _L3_ffn_in['b1'], 'L3_ffn_W2': _L3_ffn_in['W2'], 'L3_ffn_b2': _L3_ffn_in['b2']}
    _x0 = _d['L0_attn_x']
    _d['L0_attn_x'] = jax.random.normal(jax.random.fold_in(jax.random.key(seed), 1), (1, 2048, 128), dtype=_x0.dtype)
    del _x0
    return _d

def reference(L0_attn_x, L0_attn_Wq, L0_attn_bq, L0_attn_Wk, L0_attn_bk, L0_attn_Wv, L0_attn_bv, L0_attn_Wo, L0_attn_bo, L0_ffn_weight, L0_ffn_aux_weight1, L0_ffn_aux_weight2, L0_ffn_bias, L1_attn_Wq, L1_attn_bq, L1_attn_Wk, L1_attn_bk, L1_attn_Wv, L1_attn_bv, L1_ffn_router_weight, L1_ffn_e_score_bias, L1_ffn_gate_up_proj, L1_ffn_down_proj, L1_ffn_shared_gate_w, L1_ffn_shared_up_w, L1_ffn_shared_down_w, L2_attn_W_qkv, L2_attn_b_qkv, L2_ffn_Wg, L2_ffn_W1, L2_ffn_b1, L2_ffn_W2, L2_ffn_b2, L2_ffn_ln_hid_w, L2_ffn_ln_hid_b, L2_ffn_ln_out_w, L2_ffn_ln_out_b, L3_attn_qw, L3_attn_kw, L3_attn_vw, L3_attn_ow, L3_ffn_Wr, L3_ffn_br, L3_ffn_W1, L3_ffn_b1, L3_ffn_W2, L3_ffn_b2):

    def _L0_attn_ref(x, Wq, bq, Wk, bk, Wv, bv, Wo, bo):
        import jax, jax.numpy as jnp
        import numpy as np
        N_HEAD = 16
        B, T, C = x.shape
        H = N_HEAD
        d = C // H

        def proj(W, b):
            return (x @ W + b).reshape(B, T, H, d).transpose(0, 2, 1, 3)
        q = proj(Wq, bq)
        k = proj(Wk, bk)
        v = proj(Wv, bv)
        scale = jnp.float32(d) ** (-0.5)
        scores = jnp.einsum('bhtd,bhsd->bhts', q, k) * scale
        attn = jax.nn.softmax(scores, axis=-1)
        out = jnp.einsum('bhts,bhsd->bhtd', attn, v)
        out = out.transpose(0, 2, 1, 3).reshape(B, T, C)
        return out @ Wo + bo

    def _L0_ffn_ref(x, weight, aux_weight1, aux_weight2, bias):
        import jax, jax.numpy as jnp
        import numpy as np
        D_MODEL = 128
        h = jnp.einsum('btc,cd->btd', x, weight)
        h = jnp.einsum('btc,cd->btd', h, aux_weight1)
        h = jnp.einsum('btc,cd->btd', h, aux_weight2)
        return jnp.tanh(h + bias)

    def _L1_attn_ref(X, Wq, bq, Wk, bk, Wv, bv):
        import jax, jax.numpy as jnp
        import numpy as np
        B, S, D_IN, D_OUT = (4, 256, 128, 128)
        Q = X @ Wq + bq
        K = X @ Wk + bk
        V = X @ Wv + bv
        dk = jnp.sqrt(jnp.asarray(D_OUT, dtype=X.dtype))
        S_ = jnp.einsum('bqd,bkd->bqk', Q, K)
        S_ = jnp.tril(S_) / dk
        A = jax.nn.softmax(S_, axis=2)
        out = jnp.einsum('bqk,bql->bql', A, V)
        return out

    def _L1_ffn_ref(hidden_states, router_weight, e_score_bias, gate_up_proj, down_proj, shared_gate_w, shared_up_w, shared_down_w):
        import jax, jax.numpy as jnp
        import numpy as np
        H = 128
        E = 32
        I = 64
        TOP_K = 6
        IS = 128
        NORM_MIN = 1e-12
        B, S = (2, 128)
        b, s, h = hidden_states.shape
        x = hidden_states.reshape(-1, h)
        T = x.shape[0]
        shared_out = jax.nn.silu(x @ shared_gate_w.T) * (x @ shared_up_w.T) @ shared_down_w.T
        xf = x.astype(jnp.float32)
        router_logits = xf @ router_weight.T
        routing_weights = jax.nn.softmax(router_logits, axis=-1)
        corrected = routing_weights + e_score_bias
        _, top_idx = jax.lax.top_k(corrected, TOP_K)
        top_w = jnp.take_along_axis(routing_weights, top_idx, axis=-1)
        top_w = top_w / jnp.clip(top_w.sum(axis=-1, keepdims=True), NORM_MIN)
        top_w = top_w.astype(x.dtype)
        combine = jnp.zeros((T, E), x.dtype).at[jnp.arange(T)[:, None], top_idx].add(top_w)
        gu = jnp.einsum('th,eih->tei', x, gate_up_proj)
        gate, up = jnp.split(gu, 2, axis=-1)
        hmid = jax.nn.silu(gate) * up
        y = jnp.einsum('tei,ehi->teh', hmid, down_proj)
        out = jnp.einsum('teh,te->th', y, combine) + shared_out
        return out.reshape(b, s, h)

    def _L2_attn_ref(x, W_qkv, b_qkv):
        import jax, jax.numpy as jnp
        import numpy as np
        import math
        DIM = 128
        ATTN_DIM = 128
        B, S = (2, 512)
        b, s, d = x.shape
        qkv = jnp.einsum('bsd,ed->bse', x, W_qkv) + b_qkv
        q, k, v = jnp.split(qkv, 3, axis=-1)
        score = jnp.einsum('bqd,bkd->bqk', q, k)
        causal = jnp.tril(jnp.ones((s, s), dtype=bool))
        score = jnp.where(causal, score, -jnp.inf)
        attn = jax.nn.softmax(score / math.sqrt(ATTN_DIM), axis=-1)
        y = jnp.einsum('bqk,bkd->bqd', attn, v)
        return y

    def _L2_ffn_ref(x, Wg, W1, b1, W2, b2, ln_hid_w, ln_hid_b, ln_out_w, ln_out_b):
        import math
        import jax, jax.numpy as jnp
        import numpy as np
        E = 24

        def layer_norm(x, w, b, eps=1e-06):
            m = x.mean(-1, keepdims=True)
            v = x.var(-1, keepdims=True)
            return (x - m) / jnp.sqrt(v + eps) * w + b

        def top2_dispatch(x, Wg, C):
            logits = x @ Wg
            gates = jax.nn.softmax(logits, axis=-1)
            idx1 = jnp.argmax(gates, axis=-1)
            m1 = jax.nn.one_hot(idx1, E, dtype=x.dtype)
            masked = jnp.where(m1 > 0, -jnp.inf, logits)
            idx2 = jnp.argmax(masked, axis=-1)
            m2 = jax.nn.one_hot(idx2, E, dtype=x.dtype)
            loc1 = jnp.cumsum(m1, axis=0) - m1
            loc2 = jnp.cumsum(m2, axis=0) - m2 + jnp.sum(m1, axis=0, keepdims=True)
            m1 = m1 * (loc1 < C)
            m2 = m2 * (loc2 < C)
            g1 = jnp.sum(gates * m1, axis=-1)
            g2 = jnp.sum(gates * m2, axis=-1)
            denom = jnp.maximum(g1 + g2, 1e-09)
            g1, g2 = (g1 / denom, g2 / denom)
            p1 = jnp.sum(loc1 * m1, axis=-1).astype(jnp.int32)
            p2 = jnp.sum(loc2 * m2, axis=-1).astype(jnp.int32)
            c1 = g1[:, None, None] * m1[:, :, None] * jax.nn.one_hot(p1, C, dtype=x.dtype)[:, None, :]
            c2 = g2[:, None, None] * m2[:, :, None] * jax.nn.one_hot(p2, C, dtype=x.dtype)[:, None, :]
            combine = c1 + c2
            dispatch = (combine > 0).astype(x.dtype)
            return (combine, dispatch)

        def moe_apply(x, combine, dispatch, W, b):
            disp = jnp.einsum('sec,sd->ecd', dispatch, x)
            h = jnp.einsum('ecd,edf->ecf', disp, W) + b[:, None, :]
            return jnp.einsum('sec,ecf->sf', combine, h)
        bsz, seq, d = x.shape
        H = 4
        n = seq // H
        S = bsz * n
        C = math.ceil(2 * S / E)
        xg = x.reshape(bsz, H, n, d).transpose(1, 0, 2, 3).reshape(H, S, d)

        def per_group(xf, lw, lb):
            combine, dispatch = top2_dispatch(xf, Wg, C)
            h = moe_apply(xf, combine, dispatch, W1, b1)
            h = layer_norm(h, lw, lb)
            h = jax.nn.relu(h)
            return moe_apply(h, combine, dispatch, W2, b2)
        out = jax.vmap(per_group)(xg, ln_hid_w, ln_hid_b)
        out = out.reshape(H, bsz, n, d).transpose(1, 0, 2, 3).reshape(bsz, seq, d)
        return layer_norm(out + x, ln_out_w, ln_out_b)

    def _L3_attn_ref(x, qw, kw, vw, ow):
        import jax, jax.numpy as jnp
        import numpy as np
        D_MODEL, N_HEADS, BATCH, SEQ = (128, 16, 2, 256)

        def get_freqs(seq, n_dim):
            inv_freq = 1.0 / 10000.0 ** (jnp.arange(0, n_dim, 2, dtype=jnp.float32) / n_dim)
            pos = jnp.arange(seq, dtype=jnp.float32)
            return pos[:, None] * inv_freq[None, :]

        def rope(x, freq):
            cos = jnp.cos(freq)[None, :, None, :]
            sin = jnp.sin(freq)[None, :, None, :]
            x1, x2 = (x[..., ::2], x[..., 1::2])
            r1 = x1 * cos - x2 * sin
            r2 = x1 * sin + x2 * cos
            return jnp.stack([r1, r2], axis=-1).reshape(x.shape)
        batch, seq, dim = x.shape
        n_heads = N_HEADS
        n_dim = dim // n_heads
        Q = (x @ qw).astype(jnp.float32).reshape(batch, seq, n_heads, n_dim)
        K = (x @ kw).astype(jnp.float32).reshape(batch, seq, n_heads, n_dim)
        V = (x @ vw).astype(jnp.float32).reshape(batch, seq, n_heads, n_dim)
        freq = get_freqs(seq, n_dim)
        Q = rope(Q, freq)
        K = rope(K, freq)
        Q = jnp.transpose(Q, (0, 2, 1, 3))
        K = jnp.transpose(K, (0, 2, 1, 3))
        V = jnp.transpose(V, (0, 2, 1, 3))
        scale = jnp.sqrt(jnp.float32(n_dim))
        score = jnp.einsum('bhqd,bhkd->bhqk', Q, K) / scale
        causal = jnp.tril(jnp.ones((1, 1, seq, seq), dtype=jnp.float32))
        score = score - 10000000000.0 * (1.0 - causal)
        score = score - jnp.max(score, axis=-1, keepdims=True)
        weights = jax.nn.softmax(score, axis=-1)
        attn = jnp.einsum('bhqk,bhkd->bhqd', weights, V)
        merged = jnp.transpose(attn, (0, 2, 1, 3)).reshape(batch, seq, dim)
        return (merged @ ow).astype(x.dtype)

    def _L3_ffn_ref(x, Wr, br, W1, b1, W2, b2):
        import jax, jax.numpy as jnp
        import numpy as np
        H, E, DFF = (128, 8, 512)
        B, S, Hd = x.shape
        n_exp = W1.shape[0]
        xt = x.reshape(-1, Hd)
        logits = xt @ Wr + br
        probs = jax.nn.softmax(logits, axis=-1)
        gate = jnp.max(probs, axis=-1)
        idx = jnp.argmax(probs, axis=-1)
        h1 = jnp.maximum(jnp.einsum('th,ehf->etf', xt, W1) + b1[:, None, :], 0.0)
        ye = jnp.einsum('etf,efh->eth', h1, W2) + b2[:, None, :]
        onehot = jax.nn.one_hot(idx, n_exp, dtype=xt.dtype)
        y = jnp.einsum('te,eth->th', onehot, ye) * gate[:, None]
        return y.reshape(B, S, Hd)
    x = L0_attn_x
    xn = _layernorm(x, axis=-1)
    s = _L0_attn_ref(xn, L0_attn_Wq, L0_attn_bq, L0_attn_Wk, L0_attn_bk, L0_attn_Wv, L0_attn_bv, L0_attn_Wo, L0_attn_bo)
    g = _silu(_L0_ffn_ref(xn, L0_ffn_weight, L0_ffn_aux_weight1, L0_ffn_aux_weight2, L0_ffn_bias))
    x = x + s * g
    xn = _layernorm(x, axis=-1)
    s = _L1_attn_ref(xn, L1_attn_Wq, L1_attn_bq, L1_attn_Wk, L1_attn_bk, L1_attn_Wv, L1_attn_bv)
    g = _silu(_L1_ffn_ref(xn, L1_ffn_router_weight, L1_ffn_e_score_bias, L1_ffn_gate_up_proj, L1_ffn_down_proj, L1_ffn_shared_gate_w, L1_ffn_shared_up_w, L1_ffn_shared_down_w))
    x = x + s * g
    xn = _layernorm(x, axis=-1)
    s = _L2_attn_ref(xn, L2_attn_W_qkv, L2_attn_b_qkv)
    g = _silu(_L2_ffn_ref(xn, L2_ffn_Wg, L2_ffn_W1, L2_ffn_b1, L2_ffn_W2, L2_ffn_b2, L2_ffn_ln_hid_w, L2_ffn_ln_hid_b, L2_ffn_ln_out_w, L2_ffn_ln_out_b))
    x = x + s * g
    xn = _layernorm(x, axis=-1)
    s = _L3_attn_ref(xn, L3_attn_qw, L3_attn_kw, L3_attn_vw, L3_attn_ow)
    g = _silu(_L3_ffn_ref(xn, L3_ffn_Wr, L3_ffn_br, L3_ffn_W1, L3_ffn_b1, L3_ffn_W2, L3_ffn_b2))
    x = x + s * g
    return x

_drawn_inputs = setup_inputs


def setup_inputs(seed=0):
    import zlib

    import numpy as np

    out = dict(_drawn_inputs(seed))
    spreads = {'L0_attn_bq': (0.0, 0.8),
     'L0_attn_bk': (0.0, 2.0),
     'L0_attn_bv': (0.0, 0.8),
     'L0_attn_bo': (0.0, 0.8),
     'L0_ffn_bias': (0.0, 0.8),
     'L1_ffn_e_score_bias': (0.0, 0.8),
     'L2_ffn_b1': (0.0, 2.0),
     'L2_ffn_b2': (0.0, 2.0),
     'L2_ffn_ln_hid_w': (1.0, 0.6),
     'L2_ffn_ln_hid_b': (0.0, 2.0),
     'L2_ffn_ln_out_w': (1.0, 0.6),
     'L2_ffn_ln_out_b': (0.0, 2.0),
     'L3_ffn_br': (0.0, 0.8),
     'L3_ffn_b1': (0.0, 2.0),
     'L3_ffn_b2': (0.0, 2.0)}
    factors = {'L0_attn_Wq': 8.0,
     'L0_attn_Wk': 8.0,
     'L0_attn_Wv': 8.0,
     'L0_attn_Wo': 8.0,
     'L0_ffn_weight': 8.0,
     'L0_ffn_aux_weight1': 8.0,
     'L0_ffn_aux_weight2': 8.0,
     'L1_attn_Wq': 200.0,
     'L1_attn_bq': 200.0,
     'L1_attn_Wk': 200.0,
     'L1_attn_bk': 200.0,
     'L1_attn_Wv': 8.0,
     'L1_attn_bv': 8.0,
     'L1_ffn_router_weight': 8.0,
     'L1_ffn_gate_up_proj': 8.0,
     'L1_ffn_down_proj': 8.0,
     'L1_ffn_shared_gate_w': 8.0,
     'L1_ffn_shared_up_w': 8.0,
     'L1_ffn_shared_down_w': 8.0,
     'L2_attn_b_qkv': 64.0,
     'L2_ffn_W1': 23.64,
     'L3_attn_qw': 8.0,
     'L3_attn_kw': 8.0,
     'L3_attn_vw': 8.0,
     'L3_attn_ow': 8.0,
     'L3_ffn_Wr': 8.0,
     'L3_ffn_W1': 8.0,
     'L3_ffn_W2': 8.0,
     'L2_attn_W_qkv': 5.02,
     'L2_ffn_Wg': 8.0,
     'L2_ffn_W2': 8.0}
    for name, (base, spread) in spreads.items():
        noise = np.random.default_rng([zlib.crc32(name.encode()), seed]).standard_normal(out[name].shape)
        drawn = base * np.exp(spread * noise) if base else spread * noise
        out[name] = jnp.asarray(drawn.astype(out[name].dtype))
    for name, factor in factors.items():
        out[name] = (out[name] * factor).astype(out[name].dtype)
    return out
```

```python
from contextlib import ExitStack

import concourse.bass as bass
import numpy as np
from concourse import mybir

F32, BF16, I32 = mybir.dt.float32, mybir.dt.bfloat16, mybir.dt.int32
ALU, ACT, AX = mybir.AluOpType, mybir.ActivationFunctionType, mybir.AxisListType

T = 2048
D = 128
P = 128
NT = T // P
BLK = 512
NB = T // BLK
TPB = BLK // P
HEADS = 16
HD = D // HEADS
PARTS = 3
STK = PARTS * PARTS * HD
VW = 32
LN_EPS = 1e-5
NEG = -1e30
LOWEST = -3e38
RSQRT_SEED = float(0x5F3759DF)


class Kept:
    pass


class Chain:

    def __init__(self, engine, sem):
        self.engine, self.sem, self.n = engine, sem, 0

    def __call__(self, ins):
        self.n += 1
        ins.then_inc(self.sem, 1)
        self.engine.wait_ge(self.sem, self.n)


class Stage:

    def __init__(self, nc, tag):
        self.nc, self.tag, self.ctx, self.sems = nc, tag, ExitStack(), []

    def __enter__(self):
        return self

    def __exit__(self, *said):
        done = self.ctx.__exit__(*said)
        self.nc.clear_and_free_semaphores(self.sems)
        self.nc.all_engine_barrier()
        return done

    def sb(self, name, shape, dt=F32):
        return self.ctx.enter_context(self.nc.sbuf_tensor(f"{self.tag}_{name}", list(shape), dt))

    def ps(self, name, shape, dt=F32):
        return self.ctx.enter_context(self.nc.psum_tensor(f"{self.tag}_{name}", list(shape), dt))

    def sem(self, name):
        sem = self.nc.alloc_semaphore(f"{self.tag}_{name}")
        self.sems.append(sem)
        return sem

    def block(self):
        return self.ctx.enter_context(self.nc.Block())


def rsqrt(dve, chain, y, v, t):
    chain(dve.tensor_scalar(t.bitcast(I32), v.bitcast(I32), 1, None, ALU.logical_shift_right))
    chain(dve.tensor_scalar(y.bitcast(I32), t.bitcast(I32), -1.0, RSQRT_SEED, ALU.mult, ALU.add))
    for _ in range(3):
        chain(dve.tensor_tensor(t, y, y, ALU.mult))
        chain(dve.tensor_tensor(t, t, v, ALU.mult))
        chain(dve.tensor_scalar(t, t, -0.5, 1.5, ALU.mult, ALU.add))
        chain(dve.tensor_tensor(y, y, t, ALU.mult))


def load_constants(nc, K, A):
    with Stage(nc, "load") as S:
        loaded, made = S.sem("loaded"), S.sem("made")
        small = S.sb("small", [P, 4, P])
        loads = [(K.x[:, :, :], A["x"].rearrange("(t p) d -> p t d", p=P)),
                 (K.ident[:, :], A["c_ident"]), (K.iota[:, :], A["c_iota"]),
                 (K.floor[:, :], A["c_floor"]), (K.after[:, :], A["c_after"]),
                 (K.wr1[:, :], A["wr1"]), (K.wg2[:, :], A["wg2"]), (K.wr3[:, :], A["wr3"])]
        loads += [(small[:, n, :], A[c]) for n, c in enumerate(("c_ident", "c_above", "c_below", "c_ones"))]
        loads += [(K.w[n][:, :], A[n]) for n in K.w]
        loads += [(K.col[n][:, :], A[n].rearrange("(p o) -> p o", o=1)) for n in K.col]
        loads += [(K.row[n][:, :], A[n].partition_broadcast(P)) for n in K.row]
        block = S.block()

        @block.sync
        def _(sp):
            with nc.allow_non_contiguous_dma(reason="bias columns"):
                for dst, src in loads:
                    sp.dma_start(dst, src).then_inc(loaded, 16)
            for dst, n in ((K.gate1, "gate1"), (K.up1, "up1"), (K.sgate1, "sgate1"), (K.sup1, "sup1"),
                           (K.sdown1, "sdown1")):
                sp.dma_start(dst[:, :], A[n]).then_inc(K.l1_loaded, 16)
            sp.dma_start(K.down1[:, :, :], A["down1"]).then_inc(K.l1_loaded, 16)
            sp.dma_start(K.w1_3[:, :, :], A["w1_3"]).then_inc(K.l3_loaded, 16)
            sp.dma_start(K.w2_3[:, :, :, :], A["w2_3"]).then_inc(K.l3_loaded, 16)
            sp.wait_ge(loaded, 16 * len(loads))

        @block.vector
        def _(dve):
            dve.wait_ge(loaded, 16 * len(loads))
            dve.tensor_copy(K.ident_b[:, :], small[:, 0, :]).then_inc(made, 1)
            dve.tensor_copy(K.above_b[:, :], small[:, 1, :]).then_inc(made, 1)
            dve.tensor_copy(K.ones_b[:, :], small[:, 3, :]).then_inc(made, 1)
            dve.tensor_scalar(K.neg_above[:, :], small[:, 1, :], NEG, None, ALU.mult).then_inc(made, 1)
            dve.tensor_scalar(K.neg_below[:, :], small[:, 2, :], NEG, None, ALU.mult).then_inc(made, 1)


def residual_and_norm(nc, K, layer):
    with Stage(nc, f"norm{layer}") as S:
        stats, mv = S.sb("stats", [P, NT, 6]), S.sb("mv", [P, NT, 2])
        var, rstd, tmp = S.sb("var", [P, NT]), S.sb("rstd", [P, NT]), S.sb("tmp", [P, NT])
        pT = S.ps("pT", [P, 2, BLK])
        order, gated, normed, turned, kept = (S.sem(n) for n in ("order", "gated", "normed", "turned", "kept"))
        gate = S.sb("gate", [P, NT, D]) if layer else None
        block = S.block()

        @block.scalar
        def _(act):
            if layer:
                for c in range(NB):
                    act.activation(gate[:, c * TPB:(c + 1) * TPB, :], K.g[:, c * TPB:(c + 1) * TPB, :],
                                   ACT.Silu).then_inc(gated, 1)
            for c in range(NB):
                act.wait_ge(turned, c + 1)
                act.activation(K.xnT[:, c * BLK:(c + 1) * BLK], pT[:, c % 2, :], ACT.Copy).then_inc(kept, 1)

        @block.vector
        def _(dve):
            chain = Chain(dve, order)
            if layer:
                for c in range(NB):
                    ts = slice(c * TPB, (c + 1) * TPB)
                    dve.wait_ge(gated, c + 1)
                    chain(dve.tensor_tensor(gate[:, ts, :], gate[:, ts, :], K.s[:, ts, :], ALU.mult))
                    chain(dve.tensor_tensor(K.x[:, ts, :], K.x[:, ts, :], gate[:, ts, :], ALU.add))
            for t in range(NT):
                last = dve.bn_stats(stats[:, t, :], K.x[:, t, :])
            chain(last)
            for t in range(NT):
                last = dve.bn_aggr(mv[:, t, :], stats[:, t, :])
            chain(last)
            chain(dve.tensor_scalar(var[:, :], mv[:, :, 1], LN_EPS, None, ALU.add))
            rsqrt(dve, chain, rstd[:, :], var[:, :], tmp[:, :])
            for t in range(NT):
                dve.tensor_scalar(K.xn[:, t, :], K.x[:, t, :], mv[:, t, 0:1], rstd[:, t:t + 1],
                                  ALU.subtract, ALU.mult).then_inc(normed, 1)

        @block.tensor
        def _(pe):
            for t in range(NT):
                if t % TPB == 0 and t >= 2 * TPB:
                    pe.wait_ge(kept, t // TPB - 1)
                pe.wait_ge(normed, t + 1)
                mm = pe.transpose(pT[:, t // TPB % 2, t % TPB * P:(t % TPB + 1) * P], K.xn[:, t, :], K.ident[:, :])
                if t % TPB == TPB - 1:
                    mm.then_inc(turned, 1)


def store_result(nc, K, out):
    with Stage(nc, "store") as S:
        gate = S.sb("gate", [P, NT, D])
        gated, order, summed, stored = (S.sem(n) for n in ("gated", "order", "summed", "stored"))
        block = S.block()
        out_rows = out.rearrange("(t p) d -> p t d", p=P)

        @block.scalar
        def _(act):
            for c in range(NB):
                act.activation(gate[:, c * TPB:(c + 1) * TPB, :], K.g[:, c * TPB:(c + 1) * TPB, :],
                               ACT.Silu).then_inc(gated, 1)

        @block.vector
        def _(dve):
            chain = Chain(dve, order)
            for c in range(NB):
                ts = slice(c * TPB, (c + 1) * TPB)
                dve.wait_ge(gated, c + 1)
                chain(dve.tensor_tensor(gate[:, ts, :], gate[:, ts, :], K.s[:, ts, :], ALU.mult))
                dve.tensor_tensor(K.x[:, ts, :], K.x[:, ts, :], gate[:, ts, :], ALU.add).then_inc(summed, 1)

        @block.sync
        def _(sp):
            for c in range(NB):
                ts = slice(c * TPB, (c + 1) * TPB)
                sp.wait_ge(summed, c + 1)
                sp.dma_start(out_rows[:, ts, :], K.x[:, ts, :]).then_inc(stored, 16)
            sp.wait_ge(stored, 16 * NB)


def head_projections(nc, K, layer, wq, wk, wv, bq=None, bk=None, bv=None, rope=None):
    with Stage(nc, f"proj{layer}") as S:
        ws = [(wq, bq), (wk, bk)]
        scale = float(np.float32(HD) ** np.float32(-0.5))
        full = S.sb("full", [P, 4, BLK])
        rest = S.sb("rest", [P, 4, BLK])
        parts = [[S.sb(f"part{w}{a}", [P, T], BF16) for a in range(PARTS)] for w in range(2)]
        pq = S.ps("pq", [P, 4, BLK])
        pv = S.ps("pv", [P, 2, BLK])
        swp = S.sb("swp", [P, 4, BLK]) if rope else None
        cos = S.sb("cos", [P, T]) if rope else None
        sin = S.sb("sin", [P, T]) if rope else None
        ps_swap = S.ps("ps_swap", [P, 2, BLK]) if rope else None
        bias = S.sb("bias", [P, 1]) if bq is not None else None
        (projected, vproj, taken, vkept, biased, order, whole, hi, r1, mid, lo, stored, tables) = (
            S.sem(n) for n in ("projected", "vproj", "taken", "vkept", "biased", "order", "whole", "hi", "r1", "mid",
                               "lo", "stored", "tables"))
        block = S.block()
        N = 2 * NB
        out_of_psum = whole if rope else taken

        @block.sync
        def _(sp):
            if rope:
                sp.dma_start(cos[:, :], rope[2]).then_inc(tables, 16)
                sp.dma_start(sin[:, :], rope[3]).then_inc(tables, 16)
            for w in range(2):
                for a, done in enumerate((hi, mid, lo)):
                    sp.wait_ge(done, NB * (w + 1))
                    sp.dma_start(K.parts[w][:, a, :, :], parts[w][a][:, :]).then_inc(stored, 16)
            sp.wait_ge(stored, 16 * 2 * PARTS)

        @block.tensor
        def _(pe):
            for n in range(N):
                w, b = divmod(n, NB)
                if n >= 4:
                    pe.wait_ge(out_of_psum, n - 3)
                mm = pe.matmul(pq[:, n % 4, :], ws[w][0][:, :], K.xnT[:, b * BLK:(b + 1) * BLK], start=True, stop=True)
                if rope:
                    if n >= 2:
                        pe.wait_ge(out_of_psum, n - 1)
                    mm = pe.matmul(ps_swap[:, n % 2, :], rope[w][:, :], K.xnT[:, b * BLK:(b + 1) * BLK],
                                   start=True, stop=True)
                mm.then_inc(projected, 1)
            for t in range(NT):
                if t % TPB == 0 and t >= 2 * TPB:
                    pe.wait_ge(vkept, t // TPB - 1)
                mm = pe.matmul(pv[:, t // TPB % 2, t % TPB * P:(t % TPB + 1) * P], K.xnT[:, t * P:(t + 1) * P],
                               wv[:, :], start=True, stop=True)
                if t % TPB == TPB - 1:
                    mm.then_inc(vproj, 1)

        @block.scalar
        def _(act):
            if bq is not None:
                act.mul(bias[:, :], bq[:, :], scale).then_inc(biased, 1)
                act.wait_ge(biased, 1)
            for n in range(N):
                w, b = divmod(n, NB)
                cols = slice(b * BLK, (b + 1) * BLK)
                if not rope:
                    act.wait_ge(projected, n + 1)
                    if n >= 4:
                        act.wait_ge(r1, n - 3)
                    b_w = (bias, bk)[w][:, :] if bq is not None else 0.0
                    act.activation(full[:, n % 4, :], pq[:, n % 4, :], ACT.Identity, bias=b_w,
                                   scale=scale if w == 0 else 1.0).then_inc(taken, 1)
                    act.wait_ge(taken, n + 1)
                else:
                    act.wait_ge(whole, n + 1)
                act.activation(parts[w][0][:, cols], full[:, n % 4, :], ACT.Copy).then_inc(hi, 1)
                act.wait_ge(r1, n + 1)
                act.activation(parts[w][1][:, cols], rest[:, n % 4, :], ACT.Copy).then_inc(mid, 1)

        @block.vector
        def _(dve):
            chain = Chain(dve, order)
            if rope:
                dve.wait_ge(tables, 32)
            for n in range(N):
                w, b = divmod(n, NB)
                cols = slice(b * BLK, (b + 1) * BLK)
                if rope:
                    dve.wait_ge(projected, n + 1)
                    chain(dve.tensor_tensor(swp[:, n % 4, :], ps_swap[:, n % 2, :], sin[:, cols], ALU.mult))
                    chain(dve.tensor_tensor(full[:, n % 4, :], pq[:, n % 4, :], cos[:, cols], ALU.mult))
                    turned = dve.tensor_tensor(full[:, n % 4, :], full[:, n % 4, :], swp[:, n % 4, :], ALU.add)
                    if w == 0:
                        chain(turned)
                        turned = dve.tensor_scalar(full[:, n % 4, :], full[:, n % 4, :], scale, None, ALU.mult)
                    turned.then_inc(whole, 1)
                dve.wait_ge(hi, n + 1)
                dve.tensor_tensor(rest[:, n % 4, :], full[:, n % 4, :], parts[w][0][:, cols],
                                  ALU.subtract).then_inc(r1, 1)
                dve.wait_ge(mid, n + 1)
                dve.tensor_tensor(parts[w][2][:, cols], rest[:, n % 4, :], parts[w][1][:, cols],
                                  ALU.subtract).then_inc(lo, 1)
            for c in range(NB):
                dve.wait_ge(vproj, c + 1)
                src = pv[:, c % 2, :].rearrange("p (t d) -> p t d", d=D)
                dst = K.v[:, c * TPB:(c + 1) * TPB, :]
                if bv is not None:
                    dve.tensor_tensor(dst, src, bv[:, :].unsqueeze(1).broadcast_to([P, TPB, D]), ALU.add)\
                       .then_inc(vkept, 1)
                else:
                    dve.tensor_copy(dst, src).then_inc(vkept, 1)


def causal_plan(causal):
    units, runs = [], []
    for u in range(NT):
        lo = u * P if causal else 0
        halves = []
        for a in range(2):
            cols = [(b, max(b * BLK, lo), (b + 1) * BLK) for b in (2 * a, 2 * a + 1) if (b + 1) * BLK > lo]
            if cols:
                halves.append((a, cols))
        units.append(halves)
    for i in range(NT):
        hi = (i + 1) * P if causal else T
        runs += [(i, b, min(BLK, hi - b * BLK), causal and hi <= (b + 1) * BLK) for b in range(NB) if b * BLK < hi]
    return units, runs


def attention_heads(nc, K, layer, causal):
    units, runs = causal_plan(causal)
    NR = len(runs)
    chunks = [(u, a, cols) for u, halves in enumerate(units) for a, cols in halves]
    NC = len(chunks)
    first_chunk = [min(n for n, c in enumerate(chunks) if c[0] == u) for u in range(NT)] + [NC]
    PER = -(-NR // 13)
    runs_of = [[]] + [list(range(PER * k, min(NR, PER * (k + 1)))) for k in range(13)] + [[], []]
    TURN_SLOT = NR % 3
    with Stage(nc, f"heads{layer}") as S:
        qs = [S.sb(f"qs{i}", [P, T], BF16) for i in range(2)]
        ks = [S.sb(f"ks{i}", [P, T], BF16) for i in range(2)]
        vh = [S.sb(f"vh{i}", [P, NT, VW]) for i in range(2)]
        probs = [S.sb(f"probs{i}", [P, T]) for i in range(2)]
        ot = [S.sb(f"ot{i}", [P, BLK]) for i in range(2)]
        run_max = S.sb("run_max", [P, NT, NB])
        neg_max = S.sb("neg_max", [P, NT])
        left = S.sb("left", [P, NT])
        max_parts = S.sb("max_parts", [P, P // NT, NT], BF16)
        max_rows = S.sb("max_rows", [PARTS * NT, P], BF16)
        pS = S.ps("pS", [P, 2, 2 * BLK])
        pM = S.ps("pM", [P, 3, BLK])
        pO = S.ps("pO", [P, BLK])
        (stacked, preset, scored, exped, seen, maxed, splitting, split, turned, rowed, rows_in, v_in, used, ot_kept,
         zeroed) = (S.sem(n) for n in (
             "stacked", "preset", "scored", "exped", "seen", "maxed", "splitting", "split", "turned", "rowed",
             "rows_in", "v_in", "used", "ot_kept", "zeroed"))
        ot_stored = [S.sem(f"ot_stored{i}") for i in range(2)]
        v_heads = K.v[:, :, :].rearrange("p t (h two d) -> p t h two d", two=2, d=HD)
        part_heads = [K.parts[w].rearrange("(h two) a d t -> h two a d t", two=2) for w in range(2)]
        out_heads = K.head_out.rearrange("(h two) r t -> h two r t", two=2)
        block = S.block()
        LOADS = 6

        def head(p, par):
            return 2 * p + par

        @block.sync
        def _(sp):
            def load_stacks(p, par):
                for r in range(PARTS):
                    rows = slice(r * PARTS * HD, (r + 1) * PARTS * HD)
                    sp.dma_start(qs[par][rows, :], part_heads[0][p, par].rearrange("a d t -> (a d) t"))\
                      .then_inc(stacked, 16)
                    sp.dma_start(ks[par][rows, :],
                                 part_heads[1][p, par, r].unsqueeze(0).broadcast_to([PARTS, HD, T]))\
                      .then_inc(stacked, 16)

            def load_max_rows(par):
                for a in range(PARTS):
                    sp.dma_start(qs[par][STK + a:STK + a + 1, :].rearrange("o (t c) -> o t c", c=P),
                                 max_rows[a * NT:(a + 1) * NT, :]).then_inc(rows_in, 16)

            def one_head(p, par, last):
                h = head(p, par)
                if not last:
                    nxt = (p, 1) if par == 0 else (p + 1, 0)
                    sp.wait_ge(scored, NC * h + 1)
                    load_stacks(*nxt)
                    sp.wait_ge(rowed, h + 2)
                    load_max_rows(1 - par)

            sp.wait_ge(preset, 1)
            load_stacks(0, 0)
            sp.wait_ge(rowed, 1)
            load_max_rows(0)
            with sp.Fori(0, HEADS // 2 - 1) as p:
                one_head(p, 0, False)
                one_head(p, 1, False)
            one_head(HEADS // 2 - 1, 0, False)

        @block.gpsimd
        def _(pool):
            def take_v(p, par):
                pool.tensor_copy(vh[par][:, :, 0:HD], v_heads[:, :, p, par, :]).then_inc(v_in, 1)

            def store(p, par):
                pool.wait_ge(ot_kept, head(p, par) + 2)
                for b in range(NB):
                    pool.dma_start(out_heads[p, par, :, b * BLK:(b + 1) * BLK],
                                   ot[par][b * 32:b * 32 + HD + 1, :]).then_inc(ot_stored[par], 16)

            def one_head(p, par, last):
                if not last:
                    pool.wait_ge(used, NT * head(p, par) + 2)
                    take_v(*((p, 1) if par == 0 else (p + 1, 0)))
                store(p, par)

            pool.wait_ge(preset, 2)
            take_v(0, 0)
            with pool.Fori(0, HEADS // 2 - 1) as p:
                one_head(p, 0, False)
                one_head(p, 1, False)
            one_head(HEADS // 2 - 1, 0, False)
            one_head(HEADS // 2 - 1, 1, True)
            for par in range(2):
                pool.wait_ge(ot_stored[par], 16 * NB * (HEADS // 2))

        @block.tensor
        def _(pe):
            def score_run(g, par, m):
                i, b, w, masked = runs[m]
                if m >= 3:
                    pe.wait_ge(maxed, NR * g + m - 2)
                elif not isinstance(g, int) or g > 0:
                    pe.wait_ge(rowed, g)
                mm = pe.matmul(pM[:, m % 3, 0:w], qs[par][0:STK, i * P:(i + 1) * P],
                               ks[par][0:STK, b * BLK:b * BLK + w], start=True, stop=not masked)
                if masked:
                    mm = pe.matmul(pM[:, m % 3, w - P:w], K.ident_b[:, :], K.neg_above[:, :], start=False, stop=True)
                mm.then_inc(seen, 1)

            def turn_max(g):
                pe.wait_ge(split, g + 1)
                pe.transpose(pM[:, TURN_SLOT, :].bitcast(BF16)[:, 0:P], max_parts[:, :, :].rearrange("p a t -> p (a t)"),
                             K.ident_b[:, :]).then_inc(turned, 1)

            def score_unit(h, par, u):
                if u == 0:
                    pe.wait_ge(rows_in, 16 * PARTS * (h + 1))
                for n in range(first_chunk[u], first_chunk[u + 1]):
                    _, _, cols = chunks[n]
                    if not isinstance(h, int) or h > 0 or n >= 2:
                        pe.wait_ge(exped, NC * h + n - 1)
                    for b, c0, c1 in cols:
                        o = c0 % (2 * BLK)
                        diag = causal and c0 == u * P
                        mm = pe.matmul(pS[:, n % 2, o:o + c1 - c0], ks[par][0:STK + PARTS, u * P:(u + 1) * P],
                                       qs[par][0:STK + PARTS, c0:c1], start=True, stop=not diag)
                        if diag:
                            mm = pe.matmul(pS[:, n % 2, o:o + P], K.ident_b[:, :], K.neg_below[:, :],
                                           start=False, stop=True)
                    mm.then_inc(scored, 1)

            def sum_unit(h, par, u):
                pe.wait_ge(exped, NC * h + first_chunk[u + 1])
                if u == 0:
                    pe.wait_ge(v_in, h + 1)
                    pe.wait_ge(ot_kept, h + 1)
                for _, cols in units[u]:
                    for b, c0, c1 in cols:
                        mm = pe.matmul(pO[b * 32:b * 32 + VW, c0 - b * BLK:c1 - b * BLK], vh[par][:, u, :],
                                       probs[u % 2][:, c0:c1], start=(u == 0),
                                       stop=(u == (4 * b + 3 if causal else NT - 1)))
                mm.then_inc(used, 1)

            def one_head(p, par, last):
                h = head(p, par)
                for u in range(NT):
                    if u < NT - 1:
                        score_unit(h, par, u + 1)
                    if not last:
                        if u == 1:
                            pe.wait_ge(stacked, 16 * LOADS * (h + 2))
                        for m in runs_of[u]:
                            score_run(h + 1, 1 - par, m)
                    sum_unit(h, par, u)
                    if not last and u == NT - 2:
                        turn_max(h + 1)
                if not last:
                    score_unit(h + 1, 1 - par, 0)

            pe.wait_ge(preset, 2)
            pe.wait_ge(stacked, 16 * LOADS)
            for m in range(NR):
                score_run(0, 0, m)
            turn_max(0)
            score_unit(0, 0, 0)
            with pe.Fori(0, HEADS // 2 - 1) as p:
                one_head(p, 0, False)
                one_head(p, 1, False)
            one_head(HEADS // 2 - 1, 0, False)
            one_head(HEADS // 2 - 1, 1, True)

        @block.scalar
        def _(act):
            def one_head(p, par):
                h = head(p, par)
                for n, (u, a, cols) in enumerate(chunks):
                    act.wait_ge(scored, NC * h + n + 1)
                    act.wait_ge(used, NT * h + u + 1)
                    c0, c1 = cols[0][1], cols[-1][2]
                    o = c0 % (2 * BLK)
                    act.activation(probs[u % 2][:, c0:c1], pS[:, n % 2, o:o + c1 - c0], ACT.Exp).then_inc(exped, 1)

            with act.Fori(0, HEADS // 2) as p:
                one_head(p, 0)
                one_head(p, 1)

        @block.vector
        def _(dve):
            def run_maxima(g):
                for m, (i, b, w, _) in enumerate(runs):
                    dve.wait_ge(seen, NR * g + m + 1)
                    dve.reduce_max(run_max[:, i, b:b + 1], pM[:, m % 3, 0:w], AX.X).then_inc(maxed, 1)

            def split_max(g):
                dve.wait_ge(maxed, NR * (g + 1))
                dve.tensor_reduce(neg_max[:, :], run_max[:, :, :], AX.X, ALU.max, negate=True).then_inc(splitting, 1)
                dve.wait_ge(splitting, 4 * g + 1)
                dve.tensor_copy(max_parts[:, 0, :], neg_max[:, :]).then_inc(splitting, 1)
                dve.wait_ge(splitting, 4 * g + 2)
                dve.tensor_tensor(left[:, :], neg_max[:, :], max_parts[:, 0, :], ALU.subtract).then_inc(splitting, 1)
                dve.wait_ge(splitting, 4 * g + 3)
                dve.tensor_copy(max_parts[:, 1, :], left[:, :]).then_inc(splitting, 1)
                dve.wait_ge(splitting, 4 * g + 4)
                dve.tensor_tensor(max_parts[:, 2, :], left[:, :], max_parts[:, 1, :], ALU.subtract).then_inc(split, 1)
                dve.wait_ge(turned, g + 1)
                if not isinstance(g, int) or g > 0:
                    dve.wait_ge(rows_in, 16 * PARTS * g)
                dve.tensor_copy(max_rows[:, :], pM[:, TURN_SLOT, :].bitcast(BF16)[0:PARTS * NT, 0:P])\
                   .then_inc(rowed, 1)

            def keep_sums(p, par):
                h = head(p, par)
                dve.wait_ge(used, NT * (h + 1) + 2)
                if not isinstance(p, int) or p > 0:
                    dve.wait_ge(ot_stored[par], 16 * NB * p)
                dve.tensor_copy(ot[par][:, :], pO[:, :]).then_inc(ot_kept, 1)

            def one_head(p, par, last):
                if not last:
                    run_maxima(head(p, par) + 1)
                    split_max(head(p, par) + 1)
                keep_sums(p, par)

            for i in range(2):
                dve.memset(ks[i][64:96, :], 1.0)
            dve.memset(max_parts[:, PARTS:, :], 0.0)
            dve.memset(run_max[:, :, :], LOWEST).then_inc(preset, 1)
            for i in range(2):
                dve.memset(vh[i][:, :, HD:VW], 0.0).then_inc(zeroed, 1)
            dve.wait_ge(zeroed, 2)
            for i in range(2):
                last = dve.memset(vh[i][:, :, HD:HD + 1], 1.0)
            last.then_inc(preset, 1)
            dve.engine_nop().then_inc(used, 2)
            dve.engine_nop().then_inc(ot_kept, 1)
            run_maxima(0)
            split_max(0)
            one_head(0, 0, False)
            one_head(0, 1, False)
            with dve.Fori(1, HEADS // 2 - 1) as p:
                one_head(p, 0, False)
                one_head(p, 1, False)
            one_head(HEADS // 2 - 1, 0, False)
            one_head(HEADS // 2 - 1, 1, True)


def finish_layer0(nc, K, A):
    with Stage(nc, "finish0") as S:
        sums, den = S.sb("sums", [P, T]), S.sb("den", [P, T])
        h1, h2 = S.sb("h1", [P, T]), S.sb("h2", [P, T])
        biased = S.sb("biased", [P, 2, TPB, D])
        pH, pR = S.ps("pH", [P, 4, BLK]), S.ps("pR", [P, 4, BLK])
        (loaded, inverted, scaled, ffn, ffn_kept, rows, s_kept, b_kept, g_kept) = (S.sem(n) for n in (
            "loaded", "inverted", "scaled", "ffn", "ffn_kept", "rows", "s_kept", "b_kept", "g_kept"))
        block = S.block()

        @block.sync
        def _(sp):
            sp.dma_start(sums[:, :], K.head_out[:, 0:HD, :]).then_inc(loaded, 16)
            sp.dma_start(den[:, :], K.head_out[:, HD:HD + 1, :].broadcast_to([HEADS, HD, T])).then_inc(loaded, 16)
            sp.wait_ge(loaded, 32)

        @block.vector
        def _(dve):
            dve.wait_ge(loaded, 32)
            for b in range(NB):
                cols = slice(b * BLK, (b + 1) * BLK)
                dve.reciprocal(den[:, cols], den[:, cols]).then_inc(inverted, 1)
                dve.wait_ge(inverted, b + 1)
                dve.tensor_tensor(sums[:, cols], sums[:, cols], den[:, cols], ALU.mult).then_inc(scaled, 1)
            for c in range(2 * NB):
                dve.wait_ge(rows, c + 1)
                src = pR[:, c % 4, :].rearrange("p (t d) -> p t d", d=D)
                if c < NB:
                    row = K.row["L0_attn_bo"][:, :].unsqueeze(1).broadcast_to([P, TPB, D])
                    dve.tensor_tensor(K.s[:, c * TPB:(c + 1) * TPB, :], src, row, ALU.add).then_inc(s_kept, 1)
                else:
                    if c - NB >= 2:
                        dve.wait_ge(g_kept, c - NB - 1)
                    row = K.row["L0_ffn_bias"][:, :].unsqueeze(1).broadcast_to([P, TPB, D])
                    dve.tensor_tensor(biased[:, c % 2], src, row, ALU.add).then_inc(b_kept, 1)

        @block.scalar
        def _(act):
            for n in range(2 * NB):
                b = n % NB
                act.wait_ge(ffn, n + 1)
                act.activation((h1, h2)[n // NB][:, b * BLK:(b + 1) * BLK], pH[:, b, :], ACT.Copy)\
                   .then_inc(ffn_kept, 1)
            for c in range(NB):
                act.wait_ge(b_kept, c + 1)
                act.activation(K.g[:, c * TPB:(c + 1) * TPB, :], biased[:, c % 2], ACT.Tanh).then_inc(g_kept, 1)

        @block.tensor
        def _(pe):
            for n in range(2 * NB):
                b = n % NB
                if n >= NB:
                    pe.wait_ge(ffn_kept, n - NB + 1)
                w = K.w[("L0_ffn_weight", "L0_ffn_aux_weight1")[n // NB]]
                pe.matmul(pH[:, b, :], w[:, :], (K.xnT, h1)[n // NB][:, b * BLK:(b + 1) * BLK],
                          start=True, stop=True).then_inc(ffn, 1)
            for c in range(2 * NB):
                b = c % NB
                if c < NB:
                    pe.wait_ge(scaled, b + 1)
                else:
                    pe.wait_ge(ffn_kept, NB + b + 1)
                    pe.wait_ge(s_kept, b + 1)
                for t in range(TPB):
                    tok = slice(b * BLK + t * P, b * BLK + (t + 1) * P)
                    mm = pe.matmul(pR[:, b, t * P:(t + 1) * P], (sums, h2)[c // NB][:, tok],
                                   K.w[("L0_attn_Wo", "L0_ffn_aux_weight2")[c // NB]][:, :], start=True, stop=True)
                mm.then_inc(rows, 1)


def attention_row_sums(nc, K, layer, wq, wk, wv, bq, bk, bv):
    scale = float(np.float32(1.0) / np.sqrt(np.float32(D)))
    with Stage(nc, f"rowsum{layer}") as S:
        qT, kT = S.sb("qT", [P, T]), S.sb("kT", [P, T])
        probs = S.sb("probs", [P, 2, T])
        row_max, neg, den = S.sb("row_max", [P, NT]), S.sb("neg", [P, NT]), S.sb("den", [P, NT])
        zero_p, zero_neg = S.sb("zero_p", [P, NT]), S.sb("zero_neg", [P, NT])
        inv, weight = S.sb("inv", [P, NT]), S.sb("weight", [P, NT])
        pS = [S.ps(f"pS{n}", [P, T]) for n in range(2)]
        (projected, kept, vproj, vkept, scored, maxed, exped, order) = (
            S.sem(n) for n in ("projected", "kept", "vproj", "vkept", "scored", "maxed", "exped", "order"))
        block = S.block()

        @block.tensor
        def _(pe):
            for n in range(2 * NB):
                w, b = divmod(n, NB)
                pe.matmul(pS[w][:, b * BLK:(b + 1) * BLK], (wq, wk)[w][:, :], K.xnT[:, b * BLK:(b + 1) * BLK],
                          start=True, stop=True).then_inc(projected, 1)
            pe.wait_ge(kept, NB)
            for t in range(NT):
                mm = pe.matmul(pS[0][:, t * P:(t + 1) * P], K.xnT[:, t * P:(t + 1) * P], wv[:, :],
                               start=True, stop=True)
                if t % TPB == TPB - 1:
                    mm.then_inc(vproj, 1)
            pe.wait_ge(kept, 2 * NB)
            pe.wait_ge(vkept, NB)
            for i in range(NT):
                if i >= 2:
                    pe.wait_ge(exped, i - 1)
                hi = (i + 1) * P
                for b in range(-(-hi // BLK)):
                    c0, c1 = b * BLK, min((b + 1) * BLK, hi)
                    diag = c1 == hi
                    mm = pe.matmul(pS[i % 2][:, c0:c1], qT[:, i * P:(i + 1) * P], kT[:, c0:c1],
                                   start=True, stop=not diag)
                    if diag:
                        mm = pe.matmul(pS[i % 2][:, c1 - P:c1], K.ident_b[:, :], K.neg_above[:, :],
                                       start=False, stop=True)
                mm.then_inc(scored, 1)

        @block.scalar
        def _(act):
            for n in range(2 * NB):
                w, b = divmod(n, NB)
                act.wait_ge(projected, n + 1)
                act.activation((qT, kT)[w][:, b * BLK:(b + 1) * BLK], pS[w][:, b * BLK:(b + 1) * BLK], ACT.Identity,
                               bias=(bq, bk)[w][:, :]).then_inc(kept, 1)
            for i in range(NT):
                hi = (i + 1) * P
                act.wait_ge(maxed, i + 1)
                if i >= 2:
                    act.wait_ge(exped, i - 1)
                act.activation(probs[:, i % 2, 0:hi], pS[i % 2][:, 0:hi], ACT.Exp, bias=neg[:, i:i + 1], scale=scale,
                               accum_out=den[:, i:i + 1]).then_inc(exped, 1)
            act.activation(zero_p[:, :], zero_neg[:, :], ACT.Exp).then_inc(exped, 1)

        @block.vector
        def _(dve):
            chain = Chain(dve, order)
            for c in range(NB):
                dve.wait_ge(vproj, c + 1)
                dve.tensor_tensor(K.v[:, c * TPB:(c + 1) * TPB, :],
                                  pS[0][:, c * BLK:(c + 1) * BLK].rearrange("p (t d) -> p t d", d=D),
                                  bv[:, :].unsqueeze(1).broadcast_to([P, TPB, D]), ALU.add).then_inc(vkept, 1)
            for i in range(NT):
                col = slice(i, i + 1)
                dve.wait_ge(scored, i + 1)
                chain(dve.reduce_max(row_max[:, col], pS[i % 2][:, 0:(i + 1) * P], AX.X))
                chain(dve.tensor_tensor(row_max[:, col], row_max[:, col], K.floor[:, col], ALU.max))
                chain(dve.tensor_scalar(zero_neg[:, col], row_max[:, col], -scale, 0.0, ALU.mult, ALU.min))
                dve.tensor_scalar(neg[:, col], row_max[:, col], -scale, None, ALU.mult).then_inc(maxed, 1)
            dve.wait_ge(exped, NT + 1)
            chain(dve.tensor_tensor(zero_p[:, :], zero_p[:, :], K.after[:, :], ALU.mult))
            chain(dve.tensor_tensor(den[:, :], den[:, :], zero_p[:, :], ALU.add))
            chain(dve.reciprocal(inv[:, :], den[:, :]))
            chain(dve.tensor_tensor(weight[:, :], den[:, :], inv[:, :], ALU.mult))
            chain(dve.tensor_tensor(K.s[:, :, :], K.v[:, :, :], weight[:, :].unsqueeze(2).broadcast_to([P, NT, D]),
                                    ALU.mult))


def attention_single(nc, K, layer, wq, wk, wv, bq, bk, bv):
    scale = float(np.float32(1.0) / np.sqrt(np.float32(D)))
    with Stage(nc, f"single{layer}") as S:
        qT, kT = S.sb("qT", [P, T]), S.sb("kT", [P, T])
        probs = [S.sb(f"probs{n}", [P, T]) for n in range(2)]
        probsT = S.sb("probsT", [P, 2, NT, P])
        row_max, neg, den = S.sb("row_max", [P, NT]), S.sb("neg", [P, NT]), S.sb("den", [P, NT])
        inv = S.sb("inv", [P, NT])
        pS = S.ps("pS", [P, NB, BLK])
        pT = S.ps("pT", [P, 2, BLK])
        pO = S.ps("pO", [P, 2, BLK])
        (projected, kept, vproj, vkept, scored, maxed, exped, turned, turn_kept, summed, order, finished) = (
            S.sem(n) for n in ("projected", "kept", "vproj", "vkept", "scored", "maxed", "exped", "turned",
                               "turn_kept", "summed", "order", "finished"))
        block = S.block()
        groups = [-(-(i + 1) // TPB) for i in range(NT)]
        before = [sum(groups[:i]) for i in range(NT + 1)]

        @block.tensor
        def _(pe):
            for n in range(2 * NB):
                w, b = divmod(n, NB)
                if n >= NB:
                    pe.wait_ge(kept, n - NB + 1)
                pe.matmul(pS[:, b, :], (wq, wk)[w][:, :], K.xnT[:, b * BLK:(b + 1) * BLK], start=True, stop=True)\
                  .then_inc(projected, 1)
            for t in range(NT):
                c = t // TPB
                if t % TPB == 0 and c >= 2:
                    pe.wait_ge(vkept, c - 1)
                mm = pe.matmul(pT[:, c % 2, t % TPB * P:(t % TPB + 1) * P], K.xnT[:, t * P:(t + 1) * P], wv[:, :],
                               start=True, stop=True)
                if t % TPB == TPB - 1:
                    mm.then_inc(vproj, 1)
            pe.wait_ge(kept, 2 * NB)
            pe.wait_ge(vkept, NB)

            def scores(i):
                if i >= 1:
                    pe.wait_ge(exped, i)
                hi = (i + 1) * P
                for b in range(-(-hi // BLK)):
                    w = min(BLK, hi - b * BLK)
                    diag = b == i // TPB
                    mm = pe.matmul(pS[:, b, 0:w], qT[:, i * P:(i + 1) * P], kT[:, b * BLK:b * BLK + w],
                                   start=True, stop=not diag)
                    if diag:
                        mm = pe.matmul(pS[:, b, w - P:w], K.ident_b[:, :], K.neg_above[:, :], start=False, stop=True)
                mm.then_inc(scored, 1)

            def turn(i):
                pe.wait_ge(exped, i + 1)
                for c in range(groups[i]):
                    n = before[i] + c
                    if n >= 2:
                        pe.wait_ge(turn_kept, n - 1)
                    for j in range(c * TPB, min(i + 1, (c + 1) * TPB)):
                        mm = pe.transpose(pT[:, n % 2, j % TPB * P:(j % TPB + 1) * P],
                                          probs[i % 2][:, j * P:(j + 1) * P], K.ident[:, :])
                    mm.then_inc(turned, 1)

            def sums(i):
                if i >= 2:
                    pe.wait_ge(finished, i - 1)
                pe.wait_ge(turn_kept, before[i + 1])
                for j in range(i + 1):
                    mm = pe.matmul(pO[:, i % 2, 0:D], probsT[:, i % 2, j, :], K.v[:, j, :], start=(j == 0),
                                   stop=(j == i))
                mm.then_inc(summed, 1)

            for i in range(NT + 1):
                if i < NT:
                    scores(i)
                if i >= 1:
                    turn(i - 1)
                    sums(i - 1)

        @block.scalar
        def _(act):
            for n in range(2 * NB):
                w, b = divmod(n, NB)
                act.wait_ge(projected, n + 1)
                act.activation((qT, kT)[w][:, b * BLK:(b + 1) * BLK], pS[:, b, :], ACT.Identity,
                               bias=(bq, bk)[w][:, :]).then_inc(kept, 1)

            def keep_turned(i):
                for c in range(groups[i]):
                    n = before[i] + c
                    w = min(i + 1 - c * TPB, TPB) * P
                    act.wait_ge(turned, n + 1)
                    if i >= 2:
                        act.wait_ge(summed, i - 1)
                    act.activation(probsT[:, i % 2, c * TPB:c * TPB + w // P, :],
                                   pT[:, n % 2, 0:w].rearrange("p (j q) -> p j q", q=P), ACT.Copy).then_inc(turn_kept, 1)

            for i in range(NT + 1):
                if i >= 1:
                    keep_turned(i - 1)
                if i < NT:
                    act.wait_ge(maxed, i + 1)
                    act.activation(probs[i % 2][:, 0:(i + 1) * P],
                                   pS[:, :, :].rearrange("p b c -> p (b c)")[:, 0:(i + 1) * P], ACT.Exp,
                                   bias=neg[:, i:i + 1], scale=scale, accum_out=den[:, i:i + 1]).then_inc(exped, 1)

        @block.vector
        def _(dve):
            chain = Chain(dve, order)
            for c in range(NB):
                dve.wait_ge(vproj, c + 1)
                dve.tensor_tensor(K.v[:, c * TPB:(c + 1) * TPB, :], pT[:, c % 2, :].rearrange("p (t d) -> p t d", d=D),
                                  bv[:, :].unsqueeze(1).broadcast_to([P, TPB, D]), ALU.add).then_inc(vkept, 1)

            def maximum(i):
                dve.wait_ge(scored, i + 1)
                chain(dve.reduce_max(row_max[:, i:i + 1],
                                     pS[:, :, :].rearrange("p b c -> p (b c)")[:, 0:(i + 1) * P], AX.X))
                dve.tensor_scalar(neg[:, i:i + 1], row_max[:, i:i + 1], -scale, None, ALU.mult).then_inc(maxed, 1)

            def finish(i):
                dve.wait_ge(exped, i + 1)
                chain(dve.reciprocal(inv[:, i:i + 1], den[:, i:i + 1]))
                dve.wait_ge(summed, i + 1)
                dve.tensor_scalar(K.s[:, i, :], pO[:, i % 2, 0:D], inv[:, i:i + 1], None, ALU.mult)\
                   .then_inc(finished, 1)

            for i in range(NT + 1):
                if i < NT:
                    maximum(i)
                if i >= 1:
                    finish(i - 1)


L1_E, L1_I, L1_TOP = 32, 64, 6
L1_J = L1_E * L1_I // P


def softmax_over(dve, act_done, chain, logits, n, mx, shifted, total, gates, exp_ready):
    chain(dve.reduce_max(mx, logits, AX.X))
    dve.tensor_tensor(shifted, logits, mx.unsqueeze(2).broadcast_to([P, NT, n]), ALU.subtract).then_inc(exp_ready, 1)
    dve.wait_ge(act_done, 1)
    chain(dve.reduce_sum(total, gates, AX.X))
    chain(dve.reciprocal(total, total))
    chain(dve.tensor_tensor(gates, gates, total.unsqueeze(2).broadcast_to([P, NT, n]), ALU.mult))


def ffn_top6(nc, K, A):
    E = L1_E
    with Stage(nc, "top6") as S:
        shifted, gates, score = S.sb("shifted", [P, NT, E]), S.sb("gates", [P, NT, E]), S.sb("score", [P, NT, E])
        mask, hit = S.sb("mask", [P, NT, E]), S.sb("hit", [P, NT, E])
        mx, total = S.sb("mx", [P, NT]), S.sb("total", [P, NT])
        top, place = S.sb("top", [P, NT, 8]), S.sb("place", [P, NT, 8])
        place_u = S.sb("place_u", [P, NT, 8], mybir.dt.uint32)
        parts = S.sb("parts", [P, NT, PARTS, E], BF16)
        combT = S.sb("combT", [PARTS * E, T], BF16)
        sel_f, sel = S.sb("sel_f", [PARTS * E, L1_J * P]), S.sb("sel", [PARTS * E, L1_J * P], BF16)
        act_gate, hidden = S.sb("act_gate", [P, 2, BLK]), S.sb("hidden", [P, 2, BLK])
        yT = S.sb("yT", [P, BLK])
        pG, pU, pC = (S.ps(n, [P, 2, BLK]) for n in ("pG", "pU", "pC"))
        pY, pR = S.ps("pY", [P, BLK]), S.ps("pR", [P, BLK])
        (sel_in, sel_made, routed, exp_ready, exped, order, split, turned, comb_kept, opened, gated, mixed, downed,
         y_kept, y_turned, g_kept, mixing) = (S.sem(n) for n in (
             "sel_in", "sel_made", "routed", "exp_ready", "exped", "order", "split", "turned", "comb_kept", "opened",
             "gated", "mixed", "downed", "y_kept", "y_turned", "g_kept", "mixing"))
        block = S.block()
        STEPS = L1_J + 1
        logits = pR[:, :].rearrange("p (t e) -> p t e", e=E)
        turned_parts = pG[:, :, :].bitcast(BF16)
        g_blocks = K.g[:, :, :].rearrange("p (b t) d -> p b t d", t=TPB)

        @block.sync
        def _(sp):
            sp.dma_start(sel_f[:, :], A["c_sel1"]).then_inc(sel_in, 16)
            sp.wait_ge(sel_in, 16)

        @block.tensor
        def _(pe):
            for t in range(NT):
                mm = pe.matmul(pR[:, t * E:(t + 1) * E], K.xnT[:, t * P:(t + 1) * P], K.wr1[:, :],
                               start=True, stop=True)
            mm.then_inc(routed, 1)
            pe.wait_ge(split, 1)
            for t in range(NT):
                mm = pe.transpose(turned_parts[0:PARTS * E, t // 8, t % 8 * P:(t % 8 + 1) * P],
                                  parts[:, t, :, :].rearrange("p a e -> p (a e)"), K.ident_b[:, :])
            mm.then_inc(turned, 1)
            pe.wait_ge(comb_kept, 2)
            pe.wait_ge(K.l1_loaded, 16 * 6)
            pe.wait_ge(sel_made, 1)

            def open_step(b, n):
                if n >= 2:
                    pe.wait_ge(mixed, STEPS * b + n - 1)
                x = K.xnT[:, bass.ts(b, BLK)]
                gw, uw = (K.gate1[:, n * P:(n + 1) * P], K.up1[:, n * P:(n + 1) * P]) if n < L1_J else \
                    (K.sgate1[:, :], K.sup1[:, :])
                pe.matmul(pG[:, n % 2, :], gw, x, start=True, stop=True)
                mm = pe.matmul(pU[:, n % 2, :], uw, x, start=True, stop=True)
                if n < L1_J:
                    mm = pe.matmul(pC[:, n % 2, :], sel[:, n * P:(n + 1) * P], combT[:, bass.ts(b, BLK)],
                                   start=True, stop=True)
                mm.then_inc(opened, 1)

            def close_step(b, n):
                pe.wait_ge(mixed, STEPS * b + n + 1)
                w = K.down1[:, n, :] if n < L1_J else K.sdown1[:, :]
                pe.matmul(pY[:, :], w, hidden[:, n % 2, :], start=(n == 0), stop=(n == L1_J)).then_inc(downed, 1)

            with pe.Fori(0, NB) as b:
                for n in range(STEPS):
                    open_step(b, n)
                    if n >= 1:
                        close_step(b, n - 1)
                close_step(b, STEPS - 1)
                pe.wait_ge(y_kept, b + 1)
                for t in range(TPB):
                    mm = pe.transpose(pR[:, t * P:(t + 1) * P], yT[:, t * P:(t + 1) * P], K.ident[:, :])
                mm.then_inc(y_turned, 1)

        @block.scalar
        def _(act):
            act.wait_ge(sel_in, 16)
            act.activation(sel[:, :], sel_f[:, :], ACT.Copy).then_inc(sel_made, 1)
            act.wait_ge(exp_ready, 1)
            act.activation(gates[:, :, :], shifted[:, :, :], ACT.Exp).then_inc(exped, 1)
            act.wait_ge(turned, 1)
            for c in range(2):
                act.activation(combT[:, c * 8 * P:(c + 1) * 8 * P], turned_parts[0:PARTS * E, c, :], ACT.Copy)\
                   .then_inc(comb_kept, 1)
            with act.Fori(0, NB) as b:
                for n in range(STEPS):
                    act.wait_ge(opened, STEPS * b + n + 1)
                    if n >= 2:
                        act.wait_ge(mixed, STEPS * b + n - 1)
                    act.activation(act_gate[:, n % 2, :], pG[:, n % 2, :], ACT.Silu).then_inc(gated, 1)
                act.wait_ge(y_turned, b + 1)
                act.activation(g_blocks[:, b, :, :], pR[:, :].rearrange("p (t d) -> p t d", d=D), ACT.Copy)\
                   .then_inc(g_kept, 1)

        @block.vector
        def _(dve):
            chain = Chain(dve, order)
            dve.wait_ge(routed, 1)
            softmax_over(dve, exped, chain, logits, E, mx[:, :], shifted[:, :, :], total[:, :], gates[:, :, :],
                         exp_ready)
            chain(dve.tensor_tensor(score[:, :, :], gates[:, :, :],
                                    K.row["L1_ffn_e_score_bias"][:, :].unsqueeze(1).broadcast_to([P, NT, E]), ALU.add))
            for t in range(NT):
                last = dve.max(top[:, t, :], score[:, t, :])
            chain(last)
            for t in range(NT):
                last = dve.max_index(place_u[:, t, :], top[:, t, :], score[:, t, :])
            chain(last)
            chain(dve.tensor_copy(place[:, :, :], place_u[:, :, :]))
            iota = K.iota[:, 0:E].unsqueeze(1).broadcast_to([P, NT, E])
            for k in range(L1_TOP):
                at = place[:, :, k:k + 1].broadcast_to([P, NT, E])
                if k == 0:
                    chain(dve.tensor_tensor(mask[:, :, :], iota, at, ALU.is_equal))
                else:
                    chain(dve.tensor_tensor(hit[:, :, :], iota, at, ALU.is_equal))
                    chain(dve.tensor_tensor(mask[:, :, :], mask[:, :, :], hit[:, :, :], ALU.add))
            chain(dve.tensor_tensor(gates[:, :, :], gates[:, :, :], mask[:, :, :], ALU.mult))
            chain(dve.reduce_sum(total[:, :], gates[:, :, :], AX.X))
            chain(dve.tensor_scalar(total[:, :], total[:, :], 1e-12, None, ALU.max))
            chain(dve.reciprocal(total[:, :], total[:, :]))
            chain(dve.tensor_tensor(gates[:, :, :], gates[:, :, :], total[:, :].unsqueeze(2).broadcast_to([P, NT, E]),
                                    ALU.mult))
            chain(dve.tensor_copy(parts[:, :, 0, :], gates[:, :, :]))
            chain(dve.tensor_tensor(hit[:, :, :], gates[:, :, :], parts[:, :, 0, :], ALU.subtract))
            chain(dve.tensor_copy(parts[:, :, 1, :], hit[:, :, :]))
            dve.tensor_tensor(parts[:, :, 2, :], hit[:, :, :], parts[:, :, 1, :], ALU.subtract).then_inc(split, 1)
            with dve.Fori(0, NB) as b:
                for n in range(STEPS):
                    dve.wait_ge(gated, STEPS * b + n + 1)
                    if n >= 2:
                        dve.wait_ge(downed, STEPS * b + n - 1)
                    mix = dve.tensor_tensor(hidden[:, n % 2, :], act_gate[:, n % 2, :], pU[:, n % 2, :], ALU.mult)
                    if n < L1_J:
                        mix.then_inc(mixing, 1)
                        dve.wait_ge(mixing, L1_J * b + n + 1)
                        mix = dve.tensor_tensor(hidden[:, n % 2, :], hidden[:, n % 2, :], pC[:, n % 2, :], ALU.mult)
                    mix.then_inc(mixed, 1)
                dve.wait_ge(downed, STEPS * (b + 1))
                dve.tensor_copy(yT[:, :], pY[:, :]).then_inc(y_kept, 1)


L2_E, L2_H, L2_GROUPS = 24, 512, 4
L2_CAP = -(-2 * (T // L2_GROUPS) // L2_E)
L2_HALF = L2_CAP * L2_GROUPS // 2
L2_SLOTS = L2_E * 2 * L2_HALF
L2_TABLE = -(-(L2_SLOTS + 2 * T) // P) * P
L2_LN_EPS = 1e-6
LOOP_EXPERTS = 4
LOOP_HALVES = 2 * LOOP_EXPERTS
LOOPS = L2_E // LOOP_EXPERTS


def route_top2(nc, K, A):
    E, SH = L2_E, [P, NT, L2_E]
    with Stage(nc, "route2") as S:
        raw, shifted, gates = S.sb("raw", SH), S.sb("shifted", SH), S.sb("gates", SH)
        hit, cand, comb, prod = S.sb("hit", SH), S.sb("cand", SH), S.sb("comb", SH), S.sb("prod", SH)
        chosen, kept = [S.sb(f"chosen{c}", SH) for c in range(2)], [S.sb(f"kept{c}", SH) for c in range(2)]
        ones_of = [S.sb(f"ones_of{c}", SH, BF16) for c in range(2)]
        base, spare = S.sb("base", SH), S.sb("spare", [P, 2, NT])
        mx, total, idx = S.sb("mx", [P, NT]), S.sb("total", [P, NT]), S.sb("idx", [P, NT])
        weight, slot, held = S.sb("weight", [P, 2, NT]), S.sb("slot", [P, 2, NT]), S.sb("held", [P, 2, NT])
        place = S.sb("place", [P, 2, NT])
        place_i = S.sb("place_i", [P, 2, NT], I32)
        token_i, zero_i = S.sb("token_i", [P, NT], I32), S.sb("zero_i", [P, L2_TABLE // P], I32)
        pL, pA, pB = S.ps("pL", [P, BLK]), S.ps("pA", [P, BLK]), S.ps("pB", [P, BLK])
        pT = S.ps("pT", [P, NB, BLK])
        (consts_in, xn_out, routed, exp_ready, exped, order, picked, located, placed, combined, turned, comb_kept,
         zeroed, cleared, scattered, slots_in) = (S.sem(n) for n in (
             "consts_in", "xn_out", "routed", "exp_ready", "exped", "order", "picked", "located", "placed", "combined",
             "turned", "comb_kept", "zeroed", "cleared", "scattered", "slots_in"))
        block = S.block()
        logits, loc = pL[:, 0:NT * E].rearrange("p (t e) -> p t e", e=E), [
            bank[:, 0:NT * E].rearrange("p (t e) -> p t e", e=E) for bank in (pA, pB)]
        table = K.table.rearrange("(p c) o -> p (c o)", p=P)

        @block.sync
        def _(sp):
            sp.dma_start(K.xn_rows.rearrange("(t p) d -> p t d", p=P), K.xn[:, :, :]).then_inc(xn_out, 16)
            sp.dma_start(base[:, :, :], A["c_base2"]).then_inc(consts_in, 16)
            sp.dma_start(spare[:, :, :], A["c_spare2"]).then_inc(consts_in, 16)
            sp.dma_start(token_i[:, :], A["c_token"]).then_inc(consts_in, 16)
            sp.wait_ge(xn_out, 16)
            sp.wait_ge(scattered, 16 * 2 * NT)
            with nc.allow_non_contiguous_dma(reason="a slot's token per partition"):
                sp.dma_start(K.slot_token[:, :],
                             K.table[0:L2_SLOTS, :].rearrange("(n r) o -> r (n o)", r=L2_HALF)).then_inc(slots_in, 16)
            sp.wait_ge(slots_in, 16)

        @block.tensor
        def _(pe):
            for t in range(NT):
                mm = pe.matmul(pL[:, t * E:(t + 1) * E], K.xnT[:, t * P:(t + 1) * P], K.wg2[:, :],
                               start=True, stop=True)
            mm.then_inc(routed, 1)
            tiles = NT // L2_GROUPS
            for c in range(2):
                pe.wait_ge(picked, c + 1)
                for t in range(NT):
                    g0 = t // tiles * tiles
                    adds = [(ones_of[c], j) for j in range(g0, t)]
                    if c == 1:
                        adds += [(ones_of[0], j) for j in range(g0, g0 + tiles)]
                    out = (pA, pB)[c][:, t * E:(t + 1) * E]
                    mm = pe.matmul(out, K.above_b[:, :], ones_of[c][:, t, :], start=True, stop=not adds)
                    for n, (o, j) in enumerate(adds):
                        mm = pe.matmul(out, K.ones_b[:, :], o[:, j, :], start=False, stop=n == len(adds) - 1)
                mm.then_inc(located, 1)
            pe.wait_ge(combined, 1)
            for t in range(NT):
                mm = pe.transpose(pT[0:E, t // TPB, t % TPB * P:(t % TPB + 1) * P], comb[:, t, :], K.ident[:, :])
            mm.then_inc(turned, 1)

        @block.scalar
        def _(act):
            act.wait_ge(exp_ready, 1)
            act.activation(gates[:, :, :], shifted[:, :, :], ACT.Exp).then_inc(exped, 1)
            act.wait_ge(turned, 1)
            act.activation(K.combT[:, :], pT[0:E, :, :].rearrange("e b c -> e (b c)"), ACT.Copy).then_inc(comb_kept, 1)

        @block.vector
        def _(dve):
            chain = Chain(dve, order)
            iota = K.iota[:, 0:E].unsqueeze(1).broadcast_to(SH)

            def over_e(x):
                return x.unsqueeze(2).broadcast_to(SH)

            def choose(values, c):
                chain(dve.reduce_max(mx[:, :], values[:, :, :], AX.X))
                chain(dve.tensor_tensor(hit[:, :, :], values[:, :, :], over_e(mx[:, :]), ALU.is_lt))
                chain(dve.scalar_tensor_tensor(cand[:, :, :], hit[:, :, :], float(4 * E), iota, ALU.mult, ALU.add))
                chain(dve.tensor_reduce(idx[:, :], cand[:, :, :], AX.X, ALU.min))
                chain(dve.tensor_tensor(chosen[c][:, :, :], iota, over_e(idx[:, :]), ALU.is_equal))
                dve.tensor_copy(ones_of[c][:, :, :], chosen[c][:, :, :]).then_inc(picked, 1)

            dve.memset(zero_i[:, :], 0).then_inc(zeroed, 1)
            dve.wait_ge(routed, 1)
            chain(dve.tensor_copy(raw[:, :, :], logits))
            softmax_over(dve, exped, chain, raw[:, :, :], E, mx[:, :], shifted[:, :, :], total[:, :],
                         gates[:, :, :], exp_ready)
            choose(gates, 0)
            chain(dve.scalar_tensor_tensor(raw[:, :, :], chosen[0][:, :, :], LOWEST, raw[:, :, :], ALU.mult, ALU.add))
            choose(raw, 1)
            dve.wait_ge(consts_in, 48)
            for c in range(2):
                dve.wait_ge(located, c + 1)
                chain(dve.scalar_tensor_tensor(kept[c][:, :, :], loc[c], float(L2_CAP), chosen[c][:, :, :],
                                               ALU.is_lt, ALU.mult))
                chain(dve.tensor_tensor(prod[:, :, :], gates[:, :, :], kept[c][:, :, :], ALU.mult))
                chain(dve.reduce_sum(weight[:, c, :], prod[:, :, :], AX.X))
                chain(dve.tensor_tensor(prod[:, :, :], loc[c], base[:, :, :], ALU.add))
                chain(dve.tensor_tensor(prod[:, :, :], prod[:, :, :], kept[c][:, :, :], ALU.mult))
                chain(dve.reduce_sum(slot[:, c, :], prod[:, :, :], AX.X))
                chain(dve.reduce_sum(held[:, c, :], kept[c][:, :, :], AX.X))
            chain(dve.tensor_tensor(place[:, :, :], held[:, :, :], spare[:, :, :], ALU.mult))
            chain(dve.tensor_tensor(place[:, :, :], spare[:, :, :], place[:, :, :], ALU.subtract))
            chain(dve.tensor_tensor(place[:, :, :], place[:, :, :], slot[:, :, :], ALU.add))
            dve.tensor_copy(place_i[:, :, :], place[:, :, :]).then_inc(placed, 1)
            chain(dve.tensor_copy(K.slot_i[:, :, :], slot[:, :, :]))
            chain(dve.tensor_tensor(total[:, :], weight[:, 0, :], weight[:, 1, :], ALU.add))
            chain(dve.tensor_scalar(total[:, :], total[:, :], 1e-9, None, ALU.max))
            chain(dve.reciprocal(total[:, :], total[:, :]))
            for c in range(2):
                last = dve.tensor_tensor(K.coef[:, c, :], weight[:, c, :], total[:, :], ALU.mult)
            chain(last)
            for c in range(2):
                last = dve.tensor_tensor((comb, prod)[c][:, :, :], kept[c][:, :, :], over_e(K.coef[:, c, :]), ALU.mult)
            chain(last)
            dve.tensor_tensor(comb[:, :, :], comb[:, :, :], prod[:, :, :], ALU.add).then_inc(combined, 1)

        @block.gpsimd
        def _(pool):
            pool.wait_ge(zeroed, 1)
            pool.dma_start(table, zero_i[:, :]).then_inc(cleared, 16)
            pool.wait_ge(cleared, 16)
            pool.wait_ge(placed, 1)
            for c in range(2):
                for t in range(NT):
                    pool.indirect_dma_start(
                        out=K.table, out_offset=bass.IndirectOffsetOnAxis(ap=place_i[:, c, t:t + 1], axis=0),
                        in_=token_i[:, t:t + 1], in_offset=None).then_inc(scattered, 16)
            pool.wait_ge(scattered, 16 * 2 * NT)


def expert_pass(nc, K, tag, src, weights, width_in, width_out, dst):
    F = width_in // P
    R = L2_HALF
    with Stage(nc, tag) as S:
        rows = [S.sb(f"rows{k}", [R, width_in]) for k in range(LOOP_HALVES)]
        rowsT = [S.sb(f"rowsT{n}", [P, F, R]) for n in range(2)]
        w = [S.sb(f"w{j}", [P, F, width_out]) for j in range(LOOP_EXPERTS)]
        outs = [S.sb(f"outs{k}", [R, width_out]) for k in range(LOOP_HALVES)]
        pT, pY = S.ps("pT", [P, 2, BLK]), S.ps("pY", [P, 2, BLK])
        turned, turn_kept, multiplied, kept = (S.sem(n) for n in (
            "turned", "turn_kept", "multiplied", "kept"))
        gathered = [S.sem(f"gathered{k}") for k in range(LOOP_HALVES)]
        stored = [S.sem(f"stored{k}") for k in range(LOOP_HALVES)]
        w_in = [S.sem(f"w_in{j}") for j in range(LOOP_EXPERTS)]
        block = S.block()
        w_loops = weights.rearrange("(l j) p f d -> l j p f d", j=LOOP_EXPERTS)
        dst_loops = dst.rearrange("(l k r) d -> l k r d", k=LOOP_HALVES, r=R)

        def every_loop(engine, body):
            body(0, True)
            with engine.Fori(1, LOOPS) as l:
                body(l, False)

        @block.sync
        def _(sp):
            def body(l, first):
                for j in range(LOOP_EXPERTS):
                    if not first:
                        sp.wait_ge(multiplied, LOOP_HALVES * (l - 1) + 2 * j + 2)
                    sp.dma_start(w[j][:, :, :], w_loops[l, j]).then_inc(w_in[j], 16)

            every_loop(sp, body)

        @block.gpsimd
        def _(pool):
            for n in range(2 * L2_E):
                if n >= LOOP_HALVES:
                    pool.wait_ge(turned, n - LOOP_HALVES + 1)
                k = n % LOOP_HALVES
                pool.indirect_dma_start(
                    out=rows[k][:, :], out_offset=None, in_=src,
                    in_offset=bass.IndirectOffsetOnAxis(ap=K.slot_token[:, n:n + 1], axis=0)).then_inc(gathered[k], 16)

        @block.tensor
        def _(pe):
            def turn(l, first, k):
                n = LOOP_HALVES * l + k
                pe.wait_ge(gathered[k], 16 * (l + 1))
                if not first or k >= 2:
                    pe.wait_ge(turn_kept, n - 1)
                for f in range(F):
                    mm = pe.transpose(pT[:, k % 2, f * R:(f + 1) * R], rows[k][:, f * P:(f + 1) * P],
                                      K.ident[0:R, 0:R])
                mm.then_inc(turned, 1)

            def multiply(l, first, k):
                n = LOOP_HALVES * l + k
                pe.wait_ge(turn_kept, n + 1)
                if k % 2 == 0:
                    pe.wait_ge(w_in[k // 2], 16 * (l + 1))
                if not first or k >= 2:
                    pe.wait_ge(kept, n - 1)
                for f in range(F):
                    mm = pe.matmul(pY[0:R, k % 2, 0:width_out], rowsT[k % 2][:, f, :], w[k // 2][:, f, :],
                                   start=(f == 0), stop=(f == F - 1))
                mm.then_inc(multiplied, 1)

            def body(l, first):
                for k in range(LOOP_HALVES):
                    turn(l, first, k)
                    if k >= 1:
                        multiply(l, first, k - 1)
                multiply(l, first, LOOP_HALVES - 1)

            every_loop(pe, body)

        @block.vector
        def _(dve):
            def body(l, first):
                for k in range(LOOP_HALVES):
                    n = LOOP_HALVES * l + k
                    dve.wait_ge(turned, n + 1)
                    if not first or k >= 2:
                        dve.wait_ge(multiplied, n - 1)
                    dve.tensor_copy(rowsT[k % 2][:, :, :], pT[:, k % 2, 0:F * R].rearrange("p (f r) -> p f r", r=R))\
                       .then_inc(turn_kept, 1)

            every_loop(dve, body)

        @block.scalar
        def _(act):
            def body(l, first):
                for k in range(LOOP_HALVES):
                    n = LOOP_HALVES * l + k
                    act.wait_ge(multiplied, n + 1)
                    if not first:
                        act.wait_ge(stored[k], 16 * l)
                    act.activation(outs[k][:, :], pY[0:R, k % 2, 0:width_out], ACT.Copy).then_inc(kept, 1)
                    act.wait_ge(kept, n + 1)
                    act.dma_start(dst_loops[l, k], outs[k][:, :]).then_inc(stored[k], 16)

            every_loop(act, body)
            for k in range(LOOP_HALVES):
                act.wait_ge(stored[k], 16 * LOOPS)


def combine_top2(nc, K, A, last):
    W = D if last else L2_H
    G = 1 if last else L2_GROUPS
    src = K.y_rows if last else K.h_rows
    with Stage(nc, f"combine{int(last)}") as S:
        got = [S.sb(f"got{c}", [P, 2 * TPB, W]) for c in range(2)]
        mixed = S.sb("mixed", [P, NT, W])
        bias_e = S.sb("bias_e", [L2_E, W])
        ln_w, ln_b = S.sb("ln_w", [P, G, W]), S.sb("ln_b", [P, G, W])
        stats, mv = S.sb("stats", [P, NT, 6]), S.sb("mv", [P, NT, 2])
        var, rstd, tmp = S.sb("var", [P, NT]), S.sb("rstd", [P, NT]), S.sb("tmp", [P, NT])
        pB = S.ps("pB", [P, 4, BLK])
        gathered = [S.sem(f"gathered{c}") for c in range(NB)]
        (loaded, biased, summed, taken, order, normed, rectified, stored) = (S.sem(n) for n in (
            "loaded", "biased", "summed", "taken", "order", "normed", "rectified", "stored"))
        block = S.block()
        names = ("L2_ffn_b2", "L2_ffn_ln_out_w", "L2_ffn_ln_out_b") if last else (
            "L2_ffn_b1", "L2_ffn_ln_hid_w", "L2_ffn_ln_hid_b")

        @block.sync
        def _(sp):
            sp.dma_start(bias_e[:, :], A[names[0]]).then_inc(loaded, 16)
            for dst, n in ((ln_w, names[1]), (ln_b, names[2])):
                row = A[n] if not last else A[n].unsqueeze(0)
                sp.dma_start(dst[:, :, :], row.partition_broadcast(P)).then_inc(loaded, 16)
            if not last:
                hid = K.hid_rows.rearrange("(t p) d -> p t d", p=P)
                for t in range(NT):
                    sp.wait_ge(rectified, t + 1)
                    sp.dma_start(hid[:, t, :], mixed[:, t, :]).then_inc(stored, 16)
                sp.wait_ge(stored, 16 * NT)
            sp.wait_ge(loaded, 48)

        @block.gpsimd
        def _(pool):
            for t in range(NT):
                if t % TPB == 0 and t >= 2 * TPB:
                    pool.wait_ge(taken, t - TPB)
                for c in range(2):
                    pool.indirect_dma_start(
                        out=got[c][:, t % (2 * TPB), :], out_offset=None, in_=src,
                        in_offset=bass.IndirectOffsetOnAxis(ap=K.slot_i[:, c, t:t + 1], axis=0)).then_inc(gathered[t // TPB], 16)

        @block.tensor
        def _(pe):
            pe.wait_ge(loaded, 48)
            for t in range(NT):
                if t >= 4:
                    pe.wait_ge(summed, t - 3)
                pe.matmul(pB[:, t % 4, 0:W], K.combT[:, t * P:(t + 1) * P], bias_e[:, :], start=True, stop=True)\
                  .then_inc(biased, 1)

        @block.vector
        def _(dve):
            chain = Chain(dve, order)
            dve.wait_ge(loaded, 48)
            for t in range(NT):
                dve.wait_ge(biased, t + 1)
                dve.wait_ge(gathered[t // TPB], 32 * TPB)
                dve.scalar_tensor_tensor(mixed[:, t, :], got[0][:, t % (2 * TPB), :], K.coef[:, 0, t:t + 1],
                                         pB[:, t % 4, 0:W], ALU.mult, ALU.add).then_inc(summed, 1)
                dve.wait_ge(summed, t + 1)
                dve.scalar_tensor_tensor(mixed[:, t, :], got[1][:, t % (2 * TPB), :], K.coef[:, 1, t:t + 1],
                                         mixed[:, t, :], ALU.mult, ALU.add).then_inc(taken, 1)
                dve.wait_ge(taken, t + 1)
                if last:
                    chain(dve.tensor_tensor(mixed[:, t, :], mixed[:, t, :], K.xn[:, t, :], ALU.add))
                chain(dve.bn_stats(stats[:, t, :], mixed[:, t, :]))
                if t % TPB < TPB - 1:
                    continue
                ts = slice(t - TPB + 1, t + 1)
                for u in range(t - TPB + 1, t + 1):
                    end = dve.bn_aggr(mv[:, u, :], stats[:, u, :])
                chain(end)
                chain(dve.tensor_scalar(var[:, ts], mv[:, ts, 1], L2_LN_EPS, None, ALU.add))
                rsqrt(dve, chain, rstd[:, ts], var[:, ts], tmp[:, ts])
                g = 0 if last else t // TPB
                for u in range(t - TPB + 1, t + 1):
                    out = K.g[:, u, :] if last else mixed[:, u, :]
                    chain(dve.scalar_tensor_tensor(mixed[:, u, :], mixed[:, u, :], mv[:, u, 0:1], ln_w[:, g, :],
                                                   ALU.subtract, ALU.mult))
                    dve.scalar_tensor_tensor(out, mixed[:, u, :], rstd[:, u:u + 1], ln_b[:, g, :],
                                             ALU.mult, ALU.add).then_inc(normed, 1)

        @block.scalar
        def _(act):
            if not last:
                for t in range(NT):
                    act.wait_ge(normed, t + 1)
                    act.activation(mixed[:, t, :], mixed[:, t, :], ACT.Relu).then_inc(rectified, 1)


def ffn_top2(nc, K, A):
    route_top2(nc, K, A)
    expert_pass(nc, K, "experts2a", K.xn_rows, K.w1_2, D, L2_H, K.h_rows)
    combine_top2(nc, K, A, last=False)
    expert_pass(nc, K, "experts2b", K.hid_rows, K.w2_2, L2_H, D, K.y_rows)
    combine_top2(nc, K, A, last=True)


def finish_layer3(nc, K):
    with Stage(nc, "finish3") as S:
        sums, den = S.sb("sums", [P, T]), S.sb("den", [P, T])
        pR = S.ps("pR", [P, NB, BLK])
        loaded, inverted, scaled, rows, s_kept = (S.sem(n) for n in ("loaded", "inverted", "scaled", "rows", "s_kept"))
        block = S.block()

        @block.sync
        def _(sp):
            sp.dma_start(sums[:, :], K.head_out[:, 0:HD, :]).then_inc(loaded, 16)
            sp.dma_start(den[:, :], K.head_out[:, HD:HD + 1, :].broadcast_to([HEADS, HD, T])).then_inc(loaded, 16)
            sp.wait_ge(loaded, 32)

        @block.vector
        def _(dve):
            dve.wait_ge(loaded, 32)
            for b in range(NB):
                cols = slice(b * BLK, (b + 1) * BLK)
                dve.reciprocal(den[:, cols], den[:, cols]).then_inc(inverted, 1)
                dve.wait_ge(inverted, b + 1)
                dve.tensor_tensor(sums[:, cols], sums[:, cols], den[:, cols], ALU.mult).then_inc(scaled, 1)

        @block.tensor
        def _(pe):
            for b in range(NB):
                pe.wait_ge(scaled, b + 1)
                for t in range(TPB):
                    tok = slice(b * BLK + t * P, b * BLK + (t + 1) * P)
                    mm = pe.matmul(pR[:, b, t * P:(t + 1) * P], sums[:, tok], K.w["L3_attn_ow"][:, :],
                                   start=True, stop=True)
                mm.then_inc(rows, 1)

        @block.scalar
        def _(act):
            for b in range(NB):
                act.wait_ge(rows, b + 1)
                act.activation(K.s[:, b * TPB:(b + 1) * TPB, :], pR[:, b, :].rearrange("p (t d) -> p t d", d=D),
                               ACT.Copy).then_inc(s_kept, 1)


L3_E, L3_H = 8, 512
L3_F = L3_H // P
L3_SLOTS = 3


def ffn_top1(nc, K, A):
    E, SH = L3_E, [P, NT, L3_E]
    with Stage(nc, "top1") as S:
        raw, shifted, gates = S.sb("raw", SH), S.sb("shifted", SH), S.sb("gates", SH)
        hit, cand, chosen = S.sb("hit", SH), S.sb("cand", SH), S.sb("chosen", SH)
        mx, total, idx = S.sb("mx", [P, NT]), S.sb("total", [P, NT]), S.sb("idx", [P, NT])
        parts = S.sb("parts", [P, NT, PARTS, E], BF16)
        gateT = S.sb("gateT", [PARTS * E, T], BF16)
        sel_f, sel = S.sb("sel_f", [PARTS * E, E, P]), S.sb("sel", [PARTS * E, E, P], BF16)
        b1, b2_f = S.sb("b1", [P, E * L3_F]), S.sb("b2_f", [PARTS * E, D])
        b2_left, b2 = S.sb("b2_left", [PARTS * E, D]), S.sb("b2", [PARTS * E, PARTS, D], BF16)
        hidden, scaled = S.sb("hidden", [P, L3_SLOTS, BLK]), S.sb("scaled", [P, L3_SLOTS, BLK])
        yT = S.sb("yT", [P, BLK])
        pH, pC = S.ps("pH", [P, L3_SLOTS, BLK]), S.ps("pC", [P, 2, BLK])
        pY, pR = S.ps("pY", [P, BLK]), S.ps("pR", [P, BLK])
        (consts_in, sel_made, b2_made, routed, exp_ready, exped, order, split, turned, gate_kept, opened, rectified,
         weighed, downed, y_kept, y_turned, g_kept) = (S.sem(n) for n in (
             "consts_in", "sel_made", "b2_made", "routed", "exp_ready", "exped", "order", "split", "turned",
             "gate_kept", "opened", "rectified", "weighed", "downed", "y_kept", "y_turned", "g_kept"))
        block = S.block()
        STEPS, AHEAD = E * L3_F, L3_SLOTS - 1
        logits = pR[:, 0:NT * E].rearrange("p (t e) -> p t e", e=E)
        turned_parts = pH[:, :, :].bitcast(BF16)
        g_blocks = K.g[:, :, :].rearrange("p (b t) d -> p b t d", t=TPB)

        @block.sync
        def _(sp):
            sp.dma_start(sel_f[:, :, :], A["c_sel3"]).then_inc(consts_in, 16)
            sp.dma_start(b1[:, :], A["L3_b1_cols"]).then_inc(consts_in, 16)
            for a in range(PARTS):
                sp.dma_start(b2_f[a * E:(a + 1) * E, :], A["L3_ffn_b2"]).then_inc(consts_in, 16)
            sp.wait_ge(consts_in, 16 * (2 + PARTS))

        @block.tensor
        def _(pe):
            for t in range(NT):
                mm = pe.matmul(pR[:, t * E:(t + 1) * E], K.xnT[:, t * P:(t + 1) * P], K.wr3[:, :],
                               start=True, stop=True)
            mm.then_inc(routed, 1)
            pe.wait_ge(split, 1)
            for t in range(NT):
                mm = pe.transpose(turned_parts[0:PARTS * E, t // 8, t % 8 * P:(t % 8 + 1) * P],
                                  parts[:, t, :, :].rearrange("p a e -> p (a e)"), K.ident_b[:, :])
            mm.then_inc(turned, 1)
            pe.wait_ge(gate_kept, 2)
            pe.wait_ge(K.l3_loaded, 16 * 2)
            pe.wait_ge(sel_made, 1)
            pe.wait_ge(b2_made, 1)

            def open_step(b, n):
                e, f = divmod(n, L3_F)
                if n >= L3_SLOTS:
                    pe.wait_ge(rectified, STEPS * b + n - L3_SLOTS + 1)
                if f == 0 and e >= 2:
                    pe.wait_ge(weighed, STEPS * b + L3_F * (e - 1))
                mm = pe.matmul(pH[:, n % L3_SLOTS, :], K.w1_3[:, e, f * P:(f + 1) * P], K.xnT[:, bass.ts(b, BLK)],
                               start=True, stop=True)
                if f == 0:
                    mm = pe.matmul(pC[:, e % 2, :], sel[:, e, :], gateT[:, bass.ts(b, BLK)], start=True, stop=True)
                mm.then_inc(opened, 1)

            def close_step(b, n):
                pe.wait_ge(weighed, STEPS * b + n + 1)
                e, f = divmod(n, L3_F)
                pe.matmul(pY[:, :], K.w2_3[:, e, f, :], scaled[:, n % L3_SLOTS, :], start=False,
                          stop=(n == STEPS - 1)).then_inc(downed, 1)

            with pe.Fori(0, NB) as b:
                for a in range(PARTS):
                    pe.matmul(pY[:, :], b2[:, a, :], gateT[:, bass.ts(b, BLK)], start=(a == 0), stop=False)
                for n in range(STEPS + AHEAD):
                    if n < STEPS:
                        open_step(b, n)
                    if n >= AHEAD:
                        close_step(b, n - AHEAD)
                pe.wait_ge(y_kept, b + 1)
                for t in range(TPB):
                    mm = pe.transpose(pR[:, t * P:(t + 1) * P], yT[:, t * P:(t + 1) * P], K.ident[:, :])
                mm.then_inc(y_turned, 1)

        @block.scalar
        def _(act):
            act.wait_ge(exp_ready, 1)
            act.activation(gates[:, :, :], shifted[:, :, :], ACT.Exp).then_inc(exped, 1)
            act.wait_ge(consts_in, 16 * (2 + PARTS))
            act.activation(sel[:, :, :], sel_f[:, :, :], ACT.Copy).then_inc(sel_made, 1)
            act.wait_ge(turned, 1)
            for c in range(2):
                act.activation(gateT[:, c * 8 * P:(c + 1) * 8 * P], turned_parts[0:PARTS * E, c, :], ACT.Copy)\
                   .then_inc(gate_kept, 1)
            with act.Fori(0, NB) as b:
                for n in range(STEPS):
                    act.wait_ge(opened, STEPS * b + n + 1)
                    if n >= L3_SLOTS:
                        act.wait_ge(weighed, STEPS * b + n - L3_SLOTS + 1)
                    act.activation(hidden[:, n % L3_SLOTS, :], pH[:, n % L3_SLOTS, :], ACT.Relu,
                                   bias=b1[:, n:n + 1]).then_inc(rectified, 1)
                act.wait_ge(y_turned, b + 1)
                act.activation(g_blocks[:, b, :, :], pR[:, :].rearrange("p (t d) -> p t d", d=D), ACT.Copy)\
                   .then_inc(g_kept, 1)

        @block.vector
        def _(dve):
            chain = Chain(dve, order)

            def over_e(x):
                return x.unsqueeze(2).broadcast_to(SH)

            dve.wait_ge(routed, 1)
            chain(dve.tensor_tensor(raw[:, :, :], logits, K.row["L3_ffn_br"][:, :].unsqueeze(1).broadcast_to(SH),
                                    ALU.add))
            softmax_over(dve, exped, chain, raw[:, :, :], E, mx[:, :], shifted[:, :, :], total[:, :], gates[:, :, :],
                         exp_ready)
            iota = K.iota[:, 0:E].unsqueeze(1).broadcast_to(SH)
            chain(dve.reduce_max(mx[:, :], gates[:, :, :], AX.X))
            chain(dve.tensor_tensor(hit[:, :, :], gates[:, :, :], over_e(mx[:, :]), ALU.is_lt))
            chain(dve.scalar_tensor_tensor(cand[:, :, :], hit[:, :, :], float(4 * E), iota, ALU.mult, ALU.add))
            chain(dve.tensor_reduce(idx[:, :], cand[:, :, :], AX.X, ALU.min))
            chain(dve.tensor_tensor(chosen[:, :, :], iota, over_e(idx[:, :]), ALU.is_equal))
            chain(dve.tensor_tensor(chosen[:, :, :], chosen[:, :, :], over_e(mx[:, :]), ALU.mult))
            chain(dve.tensor_copy(parts[:, :, 0, :], chosen[:, :, :]))
            chain(dve.tensor_tensor(hit[:, :, :], chosen[:, :, :], parts[:, :, 0, :], ALU.subtract))
            chain(dve.tensor_copy(parts[:, :, 1, :], hit[:, :, :]))
            dve.tensor_tensor(parts[:, :, 2, :], hit[:, :, :], parts[:, :, 1, :], ALU.subtract).then_inc(split, 1)
            dve.wait_ge(consts_in, 16 * (2 + PARTS))
            chain(dve.tensor_copy(b2[:, 0, :], b2_f[:, :]))
            chain(dve.tensor_tensor(b2_left[:, :], b2_f[:, :], b2[:, 0, :], ALU.subtract))
            chain(dve.tensor_copy(b2[:, 1, :], b2_left[:, :]))
            dve.tensor_tensor(b2[:, 2, :], b2_left[:, :], b2[:, 1, :], ALU.subtract).then_inc(b2_made, 1)
            with dve.Fori(0, NB) as b:
                for n in range(STEPS):
                    dve.wait_ge(rectified, STEPS * b + n + 1)
                    if n >= L3_SLOTS:
                        dve.wait_ge(downed, STEPS * b + n - L3_SLOTS + 1)
                    dve.tensor_tensor(scaled[:, n % L3_SLOTS, :], hidden[:, n % L3_SLOTS, :], pC[:, n // L3_F % 2, :],
                                      ALU.mult).then_inc(weighed, 1)
                dve.wait_ge(downed, STEPS * (b + 1))
                dve.tensor_copy(yT[:, :], pY[:, :]).then_inc(y_kept, 1)


def recurrent_layers(nc, A, out):
    with ExitStack() as ctx:
        def sb(name, shape, dt=F32):
            return ctx.enter_context(nc.sbuf_tensor(f"k_{name}", list(shape), dt))

        def dram(name, shape, dt=F32):
            return nc.dram_tensor(f"k_{name}_dram", tuple(shape), dt, kind="Internal").ap()

        K = Kept()
        K.x, K.xn, K.s, K.g, K.v = (sb(n, [P, NT, D]) for n in ("x", "xn", "s", "g", "v"))
        K.xnT = sb("xnT", [D, T])
        K.ident, K.iota = sb("ident", [P, P]), sb("iota", [P, P])
        K.ident_b, K.above_b, K.ones_b, K.neg_above, K.neg_below = (
            sb(n, [P, P], BF16) for n in ("ident_b", "above_b", "ones_b", "neg_above", "neg_below"))
        K.w = {n: sb("w_" + n, [D, D]) for n in (
            "L0_attn_Wq", "L0_attn_Wk", "L0_attn_Wv", "L0_attn_Wo", "L0_ffn_weight", "L0_ffn_aux_weight1",
            "L0_ffn_aux_weight2", "L1_attn_Wq", "L1_attn_Wk", "L1_attn_Wv", "L2_Wq", "L2_Wk", "L2_Wv",
            "L3_attn_qw", "L3_attn_kw", "L3_attn_vw", "L3_attn_ow", "L3_qw_swapped", "L3_kw_swapped")}
        K.col = {n: sb("c_" + n, [D, 1]) for n in (
            "L0_attn_bq", "L0_attn_bk", "L1_attn_bq", "L1_attn_bk", "L2_bq", "L2_bk")}
        K.row = {n: sb("r_" + n, [P, w]) for n, w in (
            ("L0_attn_bv", D), ("L0_attn_bo", D), ("L0_ffn_bias", D), ("L1_attn_bv", D), ("L1_ffn_e_score_bias", L1_E),
            ("L2_bv", D), ("L3_ffn_br", L3_E))}
        K.floor, K.after = sb("floor", [P, NT]), sb("after", [P, NT])
        K.wr1, K.wg2, K.wr3 = sb("wr1", [D, L1_E]), sb("wg2", [D, L2_E]), sb("wr3", [D, L3_E])
        K.combT, K.slot_token = sb("combT", [L2_E, T]), sb("slot_token", [L2_HALF, 2 * L2_E], I32)
        K.slot_i, K.coef = sb("slot_i", [P, 2, NT], I32), sb("coef", [P, 2, NT])
        K.w1_3, K.w2_3 = sb("w1_3", [D, L3_E, L3_H]), sb("w2_3", [P, L3_E, L3_F, D])
        K.parts = [dram(f"parts{w}", (HEADS, PARTS, HD, T), BF16) for w in range(2)]
        K.head_out = dram("head_out", (HEADS, HD + 1, T))
        K.table = dram("table", (L2_TABLE, 1), I32)
        K.xn_rows, K.hid_rows = dram("xn_rows", (T, D)), dram("hid_rows", (T, L2_H))
        K.h_rows, K.y_rows = dram("h_rows", (L2_SLOTS, L2_H)), dram("y_rows", (L2_SLOTS, D))
        K.w1_2, K.w2_2 = A["L2_W1"], A["L2_W2"]
        K.l1_loaded, K.l3_loaded = nc.alloc_semaphore("l1_loaded"), nc.alloc_semaphore("l3_loaded")

        with ExitStack() as layer1:
            def sb1(name, shape):
                return layer1.enter_context(nc.sbuf_tensor(f"k_{name}", list(shape), F32))

            K.gate1, K.up1, K.down1 = sb1("gate1", [D, L1_E * L1_I]), sb1("up1", [D, L1_E * L1_I]), sb1(
                "down1", [P, L1_J, D])
            K.sgate1, K.sup1, K.sdown1 = (sb1(n, [P, P]) for n in ("sgate1", "sup1", "sdown1"))
            load_constants(nc, K, A)
            residual_and_norm(nc, K, 0)
            head_projections(nc, K, 0, K.w["L0_attn_Wq"], K.w["L0_attn_Wk"], K.w["L0_attn_Wv"], K.col["L0_attn_bq"],
                             K.col["L0_attn_bk"], K.row["L0_attn_bv"])
            attention_heads(nc, K, 0, causal=False)
            finish_layer0(nc, K, A)
            residual_and_norm(nc, K, 1)
            attention_row_sums(nc, K, 1, K.w["L1_attn_Wq"], K.w["L1_attn_Wk"], K.w["L1_attn_Wv"], K.col["L1_attn_bq"],
                               K.col["L1_attn_bk"], K.row["L1_attn_bv"])
            ffn_top6(nc, K, A)
        residual_and_norm(nc, K, 2)
        attention_single(nc, K, 2, K.w["L2_Wq"], K.w["L2_Wk"], K.w["L2_Wv"], K.col["L2_bq"], K.col["L2_bk"],
                         K.row["L2_bv"])
        ffn_top2(nc, K, A)
        residual_and_norm(nc, K, 3)
        head_projections(nc, K, 3, K.w["L3_attn_qw"], K.w["L3_attn_kw"], K.w["L3_attn_vw"],
                         rope=(K.w["L3_qw_swapped"], K.w["L3_kw_swapped"], A["c_cos"], A["c_sin"]))
        attention_heads(nc, K, 3, causal=True)
        finish_layer3(nc, K)
        ffn_top1(nc, K, A)
        store_result(nc, K, out)


def constants():
    i, tok = np.arange(P), np.arange(NT)[None, :] * P + np.arange(P)[:, None]
    c = {"c_ident": np.eye(P), "c_above": i[None, :] > i[:, None], "c_below": i[None, :] < i[:, None],
         "c_ones": np.ones((P, P)), "c_iota": np.broadcast_to(i, (P, P)),
         "c_floor": np.where(tok == T - 1, LOWEST, 0.0), "c_after": T - 1 - tok}
    sel1, sel3 = np.zeros((PARTS, L1_E, L1_E, L1_I)), np.zeros((PARTS, L3_E, L3_E, P))
    sel1[:, np.arange(L1_E), np.arange(L1_E)] = 1
    sel3[:, np.arange(L3_E), np.arange(L3_E)] = 1
    c["c_sel1"], c["c_sel3"] = sel1.reshape(PARTS * L1_E, L1_E * L1_I), sel3.reshape(PARTS * L3_E, L3_E, P)
    group = np.arange(NT) // (NT // L2_GROUPS)
    c["c_base2"] = np.broadcast_to(2 * L2_HALF * np.arange(L2_E) + L2_CAP * group[:, None], (P, NT, L2_E))
    c["c_spare2"] = L2_SLOTS + T * np.arange(2)[None, :, None] + tok[:, None, :]
    f32 = np.float32
    freq = np.arange(T, dtype=f32)[None, :] * (f32(1) / f32(10000) ** (np.arange(0, HD, 2, dtype=f32) / f32(HD)))[:, None]
    sign = np.where(np.arange(HD) % 2 == 0, -1, 1)[:, None]
    c["c_cos"] = np.tile(np.repeat(np.cos(freq), 2, axis=0), (HEADS, 1))
    c["c_sin"] = np.tile(np.repeat(np.sin(freq), 2, axis=0) * sign, (HEADS, 1))
    c = {n: np.ascontiguousarray(a, dtype=np.float32) for n, a in c.items()}
    c["c_token"] = np.ascontiguousarray(tok, dtype=np.int32)
    return c


def layouts(I):
    A = {n: a for n, a in I.items() if n[:3] in ("L0_", "L1_", "L3_") or n.startswith("L2_ffn")}
    A["x"] = A.pop("L0_attn_x").reshape(T, D)
    gate_up = A.pop("L1_ffn_gate_up_proj")
    A["gate1"] = gate_up[:, :L1_I].reshape(L1_E * L1_I, D).T
    A["up1"] = gate_up[:, L1_I:].reshape(L1_E * L1_I, D).T
    A["down1"] = A.pop("L1_ffn_down_proj").transpose(0, 2, 1).reshape(L1_J, P, D).transpose(1, 0, 2)
    for n, m in (("sgate1", "shared_gate_w"), ("sup1", "shared_up_w"), ("sdown1", "shared_down_w"),
                 ("wr1", "router_weight")):
        A[n] = A.pop("L1_ffn_" + m).T
    for n, m in enumerate("qkv"):
        A["L2_W" + m] = I["L2_attn_W_qkv"][n * D:(n + 1) * D].T
        A["L2_b" + m] = I["L2_attn_b_qkv"][n * D:(n + 1) * D]
    A["wg2"] = A.pop("L2_ffn_Wg")
    A["L2_W1"] = A.pop("L2_ffn_W1").reshape(L2_E, D, 1, L2_H)
    A["L2_W2"] = A.pop("L2_ffn_W2").reshape(L2_E, L2_H // P, P, D).transpose(0, 2, 1, 3)
    for m in ("qw", "kw"):
        A[f"L3_{m}_swapped"] = A["L3_attn_" + m].reshape(D, D // 2, 2)[:, :, ::-1].reshape(D, D)
    A["wr3"] = A.pop("L3_ffn_Wr")
    A["L3_b1_cols"] = A.pop("L3_ffn_b1").reshape(L3_E, L3_F, P).transpose(2, 0, 1).reshape(P, L3_E * L3_F)
    A["w1_3"] = A.pop("L3_ffn_W1").transpose(1, 0, 2)
    A["w2_3"] = A.pop("L3_ffn_W2").reshape(L3_E, L3_F, P, D).transpose(2, 0, 1, 3)
    return A


def kernel(**inputs):
    import concourse.bacc as _bacc
    from concourse.bass_utils import run_bass_kernel_spmd as _run

    nc = _bacc.Bacc("TRN2", target_bir_lowering=False, num_devices=1)
    arrays, A = {}, {}
    laid_out = layouts({n: np.asarray(a) for n, a in inputs.items()})
    laid_out.update(constants())
    for name, a in laid_out.items():
        a = np.ascontiguousarray(a)
        arrays[f"in_{name}_dram"] = a
        A[name] = nc.dram_tensor(f"in_{name}_dram", a.shape, mybir.dt.from_np(a.dtype), kind="ExternalInput").ap()
    out = nc.dram_tensor("out_0_dram", (T, D), F32, kind="ExternalOutput").ap()
    recurrent_layers(nc, A, out)
    r = _run(nc, [arrays], core_ids=[0])
    return r.results[0]["out_0_dram"].reshape(1, T, D)
```

```python
from contextlib import ExitStack

import concourse.bass as bass
import numpy as np
from concourse import mybir

F32, BF16, I32 = mybir.dt.float32, mybir.dt.bfloat16, mybir.dt.int32
ALU, ACT, AX = mybir.AluOpType, mybir.ActivationFunctionType, mybir.AxisListType

T = 2048
D = 128
P = 128
NT = T // P
BLK = 512
NB = T // BLK
TPB = BLK // P
HEADS = 16
HD = D // HEADS
PARTS = 3
STK = PARTS * PARTS * HD
VW = 32
LN_EPS = 1e-5
NEG = -1e30
LOWEST = -3e38
RSQRT_SEED = float(0x5F3759DF)


class Kept:
    pass


class Chain:

    def __init__(self, engine, sem):
        self.engine, self.sem, self.n = engine, sem, 0

    def __call__(self, ins):
        self.n += 1
        ins.then_inc(self.sem, 1)
        self.engine.wait_ge(self.sem, self.n)


class Stage:

    def __init__(self, nc, tag):
        self.nc, self.tag, self.ctx, self.sems = nc, tag, ExitStack(), []

    def __enter__(self):
        return self

    def __exit__(self, *said):
        done = self.ctx.__exit__(*said)
        self.nc.clear_and_free_semaphores(self.sems)
        self.nc.all_engine_barrier()
        return done

    def sb(self, name, shape, dt=F32):
        return self.ctx.enter_context(self.nc.sbuf_tensor(f"{self.tag}_{name}", list(shape), dt))

    def ps(self, name, shape, dt=F32):
        return self.ctx.enter_context(self.nc.psum_tensor(f"{self.tag}_{name}", list(shape), dt))

    def sem(self, name):
        sem = self.nc.alloc_semaphore(f"{self.tag}_{name}")
        self.sems.append(sem)
        return sem

    def block(self):
        return self.ctx.enter_context(self.nc.Block())


def rsqrt(dve, chain, y, v, t):
    chain(dve.tensor_scalar(t.bitcast(I32), v.bitcast(I32), 1, None, ALU.logical_shift_right))
    chain(dve.tensor_scalar(y.bitcast(I32), t.bitcast(I32), -1.0, RSQRT_SEED, ALU.mult, ALU.add))
    for _ in range(3):
        chain(dve.tensor_tensor(t, y, y, ALU.mult))
        chain(dve.tensor_tensor(t, t, v, ALU.mult))
        chain(dve.tensor_scalar(t, t, -0.5, 1.5, ALU.mult, ALU.add))
        chain(dve.tensor_tensor(y, y, t, ALU.mult))


def load_constants(nc, K, A):
    with Stage(nc, "load") as S:
        loaded, made = S.sem("loaded"), S.sem("made")
        small = S.sb("small", [P, 4, P])
        loads = [(K.x[:, :, :], A["x"].rearrange("(t p) d -> p t d", p=P)),
                 (K.ident[:, :], A["c_ident"]), (K.iota[:, :], A["c_iota"]),
                 (K.floor[:, :], A["c_floor"]), (K.after[:, :], A["c_after"]),
                 (K.wr1[:, :], A["wr1"]), (K.wg2[:, :], A["wg2"]), (K.wr3[:, :], A["wr3"])]
        loads += [(small[:, n, :], A[c]) for n, c in enumerate(("c_ident", "c_above", "c_below", "c_ones"))]
        loads += [(K.w[n][:, :], A[n]) for n in K.w]
        loads += [(K.col[n][:, :], A[n].rearrange("(p o) -> p o", o=1)) for n in K.col]
        loads += [(K.row[n][:, :], A[n].partition_broadcast(P)) for n in K.row]
        block = S.block()

        @block.sync
        def _(sp):
            with nc.allow_non_contiguous_dma(reason="bias columns"):
                for dst, src in loads:
                    sp.dma_start(dst, src).then_inc(loaded, 16)
            for dst, n in ((K.gate1, "gate1"), (K.up1, "up1"), (K.sgate1, "sgate1"), (K.sup1, "sup1"),
                           (K.sdown1, "sdown1")):
                sp.dma_start(dst[:, :], A[n]).then_inc(K.l1_loaded, 16)
            sp.dma_start(K.down1[:, :, :], A["down1"]).then_inc(K.l1_loaded, 16)
            sp.dma_start(K.w1_3[:, :, :], A["w1_3"]).then_inc(K.l3_loaded, 16)
            sp.dma_start(K.w2_3[:, :, :, :], A["w2_3"]).then_inc(K.l3_loaded, 16)
            sp.wait_ge(loaded, 16 * len(loads))

        @block.vector
        def _(dve):
            dve.wait_ge(loaded, 16 * len(loads))
            dve.tensor_copy(K.ident_b[:, :], small[:, 0, :]).then_inc(made, 1)
            dve.tensor_copy(K.above_b[:, :], small[:, 1, :]).then_inc(made, 1)
            dve.tensor_copy(K.ones_b[:, :], small[:, 3, :]).then_inc(made, 1)
            dve.tensor_scalar(K.neg_above[:, :], small[:, 1, :], NEG, None, ALU.mult).then_inc(made, 1)
            dve.tensor_scalar(K.neg_below[:, :], small[:, 2, :], NEG, None, ALU.mult).then_inc(made, 1)


def residual_and_norm(nc, K, layer):
    with Stage(nc, f"norm{layer}") as S:
        stats, mv = S.sb("stats", [P, NT, 6]), S.sb("mv", [P, NT, 2])
        var, rstd, tmp = S.sb("var", [P, NT]), S.sb("rstd", [P, NT]), S.sb("tmp", [P, NT])
        pT = S.ps("pT", [P, 2, BLK])
        order, gated, normed, turned, kept = (S.sem(n) for n in ("order", "gated", "normed", "turned", "kept"))
        gate = S.sb("gate", [P, NT, D]) if layer else None
        block = S.block()

        @block.scalar
        def _(act):
            if layer:
                for c in range(NB):
                    act.activation(gate[:, c * TPB:(c + 1) * TPB, :], K.g[:, c * TPB:(c + 1) * TPB, :],
                                   ACT.Silu).then_inc(gated, 1)
            for c in range(NB):
                act.wait_ge(turned, c + 1)
                act.activation(K.xnT[:, c * BLK:(c + 1) * BLK], pT[:, c % 2, :], ACT.Copy).then_inc(kept, 1)

        @block.vector
        def _(dve):
            chain = Chain(dve, order)
            if layer:
                for c in range(NB):
                    ts = slice(c * TPB, (c + 1) * TPB)
                    dve.wait_ge(gated, c + 1)
                    chain(dve.tensor_tensor(gate[:, ts, :], gate[:, ts, :], K.s[:, ts, :], ALU.mult))
                    chain(dve.tensor_tensor(K.x[:, ts, :], K.x[:, ts, :], gate[:, ts, :], ALU.add))
            for t in range(NT):
                last = dve.bn_stats(stats[:, t, :], K.x[:, t, :])
            chain(last)
            for t in range(NT):
                last = dve.bn_aggr(mv[:, t, :], stats[:, t, :])
            chain(last)
            chain(dve.tensor_scalar(var[:, :], mv[:, :, 1], LN_EPS, None, ALU.add))
            rsqrt(dve, chain, rstd[:, :], var[:, :], tmp[:, :])
            for t in range(NT):
                dve.tensor_scalar(K.xn[:, t, :], K.x[:, t, :], mv[:, t, 0:1], rstd[:, t:t + 1],
                                  ALU.subtract, ALU.mult).then_inc(normed, 1)

        @block.tensor
        def _(pe):
            for t in range(NT):
                if t % TPB == 0 and t >= 2 * TPB:
                    pe.wait_ge(kept, t // TPB - 1)
                pe.wait_ge(normed, t + 1)
                mm = pe.transpose(pT[:, t // TPB % 2, t % TPB * P:(t % TPB + 1) * P], K.xn[:, t, :], K.ident[:, :])
                if t % TPB == TPB - 1:
                    mm.then_inc(turned, 1)


def store_result(nc, K, out):
    with Stage(nc, "store") as S:
        gate = S.sb("gate", [P, NT, D])
        gated, order, summed, stored = (S.sem(n) for n in ("gated", "order", "summed", "stored"))
        block = S.block()
        out_rows = out.rearrange("(t p) d -> p t d", p=P)

        @block.scalar
        def _(act):
            for c in range(NB):
                act.activation(gate[:, c * TPB:(c + 1) * TPB, :], K.g[:, c * TPB:(c + 1) * TPB, :],
                               ACT.Silu).then_inc(gated, 1)

        @block.vector
        def _(dve):
            chain = Chain(dve, order)
            for c in range(NB):
                ts = slice(c * TPB, (c + 1) * TPB)
                dve.wait_ge(gated, c + 1)
                chain(dve.tensor_tensor(gate[:, ts, :], gate[:, ts, :], K.s[:, ts, :], ALU.mult))
                dve.tensor_tensor(K.x[:, ts, :], K.x[:, ts, :], gate[:, ts, :], ALU.add).then_inc(summed, 1)

        @block.sync
        def _(sp):
            for c in range(NB):
                ts = slice(c * TPB, (c + 1) * TPB)
                sp.wait_ge(summed, c + 1)
                sp.dma_start(out_rows[:, ts, :], K.x[:, ts, :]).then_inc(stored, 16)
            sp.wait_ge(stored, 16 * NB)


def head_projections(nc, K, layer, wq, wk, wv, bq=None, bk=None, bv=None, rope=None):
    with Stage(nc, f"proj{layer}") as S:
        ws = [(wq, bq), (wk, bk)]
        scale = float(np.float32(HD) ** np.float32(-0.5))
        full = S.sb("full", [P, 4, BLK])
        rest = S.sb("rest", [P, 4, BLK])
        parts = [[S.sb(f"part{w}{a}", [P, T], BF16) for a in range(PARTS)] for w in range(2)]
        pq = S.ps("pq", [P, 4, BLK])
        pv = S.ps("pv", [P, 2, BLK])
        swp = S.sb("swp", [P, 4, BLK]) if rope else None
        cos = S.sb("cos", [P, T]) if rope else None
        sin = S.sb("sin", [P, T]) if rope else None
        ps_swap = S.ps("ps_swap", [P, 2, BLK]) if rope else None
        bias = S.sb("bias", [P, 1]) if bq is not None else None
        (projected, vproj, taken, vkept, biased, order, whole, hi, r1, mid, lo, stored, tables) = (
            S.sem(n) for n in ("projected", "vproj", "taken", "vkept", "biased", "order", "whole", "hi", "r1", "mid",
                               "lo", "stored", "tables"))
        block = S.block()
        N = 2 * NB
        out_of_psum = whole if rope else taken

        @block.sync
        def _(sp):
            if rope:
                sp.dma_start(cos[:, :], rope[2]).then_inc(tables, 16)
                sp.dma_start(sin[:, :], rope[3]).then_inc(tables, 16)
            for w in range(2):
                for a, done in enumerate((hi, mid, lo)):
                    sp.wait_ge(done, NB * (w + 1))
                    sp.dma_start(K.parts[w][:, a, :, :], parts[w][a][:, :]).then_inc(stored, 16)
            sp.wait_ge(stored, 16 * 2 * PARTS)

        @block.tensor
        def _(pe):
            for n in range(N):
                w, b = divmod(n, NB)
                if n >= 4:
                    pe.wait_ge(out_of_psum, n - 3)
                mm = pe.matmul(pq[:, n % 4, :], ws[w][0][:, :], K.xnT[:, b * BLK:(b + 1) * BLK], start=True, stop=True)
                if rope:
                    if n >= 2:
                        pe.wait_ge(out_of_psum, n - 1)
                    mm = pe.matmul(ps_swap[:, n % 2, :], rope[w][:, :], K.xnT[:, b * BLK:(b + 1) * BLK],
                                   start=True, stop=True)
                mm.then_inc(projected, 1)
            for t in range(NT):
                if t % TPB == 0 and t >= 2 * TPB:
                    pe.wait_ge(vkept, t // TPB - 1)
                mm = pe.matmul(pv[:, t // TPB % 2, t % TPB * P:(t % TPB + 1) * P], K.xnT[:, t * P:(t + 1) * P],
                               wv[:, :], start=True, stop=True)
                if t % TPB == TPB - 1:
                    mm.then_inc(vproj, 1)

        @block.scalar
        def _(act):
            if bq is not None:
                act.mul(bias[:, :], bq[:, :], scale).then_inc(biased, 1)
                act.wait_ge(biased, 1)
            for n in range(N):
                w, b = divmod(n, NB)
                cols = slice(b * BLK, (b + 1) * BLK)
                if not rope:
                    act.wait_ge(projected, n + 1)
                    if n >= 4:
                        act.wait_ge(r1, n - 3)
                    b_w = (bias, bk)[w][:, :] if bq is not None else 0.0
                    act.activation(full[:, n % 4, :], pq[:, n % 4, :], ACT.Identity, bias=b_w,
                                   scale=scale if w == 0 else 1.0).then_inc(taken, 1)
                    act.wait_ge(taken, n + 1)
                else:
                    act.wait_ge(whole, n + 1)
                act.activation(parts[w][0][:, cols], full[:, n % 4, :], ACT.Copy).then_inc(hi, 1)
                act.wait_ge(r1, n + 1)
                act.activation(parts[w][1][:, cols], rest[:, n % 4, :], ACT.Copy).then_inc(mid, 1)

        @block.vector
        def _(dve):
            chain = Chain(dve, order)
            if rope:
                dve.wait_ge(tables, 32)
            for n in range(N):
                w, b = divmod(n, NB)
                cols = slice(b * BLK, (b + 1) * BLK)
                if rope:
                    dve.wait_ge(projected, n + 1)
                    chain(dve.tensor_tensor(swp[:, n % 4, :], ps_swap[:, n % 2, :], sin[:, cols], ALU.mult))
                    chain(dve.tensor_tensor(full[:, n % 4, :], pq[:, n % 4, :], cos[:, cols], ALU.mult))
                    turned = dve.tensor_tensor(full[:, n % 4, :], full[:, n % 4, :], swp[:, n % 4, :], ALU.add)
                    if w == 0:
                        chain(turned)
                        turned = dve.tensor_scalar(full[:, n % 4, :], full[:, n % 4, :], scale, None, ALU.mult)
                    turned.then_inc(whole, 1)
                dve.wait_ge(hi, n + 1)
                dve.tensor_tensor(rest[:, n % 4, :], full[:, n % 4, :], parts[w][0][:, cols],
                                  ALU.subtract).then_inc(r1, 1)
                dve.wait_ge(mid, n + 1)
                dve.tensor_tensor(parts[w][2][:, cols], rest[:, n % 4, :], parts[w][1][:, cols],
                                  ALU.subtract).then_inc(lo, 1)
            for c in range(NB):
                dve.wait_ge(vproj, c + 1)
                src = pv[:, c % 2, :].rearrange("p (t d) -> p t d", d=D)
                dst = K.v[:, c * TPB:(c + 1) * TPB, :]
                if bv is not None:
                    dve.tensor_tensor(dst, src, bv[:, :].unsqueeze(1).broadcast_to([P, TPB, D]), ALU.add)\
                       .then_inc(vkept, 1)
                else:
                    dve.tensor_copy(dst, src).then_inc(vkept, 1)


def causal_plan(causal):
    units, runs = [], []
    for u in range(NT):
        lo = u * P if causal else 0
        halves = []
        for a in range(2):
            cols = [(b, max(b * BLK, lo), (b + 1) * BLK) for b in (2 * a, 2 * a + 1) if (b + 1) * BLK > lo]
            if cols:
                halves.append((a, cols))
        units.append(halves)
    for i in range(NT):
        hi = (i + 1) * P if causal else T
        runs += [(i, b, min(BLK, hi - b * BLK), causal and hi <= (b + 1) * BLK) for b in range(NB) if b * BLK < hi]
    return units, runs


def attention_heads(nc, K, layer, causal):
    units, runs = causal_plan(causal)
    NR = len(runs)
    chunks = [(u, a, cols) for u, halves in enumerate(units) for a, cols in halves]
    NC = len(chunks)
    first_chunk = [min(n for n, c in enumerate(chunks) if c[0] == u) for u in range(NT)] + [NC]
    ROUND = 3
    LOOPED = (HEADS - 2) // ROUND * ROUND
    TURN_AT = 3
    ITEMS = NR + 1
    LEAD = TURN_AT + ITEMS // 3
    EVEN = 700
    FILLED = 3
    load = [EVEN + sum(c1 - c0 for _, cols in units[u] for _, c0, c1 in cols) for u in range(NT)]
    upto = [round(ITEMS * sum(load[:u]) / sum(load)) for u in range(NT + 1)]

    items = list(range(TURN_AT)) + [None] + list(range(TURN_AT, NR))
    first_items = [None] + list(range(NR))

    def ahead(u):
        return [(1, j) if j < ITEMS else (2, j - ITEMS) for j in range(upto[u] + LEAD, upto[u + 1] + LEAD)]

    with Stage(nc, f"heads{layer}") as S:
        qs = [S.sb(f"qs{i}", [P, T], BF16) for i in range(ROUND)]
        ks = [S.sb(f"ks{i}", [P, T], BF16) for i in range(ROUND)]
        vh = [S.sb(f"vh{i}", [P, NT, VW]) for i in range(ROUND)]
        ot = [S.sb(f"ot{i}", [P, BLK]) for i in range(ROUND)]
        probs = [S.sb(f"probs{i}", [P, T]) for i in range(2)]
        run_max = S.sb("run_max", [P, NT, NB])
        neg_max = S.sb("neg_max", [P, NT])
        left, warm = S.sb("left", [P, NT]), S.sb("warm", [P, 1])
        max_parts = S.sb("max_parts", [P, P // NT, NT], BF16)
        max_rows = S.sb("max_rows", [PARTS * NT, P], BF16)
        pS = S.ps("pS", [P, 2, 2 * BLK])
        pM = S.ps("pM", [P, FILLED, BLK])
        pO = S.ps("pO", [P, BLK])
        preset, scored, exped, filled, taken, splitting, split, rows_in, v_in, used, ot_kept, zeroed = (
            S.sem(n) for n in ("preset", "scored", "exped", "filled", "taken", "splitting", "split", "rows_in", "v_in",
                               "used", "ot_kept", "zeroed"))
        stacked = [S.sem(f"stacked{i}") for i in range(ROUND)]
        ot_stored = [S.sem(f"ot_stored{i}") for i in range(ROUND)]
        block = S.block()
        LOADS = 6

        def every_head(engine, one_head, start=0):
            for h in range(start):
                one_head(h // ROUND, h % ROUND)
            with engine.Fori(start // ROUND, LOOPED // ROUND) as p:
                for c in range(ROUND):
                    one_head(p, c)
            for h in range(LOOPED, HEADS):
                one_head(h // ROUND, h % ROUND)

        def exists(p, c):
            return not isinstance(p, int) or ROUND * p + c < HEADS

        @block.sync
        def _(sp):
            def load_stacks(p, c):
                h = ROUND * p + c
                for r in range(PARTS):
                    rows = slice(r * PARTS * HD, (r + 1) * PARTS * HD)
                    sp.dma_start(qs[c % ROUND][rows, :], K.parts[0][h].rearrange("a d t -> (a d) t"))\
                      .then_inc(stacked[c % ROUND], 16)
                    sp.dma_start(ks[c % ROUND][rows, :], K.parts[1][h, r].unsqueeze(0).broadcast_to([PARTS, HD, T]))\
                      .then_inc(stacked[c % ROUND], 16)

            def load_max_rows(p, c):
                g = ROUND * p + c
                last = not exists(p, c + 1)
                sp.wait_ge(taken, ITEMS * (g + 1) + (0 if last else TURN_AT))
                for a in range(PARTS):
                    sp.dma_start(qs[c % ROUND][STK + a:STK + a + 1, :].rearrange("o (t c) -> o t c", c=P),
                                 max_rows[a * NT:(a + 1) * NT, :]).then_inc(rows_in, 16)

            def one_head(p, c):
                if exists(p, c + 2):
                    sp.wait_ge(scored, NC * (ROUND * p + c) + 1)
                    load_stacks(p, c + 2)
                if exists(p, c + 1):
                    load_max_rows(p, c + 1)

            sp.wait_ge(preset, 1)
            load_stacks(0, 0)
            load_stacks(0, 1)
            load_max_rows(0, 0)
            every_head(sp, one_head)

        @block.gpsimd
        def _(pool):
            def take_v(p, c):
                h = ROUND * p + c
                if not isinstance(h, int) or h >= ROUND:
                    pool.wait_ge(ot_stored[c % ROUND], 16 * NB * (p + c // ROUND))
                pool.tensor_copy(vh[c % ROUND][:, :, 0:HD], K.v[:, :, bass.ds(h * HD, HD)]).then_inc(v_in, 1)

            def one_head(p, c):
                h = ROUND * p + c
                if exists(p, c + 1):
                    pool.wait_ge(used, NT * h + 2)
                    take_v(p, c + 1)
                pool.wait_ge(ot_kept, h + 2)
                for b in range(NB):
                    pool.dma_start(K.head_out[h, :, b * BLK:(b + 1) * BLK], ot[c][b * 32:b * 32 + HD + 1, :])\
                        .then_inc(ot_stored[c], 16)

            pool.wait_ge(preset, 2)
            take_v(0, 0)
            every_head(pool, one_head, start=ROUND)
            for c in range(ROUND):
                pool.wait_ge(ot_stored[c], 16 * NB * len(range(c, HEADS, ROUND)))

        @block.tensor
        def _(pe):
            def fill(p, c, j, run):
                g, n = ROUND * p + c, ITEMS * (ROUND * p + c) + j - 1
                slot = (ITEMS * c + j - 1) % FILLED
                if not isinstance(n, int) or n >= FILLED:
                    pe.wait_ge(taken, n - FILLED + 1)
                if run is None:
                    pe.wait_ge(split, g)
                    pe.transpose(pM[:, slot, :].bitcast(BF16)[:, 0:P],
                                 max_parts[:, :, :].rearrange("p a t -> p (a t)"), K.ident_b[:, :]).then_inc(filled, 1)
                else:
                    i, b, w, masked = runs[run]
                    if run == 0:
                        pe.wait_ge(stacked[c % ROUND], 16 * LOADS * (p + c // ROUND + 1))
                    mm = pe.matmul(pM[:, slot, 0:w], qs[c % ROUND][0:STK, i * P:(i + 1) * P],
                                   ks[c % ROUND][0:STK, b * BLK:b * BLK + w], start=True, stop=not masked)
                    if masked:
                        mm = pe.matmul(pM[:, slot, w - P:w], K.ident_b[:, :], K.neg_above[:, :], start=False, stop=True)
                    mm.then_inc(filled, 1)

            def score_chunk(p, c, n):
                h = ROUND * p + c
                u, _, cols = chunks[n]
                if n == 0:
                    pe.wait_ge(rows_in, 16 * PARTS * (h + 1))
                if not isinstance(h, int) or h > 0 or n >= 2:
                    pe.wait_ge(exped, NC * h + n - 1)
                for b, c0, c1 in cols:
                    o = c0 % (2 * BLK)
                    diag = causal and c0 == u * P
                    mm = pe.matmul(pS[:, (NC * c + n) % 2, o:o + c1 - c0],
                                   ks[c % ROUND][0:STK + PARTS, u * P:(u + 1) * P],
                                   qs[c % ROUND][0:STK + PARTS, c0:c1], start=True, stop=not diag)
                    if diag:
                        mm = pe.matmul(pS[:, (NC * c + n) % 2, o:o + P], K.ident_b[:, :], K.neg_below[:, :],
                                       start=False, stop=True)
                mm.then_inc(scored, 1)

            def sum_unit(p, c, u):
                h = ROUND * p + c
                if u == 0:
                    pe.wait_ge(v_in, h + 1)
                    pe.wait_ge(ot_kept, h + 1)
                pe.wait_ge(exped, NC * h + first_chunk[u + 1])
                for _, cols in units[u]:
                    for b, c0, c1 in cols:
                        mm = pe.matmul(pO[b * 32:b * 32 + VW, c0 - b * BLK:c1 - b * BLK], vh[c][:, u, :],
                                       probs[u % 2][:, c0:c1], start=(u == 0),
                                       stop=(u == (4 * b + 3 if causal else NT - 1)))
                mm.then_inc(used, 1)

            def one_head(p, c):
                for u in range(NT):
                    todo = [(c + d, j, items[j]) for d, j in ahead(u) if exists(p, c + d)]
                    if not exists(p, c + 2):
                        todo += [(c + d, 0, None) for d, j in ahead(u)
                                 if not exists(p, c + d) and exists(p, c + d - 1) and j == TURN_AT]
                    if u < NT - 1:
                        scores = [(c, n) for n in range(first_chunk[u + 1], first_chunk[u + 2])]
                    else:
                        scores = [(c + 1, n) for n in range(first_chunk[1])] if exists(p, c + 1) else []
                    places = len(scores) + 2
                    for k in range(places):
                        for item in todo[len(todo) * k // places:len(todo) * (k + 1) // places]:
                            fill(p, *item)
                        if k < len(scores):
                            score_chunk(p, *scores[k])
                        elif k == len(scores):
                            sum_unit(p, c, u)

            pe.wait_ge(preset, 2)
            for j in range(1, ITEMS):
                fill(0, 0, j, first_items[j])
            for j, run in enumerate(items[:LEAD]):
                fill(0, 1, j, run)
            for n in range(first_chunk[1]):
                score_chunk(0, 0, n)
            every_head(pe, one_head)

        @block.scalar
        def _(act):
            def one_head(p, c):
                h = ROUND * p + c
                for n, (u, _, cols) in enumerate(chunks):
                    act.wait_ge(scored, NC * h + n + 1)
                    act.wait_ge(used, NT * h + u + 1)
                    c0, c1 = cols[0][1], cols[-1][2]
                    o = c0 % (2 * BLK)
                    act.activation(probs[u % 2][:, c0:c1], pS[:, (NC * c + n) % 2, o:o + c1 - c0], ACT.Exp)\
                       .then_inc(exped, 1)

            act.activation(warm[:, :], K.x[:, 0, 0:1], ACT.Exp)
            every_head(act, one_head)

        @block.vector
        def _(dve):
            def take(p, c, j, run):
                g, n = ROUND * p + c, ITEMS * (ROUND * p + c) + j - 1
                slot = (ITEMS * c + j - 1) % FILLED
                dve.wait_ge(filled, n + 1)
                if run is not None:
                    i, b, w, _ = runs[run]
                    dve.reduce_max(run_max[:, i, b:b + 1], pM[:, slot, 0:w], AX.X).then_inc(taken, 1)
                else:
                    if not isinstance(g, int) or g > 1:
                        dve.wait_ge(rows_in, 16 * PARTS * (g - 1))
                    dve.tensor_copy(max_rows[:, :], pM[:, slot, :].bitcast(BF16)[0:PARTS * NT, 0:P]).then_inc(taken, 1)
                if j < ITEMS - 1 or not exists(p, c):
                    return
                dve.wait_ge(taken, ITEMS * (g + 1) - 1)
                dve.tensor_reduce(neg_max[:, :], run_max[:, :, :], AX.X, ALU.max, negate=True).then_inc(splitting, 1)
                dve.wait_ge(splitting, 4 * g + 1)
                dve.tensor_copy(max_parts[:, 0, :], neg_max[:, :]).then_inc(splitting, 1)
                dve.wait_ge(splitting, 4 * g + 2)
                dve.tensor_tensor(left[:, :], neg_max[:, :], max_parts[:, 0, :], ALU.subtract).then_inc(splitting, 1)
                dve.wait_ge(splitting, 4 * g + 3)
                dve.tensor_copy(max_parts[:, 1, :], left[:, :]).then_inc(splitting, 1)
                dve.wait_ge(splitting, 4 * g + 4)
                dve.tensor_tensor(max_parts[:, 2, :], left[:, :], max_parts[:, 1, :], ALU.subtract).then_inc(split, 1)

            def one_head(p, c):
                h = ROUND * p + c
                for u in range(NT):
                    for d, j in ahead(u):
                        if exists(p, c + d):
                            take(p, c + d, j, items[j])
                        elif exists(p, c + d - 1) and j == TURN_AT:
                            take(p, c + d, 0, None)
                dve.wait_ge(used, NT * (h + 1) + 2)
                dve.tensor_copy(ot[c][:, :], pO[:, :]).then_inc(ot_kept, 1)

            for i in range(ROUND):
                dve.memset(ks[i][64:96, :], 1.0)
            dve.memset(max_parts[:, PARTS:, :], 0.0)
            dve.memset(run_max[:, :, :], LOWEST).then_inc(preset, 1)
            for i in range(ROUND):
                dve.memset(vh[i][:, :, HD:VW], 0.0).then_inc(zeroed, 1)
            dve.wait_ge(zeroed, ROUND)
            for i in range(ROUND):
                last = dve.memset(vh[i][:, :, HD:HD + 1], 1.0)
            last.then_inc(preset, 1)
            dve.engine_nop().then_inc(used, 2)
            dve.engine_nop().then_inc(ot_kept, 1)
            for j in range(1, ITEMS):
                take(0, 0, j, first_items[j])
            for j, run in enumerate(items[:LEAD]):
                take(0, 1, j, run)
            every_head(dve, one_head)


def finish_layer0(nc, K, A):
    with Stage(nc, "finish0") as S:
        sums, den = S.sb("sums", [P, T]), S.sb("den", [P, T])
        h1, h2 = S.sb("h1", [P, T]), S.sb("h2", [P, T])
        biased = S.sb("biased", [P, 2, TPB, D])
        pH, pR = S.ps("pH", [P, 4, BLK]), S.ps("pR", [P, 4, BLK])
        (loaded, inverted, scaled, ffn, ffn_kept, rows, s_kept, b_kept, g_kept) = (S.sem(n) for n in (
            "loaded", "inverted", "scaled", "ffn", "ffn_kept", "rows", "s_kept", "b_kept", "g_kept"))
        block = S.block()

        @block.sync
        def _(sp):
            sp.dma_start(sums[:, :], K.head_out[:, 0:HD, :]).then_inc(loaded, 16)
            sp.dma_start(den[:, :], K.head_out[:, HD:HD + 1, :].broadcast_to([HEADS, HD, T])).then_inc(loaded, 16)
            sp.wait_ge(loaded, 32)

        @block.vector
        def _(dve):
            dve.wait_ge(loaded, 32)
            for b in range(NB):
                cols = slice(b * BLK, (b + 1) * BLK)
                dve.reciprocal(den[:, cols], den[:, cols]).then_inc(inverted, 1)
                dve.wait_ge(inverted, b + 1)
                dve.tensor_tensor(sums[:, cols], sums[:, cols], den[:, cols], ALU.mult).then_inc(scaled, 1)
            for c in range(2 * NB):
                dve.wait_ge(rows, c + 1)
                src = pR[:, c % 4, :].rearrange("p (t d) -> p t d", d=D)
                if c < NB:
                    row = K.row["L0_attn_bo"][:, :].unsqueeze(1).broadcast_to([P, TPB, D])
                    dve.tensor_tensor(K.s[:, c * TPB:(c + 1) * TPB, :], src, row, ALU.add).then_inc(s_kept, 1)
                else:
                    if c - NB >= 2:
                        dve.wait_ge(g_kept, c - NB - 1)
                    row = K.row["L0_ffn_bias"][:, :].unsqueeze(1).broadcast_to([P, TPB, D])
                    dve.tensor_tensor(biased[:, c % 2], src, row, ALU.add).then_inc(b_kept, 1)

        @block.scalar
        def _(act):
            for n in range(2 * NB):
                b = n % NB
                act.wait_ge(ffn, n + 1)
                act.activation((h1, h2)[n // NB][:, b * BLK:(b + 1) * BLK], pH[:, b, :], ACT.Copy)\
                   .then_inc(ffn_kept, 1)
            for c in range(NB):
                act.wait_ge(b_kept, c + 1)
                act.activation(K.g[:, c * TPB:(c + 1) * TPB, :], biased[:, c % 2], ACT.Tanh).then_inc(g_kept, 1)

        @block.tensor
        def _(pe):
            for n in range(2 * NB):
                b = n % NB
                if n >= NB:
                    pe.wait_ge(ffn_kept, n - NB + 1)
                w = K.w[("L0_ffn_weight", "L0_ffn_aux_weight1")[n // NB]]
                pe.matmul(pH[:, b, :], w[:, :], (K.xnT, h1)[n // NB][:, b * BLK:(b + 1) * BLK],
                          start=True, stop=True).then_inc(ffn, 1)
            for c in range(2 * NB):
                b = c % NB
                if c < NB:
                    pe.wait_ge(scaled, b + 1)
                else:
                    pe.wait_ge(ffn_kept, NB + b + 1)
                    pe.wait_ge(s_kept, b + 1)
                for t in range(TPB):
                    tok = slice(b * BLK + t * P, b * BLK + (t + 1) * P)
                    mm = pe.matmul(pR[:, b, t * P:(t + 1) * P], (sums, h2)[c // NB][:, tok],
                                   K.w[("L0_attn_Wo", "L0_ffn_aux_weight2")[c // NB]][:, :], start=True, stop=True)
                mm.then_inc(rows, 1)


def attention_row_sums(nc, K, layer, wq, wk, wv, bq, bk, bv):
    scale = float(np.float32(1.0) / np.sqrt(np.float32(D)))
    with Stage(nc, f"rowsum{layer}") as S:
        qT, kT = S.sb("qT", [P, T]), S.sb("kT", [P, T])
        probs = S.sb("probs", [P, 2, T])
        row_max, neg, den = S.sb("row_max", [P, NT]), S.sb("neg", [P, NT]), S.sb("den", [P, NT])
        zero_p, zero_neg = S.sb("zero_p", [P, NT]), S.sb("zero_neg", [P, NT])
        inv, weight = S.sb("inv", [P, NT]), S.sb("weight", [P, NT])
        pS = [S.ps(f"pS{n}", [P, T]) for n in range(2)]
        (projected, kept, vproj, vkept, scored, maxed, exped, order) = (
            S.sem(n) for n in ("projected", "kept", "vproj", "vkept", "scored", "maxed", "exped", "order"))
        block = S.block()

        @block.tensor
        def _(pe):
            for n in range(2 * NB):
                w, b = divmod(n, NB)
                pe.matmul(pS[w][:, b * BLK:(b + 1) * BLK], (wq, wk)[w][:, :], K.xnT[:, b * BLK:(b + 1) * BLK],
                          start=True, stop=True).then_inc(projected, 1)
            pe.wait_ge(kept, NB)
            for t in range(NT):
                mm = pe.matmul(pS[0][:, t * P:(t + 1) * P], K.xnT[:, t * P:(t + 1) * P], wv[:, :],
                               start=True, stop=True)
                if t % TPB == TPB - 1:
                    mm.then_inc(vproj, 1)
            pe.wait_ge(kept, 2 * NB)
            pe.wait_ge(vkept, NB)
            for i in range(NT):
                if i >= 2:
                    pe.wait_ge(exped, i - 1)
                hi = (i + 1) * P
                for b in range(-(-hi // BLK)):
                    c0, c1 = b * BLK, min((b + 1) * BLK, hi)
                    diag = c1 == hi
                    mm = pe.matmul(pS[i % 2][:, c0:c1], qT[:, i * P:(i + 1) * P], kT[:, c0:c1],
                                   start=True, stop=not diag)
                    if diag:
                        mm = pe.matmul(pS[i % 2][:, c1 - P:c1], K.ident_b[:, :], K.neg_above[:, :],
                                       start=False, stop=True)
                mm.then_inc(scored, 1)

        @block.scalar
        def _(act):
            for n in range(2 * NB):
                w, b = divmod(n, NB)
                act.wait_ge(projected, n + 1)
                act.activation((qT, kT)[w][:, b * BLK:(b + 1) * BLK], pS[w][:, b * BLK:(b + 1) * BLK], ACT.Identity,
                               bias=(bq, bk)[w][:, :]).then_inc(kept, 1)
            for i in range(NT):
                hi = (i + 1) * P
                act.wait_ge(maxed, i + 1)
                if i >= 2:
                    act.wait_ge(exped, i - 1)
                act.activation(probs[:, i % 2, 0:hi], pS[i % 2][:, 0:hi], ACT.Exp, bias=neg[:, i:i + 1], scale=scale,
                               accum_out=den[:, i:i + 1]).then_inc(exped, 1)
            act.activation(zero_p[:, :], zero_neg[:, :], ACT.Exp).then_inc(exped, 1)

        @block.vector
        def _(dve):
            chain = Chain(dve, order)
            for c in range(NB):
                dve.wait_ge(vproj, c + 1)
                dve.tensor_tensor(K.v[:, c * TPB:(c + 1) * TPB, :],
                                  pS[0][:, c * BLK:(c + 1) * BLK].rearrange("p (t d) -> p t d", d=D),
                                  bv[:, :].unsqueeze(1).broadcast_to([P, TPB, D]), ALU.add).then_inc(vkept, 1)
            for i in range(NT):
                col = slice(i, i + 1)
                dve.wait_ge(scored, i + 1)
                chain(dve.reduce_max(row_max[:, col], pS[i % 2][:, 0:(i + 1) * P], AX.X))
                chain(dve.tensor_tensor(row_max[:, col], row_max[:, col], K.floor[:, col], ALU.max))
                chain(dve.tensor_scalar(zero_neg[:, col], row_max[:, col], -scale, 0.0, ALU.mult, ALU.min))
                dve.tensor_scalar(neg[:, col], row_max[:, col], -scale, None, ALU.mult).then_inc(maxed, 1)
            dve.wait_ge(exped, NT + 1)
            chain(dve.tensor_tensor(zero_p[:, :], zero_p[:, :], K.after[:, :], ALU.mult))
            chain(dve.tensor_tensor(den[:, :], den[:, :], zero_p[:, :], ALU.add))
            chain(dve.reciprocal(inv[:, :], den[:, :]))
            chain(dve.tensor_tensor(weight[:, :], den[:, :], inv[:, :], ALU.mult))
            chain(dve.tensor_tensor(K.s[:, :, :], K.v[:, :, :], weight[:, :].unsqueeze(2).broadcast_to([P, NT, D]),
                                    ALU.mult))


def attention_single(nc, K, layer, wq, wk, wv, bq, bk, bv):
    scale = float(np.float32(1.0) / np.sqrt(np.float32(D)))
    with Stage(nc, f"single{layer}") as S:
        qT, kT = S.sb("qT", [P, T]), S.sb("kT", [P, T])
        probs = [S.sb(f"probs{n}", [P, T]) for n in range(2)]
        probsT = S.sb("probsT", [P, 2, NT, P])
        row_max, neg, den = S.sb("row_max", [P, NT]), S.sb("neg", [P, NT]), S.sb("den", [P, NT])
        inv = S.sb("inv", [P, NT])
        pS = S.ps("pS", [P, NB, BLK])
        pT = S.ps("pT", [P, 2, BLK])
        pO = S.ps("pO", [P, 2, BLK])
        (projected, kept, vproj, vkept, scored, maxed, exped, turned, turn_kept, summed, order, finished) = (
            S.sem(n) for n in ("projected", "kept", "vproj", "vkept", "scored", "maxed", "exped", "turned",
                               "turn_kept", "summed", "order", "finished"))
        block = S.block()
        groups = [-(-(i + 1) // TPB) for i in range(NT)]
        before = [sum(groups[:i]) for i in range(NT + 1)]

        @block.tensor
        def _(pe):
            for n in range(2 * NB):
                w, b = divmod(n, NB)
                if n >= NB:
                    pe.wait_ge(kept, n - NB + 1)
                pe.matmul(pS[:, b, :], (wq, wk)[w][:, :], K.xnT[:, b * BLK:(b + 1) * BLK], start=True, stop=True)\
                  .then_inc(projected, 1)
            for t in range(NT):
                c = t // TPB
                if t % TPB == 0 and c >= 2:
                    pe.wait_ge(vkept, c - 1)
                mm = pe.matmul(pT[:, c % 2, t % TPB * P:(t % TPB + 1) * P], K.xnT[:, t * P:(t + 1) * P], wv[:, :],
                               start=True, stop=True)
                if t % TPB == TPB - 1:
                    mm.then_inc(vproj, 1)
            pe.wait_ge(kept, 2 * NB)
            pe.wait_ge(vkept, NB)

            def scores(i):
                if i >= 1:
                    pe.wait_ge(exped, i)
                hi = (i + 1) * P
                for b in range(-(-hi // BLK)):
                    w = min(BLK, hi - b * BLK)
                    diag = b == i // TPB
                    mm = pe.matmul(pS[:, b, 0:w], qT[:, i * P:(i + 1) * P], kT[:, b * BLK:b * BLK + w],
                                   start=True, stop=not diag)
                    if diag:
                        mm = pe.matmul(pS[:, b, w - P:w], K.ident_b[:, :], K.neg_above[:, :], start=False, stop=True)
                mm.then_inc(scored, 1)

            def turn(i):
                pe.wait_ge(exped, i + 1)
                for c in range(groups[i]):
                    n = before[i] + c
                    if n >= 2:
                        pe.wait_ge(turn_kept, n - 1)
                    for j in range(c * TPB, min(i + 1, (c + 1) * TPB)):
                        mm = pe.transpose(pT[:, n % 2, j % TPB * P:(j % TPB + 1) * P],
                                          probs[i % 2][:, j * P:(j + 1) * P], K.ident[:, :])
                    mm.then_inc(turned, 1)

            def sums(i):
                if i >= 2:
                    pe.wait_ge(finished, i - 1)
                pe.wait_ge(turn_kept, before[i + 1])
                for j in range(i + 1):
                    mm = pe.matmul(pO[:, i % 2, 0:D], probsT[:, i % 2, j, :], K.v[:, j, :], start=(j == 0),
                                   stop=(j == i))
                mm.then_inc(summed, 1)

            for i in range(NT + 1):
                if i < NT:
                    scores(i)
                if i >= 1:
                    turn(i - 1)
                    sums(i - 1)

        @block.scalar
        def _(act):
            for n in range(2 * NB):
                w, b = divmod(n, NB)
                act.wait_ge(projected, n + 1)
                act.activation((qT, kT)[w][:, b * BLK:(b + 1) * BLK], pS[:, b, :], ACT.Identity,
                               bias=(bq, bk)[w][:, :]).then_inc(kept, 1)

            def keep_turned(i):
                for c in range(groups[i]):
                    n = before[i] + c
                    w = min(i + 1 - c * TPB, TPB) * P
                    act.wait_ge(turned, n + 1)
                    if i >= 2:
                        act.wait_ge(summed, i - 1)
                    act.activation(probsT[:, i % 2, c * TPB:c * TPB + w // P, :],
                                   pT[:, n % 2, 0:w].rearrange("p (j q) -> p j q", q=P), ACT.Copy).then_inc(turn_kept, 1)

            for i in range(NT + 1):
                if i >= 1:
                    keep_turned(i - 1)
                if i < NT:
                    act.wait_ge(maxed, i + 1)
                    act.activation(probs[i % 2][:, 0:(i + 1) * P],
                                   pS[:, :, :].rearrange("p b c -> p (b c)")[:, 0:(i + 1) * P], ACT.Exp,
                                   bias=neg[:, i:i + 1], scale=scale, accum_out=den[:, i:i + 1]).then_inc(exped, 1)

        @block.vector
        def _(dve):
            chain = Chain(dve, order)
            for c in range(NB):
                dve.wait_ge(vproj, c + 1)
                dve.tensor_tensor(K.v[:, c * TPB:(c + 1) * TPB, :], pT[:, c % 2, :].rearrange("p (t d) -> p t d", d=D),
                                  bv[:, :].unsqueeze(1).broadcast_to([P, TPB, D]), ALU.add).then_inc(vkept, 1)

            def maximum(i):
                dve.wait_ge(scored, i + 1)
                chain(dve.reduce_max(row_max[:, i:i + 1],
                                     pS[:, :, :].rearrange("p b c -> p (b c)")[:, 0:(i + 1) * P], AX.X))
                dve.tensor_scalar(neg[:, i:i + 1], row_max[:, i:i + 1], -scale, None, ALU.mult).then_inc(maxed, 1)

            def finish(i):
                dve.wait_ge(exped, i + 1)
                chain(dve.reciprocal(inv[:, i:i + 1], den[:, i:i + 1]))
                dve.wait_ge(summed, i + 1)
                dve.tensor_scalar(K.s[:, i, :], pO[:, i % 2, 0:D], inv[:, i:i + 1], None, ALU.mult)\
                   .then_inc(finished, 1)

            for i in range(NT + 1):
                if i < NT:
                    maximum(i)
                if i >= 1:
                    finish(i - 1)


L1_E, L1_I, L1_TOP = 32, 64, 6
L1_J = L1_E * L1_I // P


def softmax_over(dve, act_done, chain, logits, n, mx, shifted, total, gates, exp_ready):
    chain(dve.reduce_max(mx, logits, AX.X))
    dve.tensor_tensor(shifted, logits, mx.unsqueeze(2).broadcast_to([P, NT, n]), ALU.subtract).then_inc(exp_ready, 1)
    dve.wait_ge(act_done, 1)
    chain(dve.reduce_sum(total, gates, AX.X))
    chain(dve.reciprocal(total, total))
    chain(dve.tensor_tensor(gates, gates, total.unsqueeze(2).broadcast_to([P, NT, n]), ALU.mult))


def ffn_top6(nc, K, A):
    E = L1_E
    with Stage(nc, "top6") as S:
        shifted, gates, score = S.sb("shifted", [P, NT, E]), S.sb("gates", [P, NT, E]), S.sb("score", [P, NT, E])
        mask, hit = S.sb("mask", [P, NT, E]), S.sb("hit", [P, NT, E])
        mx, total = S.sb("mx", [P, NT]), S.sb("total", [P, NT])
        top, place = S.sb("top", [P, NT, 8]), S.sb("place", [P, NT, 8])
        place_u = S.sb("place_u", [P, NT, 8], mybir.dt.uint32)
        parts = S.sb("parts", [P, NT, PARTS, E], BF16)
        combT = S.sb("combT", [PARTS * E, T], BF16)
        sel_f, sel = S.sb("sel_f", [PARTS * E, L1_J * P]), S.sb("sel", [PARTS * E, L1_J * P], BF16)
        act_gate, hidden = S.sb("act_gate", [P, 2, BLK]), S.sb("hidden", [P, 2, BLK])
        yT = S.sb("yT", [P, BLK])
        pG, pU, pC = (S.ps(n, [P, 2, BLK]) for n in ("pG", "pU", "pC"))
        pY, pR = S.ps("pY", [P, BLK]), S.ps("pR", [P, BLK])
        (sel_in, sel_made, routed, exp_ready, exped, order, split, turned, comb_kept, opened, gated, mixed, downed,
         y_kept, y_turned, g_kept, mixing) = (S.sem(n) for n in (
             "sel_in", "sel_made", "routed", "exp_ready", "exped", "order", "split", "turned", "comb_kept", "opened",
             "gated", "mixed", "downed", "y_kept", "y_turned", "g_kept", "mixing"))
        block = S.block()
        STEPS = L1_J + 1
        logits = pR[:, :].rearrange("p (t e) -> p t e", e=E)
        turned_parts = pG[:, :, :].bitcast(BF16)
        g_blocks = K.g[:, :, :].rearrange("p (b t) d -> p b t d", t=TPB)

        @block.sync
        def _(sp):
            sp.dma_start(sel_f[:, :], A["c_sel1"]).then_inc(sel_in, 16)
            sp.wait_ge(sel_in, 16)

        @block.tensor
        def _(pe):
            for t in range(NT):
                mm = pe.matmul(pR[:, t * E:(t + 1) * E], K.xnT[:, t * P:(t + 1) * P], K.wr1[:, :],
                               start=True, stop=True)
            mm.then_inc(routed, 1)
            pe.wait_ge(split, 1)
            for t in range(NT):
                mm = pe.transpose(turned_parts[0:PARTS * E, t // 8, t % 8 * P:(t % 8 + 1) * P],
                                  parts[:, t, :, :].rearrange("p a e -> p (a e)"), K.ident_b[:, :])
            mm.then_inc(turned, 1)
            pe.wait_ge(comb_kept, 2)
            pe.wait_ge(K.l1_loaded, 16 * 6)
            pe.wait_ge(sel_made, 1)

            def open_step(b, n):
                if n >= 2:
                    pe.wait_ge(mixed, STEPS * b + n - 1)
                x = K.xnT[:, bass.ts(b, BLK)]
                gw, uw = (K.gate1[:, n * P:(n + 1) * P], K.up1[:, n * P:(n + 1) * P]) if n < L1_J else \
                    (K.sgate1[:, :], K.sup1[:, :])
                pe.matmul(pG[:, n % 2, :], gw, x, start=True, stop=True)
                mm = pe.matmul(pU[:, n % 2, :], uw, x, start=True, stop=True)
                if n < L1_J:
                    mm = pe.matmul(pC[:, n % 2, :], sel[:, n * P:(n + 1) * P], combT[:, bass.ts(b, BLK)],
                                   start=True, stop=True)
                mm.then_inc(opened, 1)

            def close_step(b, n):
                pe.wait_ge(mixed, STEPS * b + n + 1)
                w = K.down1[:, n, :] if n < L1_J else K.sdown1[:, :]
                pe.matmul(pY[:, :], w, hidden[:, n % 2, :], start=(n == 0), stop=(n == L1_J)).then_inc(downed, 1)

            with pe.Fori(0, NB) as b:
                for n in range(STEPS):
                    open_step(b, n)
                    if n >= 1:
                        close_step(b, n - 1)
                close_step(b, STEPS - 1)
                pe.wait_ge(y_kept, b + 1)
                for t in range(TPB):
                    mm = pe.transpose(pR[:, t * P:(t + 1) * P], yT[:, t * P:(t + 1) * P], K.ident[:, :])
                mm.then_inc(y_turned, 1)

        @block.scalar
        def _(act):
            act.wait_ge(sel_in, 16)
            act.activation(sel[:, :], sel_f[:, :], ACT.Copy).then_inc(sel_made, 1)
            act.wait_ge(exp_ready, 1)
            act.activation(gates[:, :, :], shifted[:, :, :], ACT.Exp).then_inc(exped, 1)
            act.wait_ge(turned, 1)
            for c in range(2):
                act.activation(combT[:, c * 8 * P:(c + 1) * 8 * P], turned_parts[0:PARTS * E, c, :], ACT.Copy)\
                   .then_inc(comb_kept, 1)
            with act.Fori(0, NB) as b:
                for n in range(STEPS):
                    act.wait_ge(opened, STEPS * b + n + 1)
                    if n >= 2:
                        act.wait_ge(mixed, STEPS * b + n - 1)
                    act.activation(act_gate[:, n % 2, :], pG[:, n % 2, :], ACT.Silu).then_inc(gated, 1)
                act.wait_ge(y_turned, b + 1)
                act.activation(g_blocks[:, b, :, :], pR[:, :].rearrange("p (t d) -> p t d", d=D), ACT.Copy)\
                   .then_inc(g_kept, 1)

        @block.vector
        def _(dve):
            chain = Chain(dve, order)
            dve.wait_ge(routed, 1)
            softmax_over(dve, exped, chain, logits, E, mx[:, :], shifted[:, :, :], total[:, :], gates[:, :, :],
                         exp_ready)
            chain(dve.tensor_tensor(score[:, :, :], gates[:, :, :],
                                    K.row["L1_ffn_e_score_bias"][:, :].unsqueeze(1).broadcast_to([P, NT, E]), ALU.add))
            for t in range(NT):
                last = dve.max(top[:, t, :], score[:, t, :])
            chain(last)
            for t in range(NT):
                last = dve.max_index(place_u[:, t, :], top[:, t, :], score[:, t, :])
            chain(last)
            chain(dve.tensor_copy(place[:, :, :], place_u[:, :, :]))
            iota = K.iota[:, 0:E].unsqueeze(1).broadcast_to([P, NT, E])
            for k in range(L1_TOP):
                at = place[:, :, k:k + 1].broadcast_to([P, NT, E])
                if k == 0:
                    chain(dve.tensor_tensor(mask[:, :, :], iota, at, ALU.is_equal))
                else:
                    chain(dve.tensor_tensor(hit[:, :, :], iota, at, ALU.is_equal))
                    chain(dve.tensor_tensor(mask[:, :, :], mask[:, :, :], hit[:, :, :], ALU.add))
            chain(dve.tensor_tensor(gates[:, :, :], gates[:, :, :], mask[:, :, :], ALU.mult))
            chain(dve.reduce_sum(total[:, :], gates[:, :, :], AX.X))
            chain(dve.tensor_scalar(total[:, :], total[:, :], 1e-12, None, ALU.max))
            chain(dve.reciprocal(total[:, :], total[:, :]))
            chain(dve.tensor_tensor(gates[:, :, :], gates[:, :, :], total[:, :].unsqueeze(2).broadcast_to([P, NT, E]),
                                    ALU.mult))
            chain(dve.tensor_copy(parts[:, :, 0, :], gates[:, :, :]))
            chain(dve.tensor_tensor(hit[:, :, :], gates[:, :, :], parts[:, :, 0, :], ALU.subtract))
            chain(dve.tensor_copy(parts[:, :, 1, :], hit[:, :, :]))
            dve.tensor_tensor(parts[:, :, 2, :], hit[:, :, :], parts[:, :, 1, :], ALU.subtract).then_inc(split, 1)
            with dve.Fori(0, NB) as b:
                for n in range(STEPS):
                    dve.wait_ge(gated, STEPS * b + n + 1)
                    if n >= 2:
                        dve.wait_ge(downed, STEPS * b + n - 1)
                    mix = dve.tensor_tensor(hidden[:, n % 2, :], act_gate[:, n % 2, :], pU[:, n % 2, :], ALU.mult)
                    if n < L1_J:
                        mix.then_inc(mixing, 1)
                        dve.wait_ge(mixing, L1_J * b + n + 1)
                        mix = dve.tensor_tensor(hidden[:, n % 2, :], hidden[:, n % 2, :], pC[:, n % 2, :], ALU.mult)
                    mix.then_inc(mixed, 1)
                dve.wait_ge(downed, STEPS * (b + 1))
                dve.tensor_copy(yT[:, :], pY[:, :]).then_inc(y_kept, 1)


L2_E, L2_H, L2_GROUPS = 24, 512, 4
L2_CAP = -(-2 * (T // L2_GROUPS) // L2_E)
L2_HALF = L2_CAP * L2_GROUPS // 2
L2_SLOTS = L2_E * 2 * L2_HALF
L2_TABLE = -(-(L2_SLOTS + 2 * T) // P) * P
L2_LN_EPS = 1e-6
LOOP_EXPERTS = 4
LOOP_HALVES = 2 * LOOP_EXPERTS
LOOPS = L2_E // LOOP_EXPERTS


def route_top2(nc, K, A):
    E, SH = L2_E, [P, NT, L2_E]
    with Stage(nc, "route2") as S:
        raw, shifted, gates = S.sb("raw", SH), S.sb("shifted", SH), S.sb("gates", SH)
        hit, cand, comb, prod = S.sb("hit", SH), S.sb("cand", SH), S.sb("comb", SH), S.sb("prod", SH)
        chosen, kept = [S.sb(f"chosen{c}", SH) for c in range(2)], [S.sb(f"kept{c}", SH) for c in range(2)]
        ones_of = [S.sb(f"ones_of{c}", SH, BF16) for c in range(2)]
        base, spare = S.sb("base", SH), S.sb("spare", [P, 2, NT])
        mx, total, idx = S.sb("mx", [P, NT]), S.sb("total", [P, NT]), S.sb("idx", [P, NT])
        weight, slot, held = S.sb("weight", [P, 2, NT]), S.sb("slot", [P, 2, NT]), S.sb("held", [P, 2, NT])
        place = S.sb("place", [P, 2, NT])
        place_i = S.sb("place_i", [P, 2, NT], I32)
        token_i, zero_i = S.sb("token_i", [P, NT], I32), S.sb("zero_i", [P, L2_TABLE // P], I32)
        pL, pA, pB = S.ps("pL", [P, BLK]), S.ps("pA", [P, BLK]), S.ps("pB", [P, BLK])
        pT = S.ps("pT", [P, NB, BLK])
        (consts_in, xn_out, routed, exp_ready, exped, order, picked, located, placed, combined, turned, comb_kept,
         zeroed, cleared, scattered, slots_in) = (S.sem(n) for n in (
             "consts_in", "xn_out", "routed", "exp_ready", "exped", "order", "picked", "located", "placed", "combined",
             "turned", "comb_kept", "zeroed", "cleared", "scattered", "slots_in"))
        block = S.block()
        logits, loc = pL[:, 0:NT * E].rearrange("p (t e) -> p t e", e=E), [
            bank[:, 0:NT * E].rearrange("p (t e) -> p t e", e=E) for bank in (pA, pB)]
        table = K.table.rearrange("(p c) o -> p (c o)", p=P)

        @block.sync
        def _(sp):
            sp.dma_start(K.xn_rows.rearrange("(t p) d -> p t d", p=P), K.xn[:, :, :]).then_inc(xn_out, 16)
            sp.dma_start(base[:, :, :], A["c_base2"]).then_inc(consts_in, 16)
            sp.dma_start(spare[:, :, :], A["c_spare2"]).then_inc(consts_in, 16)
            sp.dma_start(token_i[:, :], A["c_token"]).then_inc(consts_in, 16)
            sp.wait_ge(xn_out, 16)
            sp.wait_ge(scattered, 16 * 2 * NT)
            with nc.allow_non_contiguous_dma(reason="a slot's token per partition"):
                sp.dma_start(K.slot_token[:, :],
                             K.table[0:L2_SLOTS, :].rearrange("(n r) o -> r (n o)", r=L2_HALF)).then_inc(slots_in, 16)
            sp.wait_ge(slots_in, 16)

        @block.tensor
        def _(pe):
            for t in range(NT):
                mm = pe.matmul(pL[:, t * E:(t + 1) * E], K.xnT[:, t * P:(t + 1) * P], K.wg2[:, :],
                               start=True, stop=True)
            mm.then_inc(routed, 1)
            tiles = NT // L2_GROUPS
            for c in range(2):
                pe.wait_ge(picked, c + 1)
                for t in range(NT):
                    g0 = t // tiles * tiles
                    adds = [(ones_of[c], j) for j in range(g0, t)]
                    if c == 1:
                        adds += [(ones_of[0], j) for j in range(g0, g0 + tiles)]
                    out = (pA, pB)[c][:, t * E:(t + 1) * E]
                    mm = pe.matmul(out, K.above_b[:, :], ones_of[c][:, t, :], start=True, stop=not adds)
                    for n, (o, j) in enumerate(adds):
                        mm = pe.matmul(out, K.ones_b[:, :], o[:, j, :], start=False, stop=n == len(adds) - 1)
                mm.then_inc(located, 1)
            pe.wait_ge(combined, 1)
            for t in range(NT):
                mm = pe.transpose(pT[0:E, t // TPB, t % TPB * P:(t % TPB + 1) * P], comb[:, t, :], K.ident[:, :])
            mm.then_inc(turned, 1)

        @block.scalar
        def _(act):
            act.wait_ge(exp_ready, 1)
            act.activation(gates[:, :, :], shifted[:, :, :], ACT.Exp).then_inc(exped, 1)
            act.wait_ge(turned, 1)
            act.activation(K.combT[:, :], pT[0:E, :, :].rearrange("e b c -> e (b c)"), ACT.Copy).then_inc(comb_kept, 1)

        @block.vector
        def _(dve):
            chain = Chain(dve, order)
            iota = K.iota[:, 0:E].unsqueeze(1).broadcast_to(SH)

            def over_e(x):
                return x.unsqueeze(2).broadcast_to(SH)

            def choose(values, c):
                chain(dve.reduce_max(mx[:, :], values[:, :, :], AX.X))
                chain(dve.tensor_tensor(hit[:, :, :], values[:, :, :], over_e(mx[:, :]), ALU.is_lt))
                chain(dve.scalar_tensor_tensor(cand[:, :, :], hit[:, :, :], float(4 * E), iota, ALU.mult, ALU.add))
                chain(dve.tensor_reduce(idx[:, :], cand[:, :, :], AX.X, ALU.min))
                chain(dve.tensor_tensor(chosen[c][:, :, :], iota, over_e(idx[:, :]), ALU.is_equal))
                dve.tensor_copy(ones_of[c][:, :, :], chosen[c][:, :, :]).then_inc(picked, 1)

            dve.memset(zero_i[:, :], 0).then_inc(zeroed, 1)
            dve.wait_ge(routed, 1)
            chain(dve.tensor_copy(raw[:, :, :], logits))
            softmax_over(dve, exped, chain, raw[:, :, :], E, mx[:, :], shifted[:, :, :], total[:, :],
                         gates[:, :, :], exp_ready)
            choose(gates, 0)
            chain(dve.scalar_tensor_tensor(raw[:, :, :], chosen[0][:, :, :], LOWEST, raw[:, :, :], ALU.mult, ALU.add))
            choose(raw, 1)
            dve.wait_ge(consts_in, 48)
            for c in range(2):
                dve.wait_ge(located, c + 1)
                chain(dve.scalar_tensor_tensor(kept[c][:, :, :], loc[c], float(L2_CAP), chosen[c][:, :, :],
                                               ALU.is_lt, ALU.mult))
                chain(dve.tensor_tensor(prod[:, :, :], gates[:, :, :], kept[c][:, :, :], ALU.mult))
                chain(dve.reduce_sum(weight[:, c, :], prod[:, :, :], AX.X))
                chain(dve.tensor_tensor(prod[:, :, :], loc[c], base[:, :, :], ALU.add))
                chain(dve.tensor_tensor(prod[:, :, :], prod[:, :, :], kept[c][:, :, :], ALU.mult))
                chain(dve.reduce_sum(slot[:, c, :], prod[:, :, :], AX.X))
                chain(dve.reduce_sum(held[:, c, :], kept[c][:, :, :], AX.X))
            chain(dve.tensor_tensor(place[:, :, :], held[:, :, :], spare[:, :, :], ALU.mult))
            chain(dve.tensor_tensor(place[:, :, :], spare[:, :, :], place[:, :, :], ALU.subtract))
            chain(dve.tensor_tensor(place[:, :, :], place[:, :, :], slot[:, :, :], ALU.add))
            dve.tensor_copy(place_i[:, :, :], place[:, :, :]).then_inc(placed, 1)
            chain(dve.tensor_copy(K.slot_i[:, :, :], slot[:, :, :]))
            chain(dve.tensor_tensor(total[:, :], weight[:, 0, :], weight[:, 1, :], ALU.add))
            chain(dve.tensor_scalar(total[:, :], total[:, :], 1e-9, None, ALU.max))
            chain(dve.reciprocal(total[:, :], total[:, :]))
            for c in range(2):
                last = dve.tensor_tensor(K.coef[:, c, :], weight[:, c, :], total[:, :], ALU.mult)
            chain(last)
            for c in range(2):
                last = dve.tensor_tensor((comb, prod)[c][:, :, :], kept[c][:, :, :], over_e(K.coef[:, c, :]), ALU.mult)
            chain(last)
            dve.tensor_tensor(comb[:, :, :], comb[:, :, :], prod[:, :, :], ALU.add).then_inc(combined, 1)

        @block.gpsimd
        def _(pool):
            pool.wait_ge(zeroed, 1)
            pool.dma_start(table, zero_i[:, :]).then_inc(cleared, 16)
            pool.wait_ge(cleared, 16)
            pool.wait_ge(placed, 1)
            for c in range(2):
                for t in range(NT):
                    pool.indirect_dma_start(
                        out=K.table, out_offset=bass.IndirectOffsetOnAxis(ap=place_i[:, c, t:t + 1], axis=0),
                        in_=token_i[:, t:t + 1], in_offset=None).then_inc(scattered, 16)
            pool.wait_ge(scattered, 16 * 2 * NT)


def expert_pass(nc, K, tag, src, weights, width_in, width_out, dst):
    F = width_in // P
    R = L2_HALF
    with Stage(nc, tag) as S:
        rows = [S.sb(f"rows{k}", [R, width_in]) for k in range(LOOP_HALVES)]
        rowsT = [S.sb(f"rowsT{n}", [P, F, R]) for n in range(2)]
        w = [S.sb(f"w{j}", [P, F, width_out]) for j in range(LOOP_EXPERTS)]
        outs = [S.sb(f"outs{k}", [R, width_out]) for k in range(LOOP_HALVES)]
        pT, pY = S.ps("pT", [P, 2, BLK]), S.ps("pY", [P, 2, BLK])
        turned, turn_kept, multiplied, kept = (S.sem(n) for n in (
            "turned", "turn_kept", "multiplied", "kept"))
        gathered = [S.sem(f"gathered{k}") for k in range(LOOP_HALVES)]
        stored = [S.sem(f"stored{k}") for k in range(LOOP_HALVES)]
        w_in = [S.sem(f"w_in{j}") for j in range(LOOP_EXPERTS)]
        block = S.block()
        w_loops = weights.rearrange("(l j) p f d -> l j p f d", j=LOOP_EXPERTS)
        dst_loops = dst.rearrange("(l k r) d -> l k r d", k=LOOP_HALVES, r=R)

        def every_loop(engine, body):
            body(0, True)
            with engine.Fori(1, LOOPS) as l:
                body(l, False)

        @block.sync
        def _(sp):
            def body(l, first):
                for j in range(LOOP_EXPERTS):
                    if not first:
                        sp.wait_ge(multiplied, LOOP_HALVES * (l - 1) + 2 * j + 2)
                    sp.dma_start(w[j][:, :, :], w_loops[l, j]).then_inc(w_in[j], 16)

            every_loop(sp, body)

        @block.gpsimd
        def _(pool):
            for n in range(2 * L2_E):
                if n >= LOOP_HALVES:
                    pool.wait_ge(turned, n - LOOP_HALVES + 1)
                k = n % LOOP_HALVES
                pool.indirect_dma_start(
                    out=rows[k][:, :], out_offset=None, in_=src,
                    in_offset=bass.IndirectOffsetOnAxis(ap=K.slot_token[:, n:n + 1], axis=0)).then_inc(gathered[k], 16)

        @block.tensor
        def _(pe):
            def turn(l, first, k):
                n = LOOP_HALVES * l + k
                pe.wait_ge(gathered[k], 16 * (l + 1))
                if not first or k >= 2:
                    pe.wait_ge(turn_kept, n - 1)
                for f in range(F):
                    mm = pe.transpose(pT[:, k % 2, f * R:(f + 1) * R], rows[k][:, f * P:(f + 1) * P],
                                      K.ident[0:R, 0:R])
                mm.then_inc(turned, 1)

            def multiply(l, first, k):
                n = LOOP_HALVES * l + k
                pe.wait_ge(turn_kept, n + 1)
                if k % 2 == 0:
                    pe.wait_ge(w_in[k // 2], 16 * (l + 1))
                if not first or k >= 2:
                    pe.wait_ge(kept, n - 1)
                for f in range(F):
                    mm = pe.matmul(pY[0:R, k % 2, 0:width_out], rowsT[k % 2][:, f, :], w[k // 2][:, f, :],
                                   start=(f == 0), stop=(f == F - 1))
                mm.then_inc(multiplied, 1)

            def body(l, first):
                for k in range(LOOP_HALVES):
                    turn(l, first, k)
                    if k >= 1:
                        multiply(l, first, k - 1)
                multiply(l, first, LOOP_HALVES - 1)

            every_loop(pe, body)

        @block.vector
        def _(dve):
            def body(l, first):
                for k in range(LOOP_HALVES):
                    n = LOOP_HALVES * l + k
                    dve.wait_ge(turned, n + 1)
                    if not first or k >= 2:
                        dve.wait_ge(multiplied, n - 1)
                    dve.tensor_copy(rowsT[k % 2][:, :, :], pT[:, k % 2, 0:F * R].rearrange("p (f r) -> p f r", r=R))\
                       .then_inc(turn_kept, 1)

            every_loop(dve, body)

        @block.scalar
        def _(act):
            def body(l, first):
                for k in range(LOOP_HALVES):
                    n = LOOP_HALVES * l + k
                    act.wait_ge(multiplied, n + 1)
                    if not first:
                        act.wait_ge(stored[k], 16 * l)
                    act.activation(outs[k][:, :], pY[0:R, k % 2, 0:width_out], ACT.Copy).then_inc(kept, 1)
                    act.wait_ge(kept, n + 1)
                    act.dma_start(dst_loops[l, k], outs[k][:, :]).then_inc(stored[k], 16)

            every_loop(act, body)
            for k in range(LOOP_HALVES):
                act.wait_ge(stored[k], 16 * LOOPS)


def combine_top2(nc, K, A, last):
    W = D if last else L2_H
    G = 1 if last else L2_GROUPS
    src = K.y_rows if last else K.h_rows
    with Stage(nc, f"combine{int(last)}") as S:
        got = [S.sb(f"got{c}", [P, 2 * TPB, W]) for c in range(2)]
        mixed = S.sb("mixed", [P, NT, W])
        bias_e = S.sb("bias_e", [L2_E, W])
        ln_w, ln_b = S.sb("ln_w", [P, G, W]), S.sb("ln_b", [P, G, W])
        stats, mv = S.sb("stats", [P, NT, 6]), S.sb("mv", [P, NT, 2])
        var, rstd, tmp = S.sb("var", [P, NT]), S.sb("rstd", [P, NT]), S.sb("tmp", [P, NT])
        pB = S.ps("pB", [P, 4, BLK])
        gathered = [S.sem(f"gathered{c}") for c in range(NB)]
        (loaded, biased, summed, taken, order, normed, rectified, stored) = (S.sem(n) for n in (
            "loaded", "biased", "summed", "taken", "order", "normed", "rectified", "stored"))
        block = S.block()
        names = ("L2_ffn_b2", "L2_ffn_ln_out_w", "L2_ffn_ln_out_b") if last else (
            "L2_ffn_b1", "L2_ffn_ln_hid_w", "L2_ffn_ln_hid_b")

        @block.sync
        def _(sp):
            sp.dma_start(bias_e[:, :], A[names[0]]).then_inc(loaded, 16)
            for dst, n in ((ln_w, names[1]), (ln_b, names[2])):
                row = A[n] if not last else A[n].unsqueeze(0)
                sp.dma_start(dst[:, :, :], row.partition_broadcast(P)).then_inc(loaded, 16)
            if not last:
                hid = K.hid_rows.rearrange("(t p) d -> p t d", p=P)
                for t in range(NT):
                    sp.wait_ge(rectified, t + 1)
                    sp.dma_start(hid[:, t, :], mixed[:, t, :]).then_inc(stored, 16)
                sp.wait_ge(stored, 16 * NT)
            sp.wait_ge(loaded, 48)

        @block.gpsimd
        def _(pool):
            for t in range(NT):
                if t % TPB == 0 and t >= 2 * TPB:
                    pool.wait_ge(taken, t - TPB)
                for c in range(2):
                    pool.indirect_dma_start(
                        out=got[c][:, t % (2 * TPB), :], out_offset=None, in_=src,
                        in_offset=bass.IndirectOffsetOnAxis(ap=K.slot_i[:, c, t:t + 1], axis=0)).then_inc(gathered[t // TPB], 16)

        @block.tensor
        def _(pe):
            pe.wait_ge(loaded, 48)
            for t in range(NT):
                if t >= 4:
                    pe.wait_ge(summed, t - 3)
                pe.matmul(pB[:, t % 4, 0:W], K.combT[:, t * P:(t + 1) * P], bias_e[:, :], start=True, stop=True)\
                  .then_inc(biased, 1)

        @block.vector
        def _(dve):
            chain = Chain(dve, order)
            dve.wait_ge(loaded, 48)
            for t in range(NT):
                dve.wait_ge(biased, t + 1)
                dve.wait_ge(gathered[t // TPB], 32 * TPB)
                dve.scalar_tensor_tensor(mixed[:, t, :], got[0][:, t % (2 * TPB), :], K.coef[:, 0, t:t + 1],
                                         pB[:, t % 4, 0:W], ALU.mult, ALU.add).then_inc(summed, 1)
                dve.wait_ge(summed, t + 1)
                dve.scalar_tensor_tensor(mixed[:, t, :], got[1][:, t % (2 * TPB), :], K.coef[:, 1, t:t + 1],
                                         mixed[:, t, :], ALU.mult, ALU.add).then_inc(taken, 1)
                dve.wait_ge(taken, t + 1)
                if last:
                    chain(dve.tensor_tensor(mixed[:, t, :], mixed[:, t, :], K.xn[:, t, :], ALU.add))
                chain(dve.bn_stats(stats[:, t, :], mixed[:, t, :]))
                if t % TPB < TPB - 1:
                    continue
                ts = slice(t - TPB + 1, t + 1)
                for u in range(t - TPB + 1, t + 1):
                    end = dve.bn_aggr(mv[:, u, :], stats[:, u, :])
                chain(end)
                chain(dve.tensor_scalar(var[:, ts], mv[:, ts, 1], L2_LN_EPS, None, ALU.add))
                rsqrt(dve, chain, rstd[:, ts], var[:, ts], tmp[:, ts])
                g = 0 if last else t // TPB
                for u in range(t - TPB + 1, t + 1):
                    out = K.g[:, u, :] if last else mixed[:, u, :]
                    chain(dve.scalar_tensor_tensor(mixed[:, u, :], mixed[:, u, :], mv[:, u, 0:1], ln_w[:, g, :],
                                                   ALU.subtract, ALU.mult))
                    dve.scalar_tensor_tensor(out, mixed[:, u, :], rstd[:, u:u + 1], ln_b[:, g, :],
                                             ALU.mult, ALU.add).then_inc(normed, 1)

        @block.scalar
        def _(act):
            if not last:
                for t in range(NT):
                    act.wait_ge(normed, t + 1)
                    act.activation(mixed[:, t, :], mixed[:, t, :], ACT.Relu).then_inc(rectified, 1)


def ffn_top2(nc, K, A):
    route_top2(nc, K, A)
    expert_pass(nc, K, "experts2a", K.xn_rows, K.w1_2, D, L2_H, K.h_rows)
    combine_top2(nc, K, A, last=False)
    expert_pass(nc, K, "experts2b", K.hid_rows, K.w2_2, L2_H, D, K.y_rows)
    combine_top2(nc, K, A, last=True)


def finish_layer3(nc, K):
    with Stage(nc, "finish3") as S:
        sums, den = S.sb("sums", [P, T]), S.sb("den", [P, T])
        pR = S.ps("pR", [P, NB, BLK])
        loaded, inverted, scaled, rows, s_kept = (S.sem(n) for n in ("loaded", "inverted", "scaled", "rows", "s_kept"))
        block = S.block()

        @block.sync
        def _(sp):
            sp.dma_start(sums[:, :], K.head_out[:, 0:HD, :]).then_inc(loaded, 16)
            sp.dma_start(den[:, :], K.head_out[:, HD:HD + 1, :].broadcast_to([HEADS, HD, T])).then_inc(loaded, 16)
            sp.wait_ge(loaded, 32)

        @block.vector
        def _(dve):
            dve.wait_ge(loaded, 32)
            for b in range(NB):
                cols = slice(b * BLK, (b + 1) * BLK)
                dve.reciprocal(den[:, cols], den[:, cols]).then_inc(inverted, 1)
                dve.wait_ge(inverted, b + 1)
                dve.tensor_tensor(sums[:, cols], sums[:, cols], den[:, cols], ALU.mult).then_inc(scaled, 1)

        @block.tensor
        def _(pe):
            for b in range(NB):
                pe.wait_ge(scaled, b + 1)
                for t in range(TPB):
                    tok = slice(b * BLK + t * P, b * BLK + (t + 1) * P)
                    mm = pe.matmul(pR[:, b, t * P:(t + 1) * P], sums[:, tok], K.w["L3_attn_ow"][:, :],
                                   start=True, stop=True)
                mm.then_inc(rows, 1)

        @block.scalar
        def _(act):
            for b in range(NB):
                act.wait_ge(rows, b + 1)
                act.activation(K.s[:, b * TPB:(b + 1) * TPB, :], pR[:, b, :].rearrange("p (t d) -> p t d", d=D),
                               ACT.Copy).then_inc(s_kept, 1)


L3_E, L3_H = 8, 512
L3_F = L3_H // P
L3_SLOTS = 3


def ffn_top1(nc, K, A):
    E, SH = L3_E, [P, NT, L3_E]
    with Stage(nc, "top1") as S:
        raw, shifted, gates = S.sb("raw", SH), S.sb("shifted", SH), S.sb("gates", SH)
        hit, cand, chosen = S.sb("hit", SH), S.sb("cand", SH), S.sb("chosen", SH)
        mx, total, idx = S.sb("mx", [P, NT]), S.sb("total", [P, NT]), S.sb("idx", [P, NT])
        parts = S.sb("parts", [P, NT, PARTS, E], BF16)
        gateT = S.sb("gateT", [PARTS * E, T], BF16)
        sel_f, sel = S.sb("sel_f", [PARTS * E, E, P]), S.sb("sel", [PARTS * E, E, P], BF16)
        b1, b2_f = S.sb("b1", [P, E * L3_F]), S.sb("b2_f", [PARTS * E, D])
        b2_left, b2 = S.sb("b2_left", [PARTS * E, D]), S.sb("b2", [PARTS * E, PARTS, D], BF16)
        hidden, scaled = S.sb("hidden", [P, L3_SLOTS, BLK]), S.sb("scaled", [P, L3_SLOTS, BLK])
        yT = S.sb("yT", [P, BLK])
        pH, pC = S.ps("pH", [P, L3_SLOTS, BLK]), S.ps("pC", [P, 2, BLK])
        pY, pR = S.ps("pY", [P, BLK]), S.ps("pR", [P, BLK])
        (consts_in, sel_made, b2_made, routed, exp_ready, exped, order, split, turned, gate_kept, opened, rectified,
         weighed, downed, y_kept, y_turned, g_kept) = (S.sem(n) for n in (
             "consts_in", "sel_made", "b2_made", "routed", "exp_ready", "exped", "order", "split", "turned",
             "gate_kept", "opened", "rectified", "weighed", "downed", "y_kept", "y_turned", "g_kept"))
        block = S.block()
        STEPS, AHEAD = E * L3_F, L3_SLOTS - 1
        logits = pR[:, 0:NT * E].rearrange("p (t e) -> p t e", e=E)
        turned_parts = pH[:, :, :].bitcast(BF16)
        g_blocks = K.g[:, :, :].rearrange("p (b t) d -> p b t d", t=TPB)

        @block.sync
        def _(sp):
            sp.dma_start(sel_f[:, :, :], A["c_sel3"]).then_inc(consts_in, 16)
            sp.dma_start(b1[:, :], A["L3_b1_cols"]).then_inc(consts_in, 16)
            for a in range(PARTS):
                sp.dma_start(b2_f[a * E:(a + 1) * E, :], A["L3_ffn_b2"]).then_inc(consts_in, 16)
            sp.wait_ge(consts_in, 16 * (2 + PARTS))

        @block.tensor
        def _(pe):
            for t in range(NT):
                mm = pe.matmul(pR[:, t * E:(t + 1) * E], K.xnT[:, t * P:(t + 1) * P], K.wr3[:, :],
                               start=True, stop=True)
            mm.then_inc(routed, 1)
            pe.wait_ge(split, 1)
            for t in range(NT):
                mm = pe.transpose(turned_parts[0:PARTS * E, t // 8, t % 8 * P:(t % 8 + 1) * P],
                                  parts[:, t, :, :].rearrange("p a e -> p (a e)"), K.ident_b[:, :])
            mm.then_inc(turned, 1)
            pe.wait_ge(gate_kept, 2)
            pe.wait_ge(K.l3_loaded, 16 * 2)
            pe.wait_ge(sel_made, 1)
            pe.wait_ge(b2_made, 1)

            def open_step(b, n):
                e, f = divmod(n, L3_F)
                if n >= L3_SLOTS:
                    pe.wait_ge(rectified, STEPS * b + n - L3_SLOTS + 1)
                if f == 0 and e >= 2:
                    pe.wait_ge(weighed, STEPS * b + L3_F * (e - 1))
                mm = pe.matmul(pH[:, n % L3_SLOTS, :], K.w1_3[:, e, f * P:(f + 1) * P], K.xnT[:, bass.ts(b, BLK)],
                               start=True, stop=True)
                if f == 0:
                    mm = pe.matmul(pC[:, e % 2, :], sel[:, e, :], gateT[:, bass.ts(b, BLK)], start=True, stop=True)
                mm.then_inc(opened, 1)

            def close_step(b, n):
                pe.wait_ge(weighed, STEPS * b + n + 1)
                e, f = divmod(n, L3_F)
                pe.matmul(pY[:, :], K.w2_3[:, e, f, :], scaled[:, n % L3_SLOTS, :], start=False,
                          stop=(n == STEPS - 1)).then_inc(downed, 1)

            with pe.Fori(0, NB) as b:
                for a in range(PARTS):
                    pe.matmul(pY[:, :], b2[:, a, :], gateT[:, bass.ts(b, BLK)], start=(a == 0), stop=False)
                for n in range(STEPS + AHEAD):
                    if n < STEPS:
                        open_step(b, n)
                    if n >= AHEAD:
                        close_step(b, n - AHEAD)
                pe.wait_ge(y_kept, b + 1)
                for t in range(TPB):
                    mm = pe.transpose(pR[:, t * P:(t + 1) * P], yT[:, t * P:(t + 1) * P], K.ident[:, :])
                mm.then_inc(y_turned, 1)

        @block.scalar
        def _(act):
            act.wait_ge(exp_ready, 1)
            act.activation(gates[:, :, :], shifted[:, :, :], ACT.Exp).then_inc(exped, 1)
            act.wait_ge(consts_in, 16 * (2 + PARTS))
            act.activation(sel[:, :, :], sel_f[:, :, :], ACT.Copy).then_inc(sel_made, 1)
            act.wait_ge(turned, 1)
            for c in range(2):
                act.activation(gateT[:, c * 8 * P:(c + 1) * 8 * P], turned_parts[0:PARTS * E, c, :], ACT.Copy)\
                   .then_inc(gate_kept, 1)
            with act.Fori(0, NB) as b:
                for n in range(STEPS):
                    act.wait_ge(opened, STEPS * b + n + 1)
                    if n >= L3_SLOTS:
                        act.wait_ge(weighed, STEPS * b + n - L3_SLOTS + 1)
                    act.activation(hidden[:, n % L3_SLOTS, :], pH[:, n % L3_SLOTS, :], ACT.Relu,
                                   bias=b1[:, n:n + 1]).then_inc(rectified, 1)
                act.wait_ge(y_turned, b + 1)
                act.activation(g_blocks[:, b, :, :], pR[:, :].rearrange("p (t d) -> p t d", d=D), ACT.Copy)\
                   .then_inc(g_kept, 1)

        @block.vector
        def _(dve):
            chain = Chain(dve, order)

            def over_e(x):
                return x.unsqueeze(2).broadcast_to(SH)

            dve.wait_ge(routed, 1)
            chain(dve.tensor_tensor(raw[:, :, :], logits, K.row["L3_ffn_br"][:, :].unsqueeze(1).broadcast_to(SH),
                                    ALU.add))
            softmax_over(dve, exped, chain, raw[:, :, :], E, mx[:, :], shifted[:, :, :], total[:, :], gates[:, :, :],
                         exp_ready)
            iota = K.iota[:, 0:E].unsqueeze(1).broadcast_to(SH)
            chain(dve.reduce_max(mx[:, :], gates[:, :, :], AX.X))
            chain(dve.tensor_tensor(hit[:, :, :], gates[:, :, :], over_e(mx[:, :]), ALU.is_lt))
            chain(dve.scalar_tensor_tensor(cand[:, :, :], hit[:, :, :], float(4 * E), iota, ALU.mult, ALU.add))
            chain(dve.tensor_reduce(idx[:, :], cand[:, :, :], AX.X, ALU.min))
            chain(dve.tensor_tensor(chosen[:, :, :], iota, over_e(idx[:, :]), ALU.is_equal))
            chain(dve.tensor_tensor(chosen[:, :, :], chosen[:, :, :], over_e(mx[:, :]), ALU.mult))
            chain(dve.tensor_copy(parts[:, :, 0, :], chosen[:, :, :]))
            chain(dve.tensor_tensor(hit[:, :, :], chosen[:, :, :], parts[:, :, 0, :], ALU.subtract))
            chain(dve.tensor_copy(parts[:, :, 1, :], hit[:, :, :]))
            dve.tensor_tensor(parts[:, :, 2, :], hit[:, :, :], parts[:, :, 1, :], ALU.subtract).then_inc(split, 1)
            dve.wait_ge(consts_in, 16 * (2 + PARTS))
            chain(dve.tensor_copy(b2[:, 0, :], b2_f[:, :]))
            chain(dve.tensor_tensor(b2_left[:, :], b2_f[:, :], b2[:, 0, :], ALU.subtract))
            chain(dve.tensor_copy(b2[:, 1, :], b2_left[:, :]))
            dve.tensor_tensor(b2[:, 2, :], b2_left[:, :], b2[:, 1, :], ALU.subtract).then_inc(b2_made, 1)
            with dve.Fori(0, NB) as b:
                for n in range(STEPS):
                    dve.wait_ge(rectified, STEPS * b + n + 1)
                    if n >= L3_SLOTS:
                        dve.wait_ge(downed, STEPS * b + n - L3_SLOTS + 1)
                    dve.tensor_tensor(scaled[:, n % L3_SLOTS, :], hidden[:, n % L3_SLOTS, :], pC[:, n // L3_F % 2, :],
                                      ALU.mult).then_inc(weighed, 1)
                dve.wait_ge(downed, STEPS * (b + 1))
                dve.tensor_copy(yT[:, :], pY[:, :]).then_inc(y_kept, 1)


def recurrent_layers(nc, A, out):
    with ExitStack() as ctx:
        def sb(name, shape, dt=F32):
            return ctx.enter_context(nc.sbuf_tensor(f"k_{name}", list(shape), dt))

        def dram(name, shape, dt=F32):
            return nc.dram_tensor(f"k_{name}_dram", tuple(shape), dt, kind="Internal").ap()

        K = Kept()
        K.x, K.xn, K.s, K.g, K.v = (sb(n, [P, NT, D]) for n in ("x", "xn", "s", "g", "v"))
        K.xnT = sb("xnT", [D, T])
        K.ident, K.iota = sb("ident", [P, P]), sb("iota", [P, P])
        K.ident_b, K.above_b, K.ones_b, K.neg_above, K.neg_below = (
            sb(n, [P, P], BF16) for n in ("ident_b", "above_b", "ones_b", "neg_above", "neg_below"))
        K.w = {n: sb("w_" + n, [D, D]) for n in (
            "L0_attn_Wq", "L0_attn_Wk", "L0_attn_Wv", "L0_attn_Wo", "L0_ffn_weight", "L0_ffn_aux_weight1",
            "L0_ffn_aux_weight2", "L1_attn_Wq", "L1_attn_Wk", "L1_attn_Wv", "L2_Wq", "L2_Wk", "L2_Wv",
            "L3_attn_qw", "L3_attn_kw", "L3_attn_vw", "L3_attn_ow", "L3_qw_swapped", "L3_kw_swapped")}
        K.col = {n: sb("c_" + n, [D, 1]) for n in (
            "L0_attn_bq", "L0_attn_bk", "L1_attn_bq", "L1_attn_bk", "L2_bq", "L2_bk")}
        K.row = {n: sb("r_" + n, [P, w]) for n, w in (
            ("L0_attn_bv", D), ("L0_attn_bo", D), ("L0_ffn_bias", D), ("L1_attn_bv", D), ("L1_ffn_e_score_bias", L1_E),
            ("L2_bv", D), ("L3_ffn_br", L3_E))}
        K.floor, K.after = sb("floor", [P, NT]), sb("after", [P, NT])
        K.wr1, K.wg2, K.wr3 = sb("wr1", [D, L1_E]), sb("wg2", [D, L2_E]), sb("wr3", [D, L3_E])
        K.combT, K.slot_token = sb("combT", [L2_E, T]), sb("slot_token", [L2_HALF, 2 * L2_E], I32)
        K.slot_i, K.coef = sb("slot_i", [P, 2, NT], I32), sb("coef", [P, 2, NT])
        K.w1_3, K.w2_3 = sb("w1_3", [D, L3_E, L3_H]), sb("w2_3", [P, L3_E, L3_F, D])
        K.parts = [dram(f"parts{w}", (HEADS, PARTS, HD, T), BF16) for w in range(2)]
        K.head_out = dram("head_out", (HEADS, HD + 1, T))
        K.table = dram("table", (L2_TABLE, 1), I32)
        K.xn_rows, K.hid_rows = dram("xn_rows", (T, D)), dram("hid_rows", (T, L2_H))
        K.h_rows, K.y_rows = dram("h_rows", (L2_SLOTS, L2_H)), dram("y_rows", (L2_SLOTS, D))
        K.w1_2, K.w2_2 = A["L2_W1"], A["L2_W2"]
        K.l1_loaded, K.l3_loaded = nc.alloc_semaphore("l1_loaded"), nc.alloc_semaphore("l3_loaded")

        with ExitStack() as layer1:
            def sb1(name, shape):
                return layer1.enter_context(nc.sbuf_tensor(f"k_{name}", list(shape), F32))

            K.gate1, K.up1, K.down1 = sb1("gate1", [D, L1_E * L1_I]), sb1("up1", [D, L1_E * L1_I]), sb1(
                "down1", [P, L1_J, D])
            K.sgate1, K.sup1, K.sdown1 = (sb1(n, [P, P]) for n in ("sgate1", "sup1", "sdown1"))
            load_constants(nc, K, A)
            residual_and_norm(nc, K, 0)
            head_projections(nc, K, 0, K.w["L0_attn_Wq"], K.w["L0_attn_Wk"], K.w["L0_attn_Wv"], K.col["L0_attn_bq"],
                             K.col["L0_attn_bk"], K.row["L0_attn_bv"])
            attention_heads(nc, K, 0, causal=False)
            finish_layer0(nc, K, A)
            residual_and_norm(nc, K, 1)
            attention_row_sums(nc, K, 1, K.w["L1_attn_Wq"], K.w["L1_attn_Wk"], K.w["L1_attn_Wv"], K.col["L1_attn_bq"],
                               K.col["L1_attn_bk"], K.row["L1_attn_bv"])
            ffn_top6(nc, K, A)
        residual_and_norm(nc, K, 2)
        attention_single(nc, K, 2, K.w["L2_Wq"], K.w["L2_Wk"], K.w["L2_Wv"], K.col["L2_bq"], K.col["L2_bk"],
                         K.row["L2_bv"])
        ffn_top2(nc, K, A)
        residual_and_norm(nc, K, 3)
        head_projections(nc, K, 3, K.w["L3_attn_qw"], K.w["L3_attn_kw"], K.w["L3_attn_vw"],
                         rope=(K.w["L3_qw_swapped"], K.w["L3_kw_swapped"], A["c_cos"], A["c_sin"]))
        attention_heads(nc, K, 3, causal=True)
        finish_layer3(nc, K)
        ffn_top1(nc, K, A)
        store_result(nc, K, out)


def constants():
    i, tok = np.arange(P), np.arange(NT)[None, :] * P + np.arange(P)[:, None]
    c = {"c_ident": np.eye(P), "c_above": i[None, :] > i[:, None], "c_below": i[None, :] < i[:, None],
         "c_ones": np.ones((P, P)), "c_iota": np.broadcast_to(i, (P, P)),
         "c_floor": np.where(tok == T - 1, LOWEST, 0.0), "c_after": T - 1 - tok}
    sel1, sel3 = np.zeros((PARTS, L1_E, L1_E, L1_I)), np.zeros((PARTS, L3_E, L3_E, P))
    sel1[:, np.arange(L1_E), np.arange(L1_E)] = 1
    sel3[:, np.arange(L3_E), np.arange(L3_E)] = 1
    c["c_sel1"], c["c_sel3"] = sel1.reshape(PARTS * L1_E, L1_E * L1_I), sel3.reshape(PARTS * L3_E, L3_E, P)
    group = np.arange(NT) // (NT // L2_GROUPS)
    c["c_base2"] = np.broadcast_to(2 * L2_HALF * np.arange(L2_E) + L2_CAP * group[:, None], (P, NT, L2_E))
    c["c_spare2"] = L2_SLOTS + T * np.arange(2)[None, :, None] + tok[:, None, :]
    f32 = np.float32
    freq = np.arange(T, dtype=f32)[None, :] * (f32(1) / f32(10000) ** (np.arange(0, HD, 2, dtype=f32) / f32(HD)))[:, None]
    sign = np.where(np.arange(HD) % 2 == 0, -1, 1)[:, None]
    c["c_cos"] = np.tile(np.repeat(np.cos(freq), 2, axis=0), (HEADS, 1))
    c["c_sin"] = np.tile(np.repeat(np.sin(freq), 2, axis=0) * sign, (HEADS, 1))
    c = {n: np.ascontiguousarray(a, dtype=np.float32) for n, a in c.items()}
    c["c_token"] = np.ascontiguousarray(tok, dtype=np.int32)
    return c


def layouts(I):
    A = {n: a for n, a in I.items() if n[:3] in ("L0_", "L1_", "L3_") or n.startswith("L2_ffn")}
    A["x"] = A.pop("L0_attn_x").reshape(T, D)
    gate_up = A.pop("L1_ffn_gate_up_proj")
    A["gate1"] = gate_up[:, :L1_I].reshape(L1_E * L1_I, D).T
    A["up1"] = gate_up[:, L1_I:].reshape(L1_E * L1_I, D).T
    A["down1"] = A.pop("L1_ffn_down_proj").transpose(0, 2, 1).reshape(L1_J, P, D).transpose(1, 0, 2)
    for n, m in (("sgate1", "shared_gate_w"), ("sup1", "shared_up_w"), ("sdown1", "shared_down_w"),
                 ("wr1", "router_weight")):
        A[n] = A.pop("L1_ffn_" + m).T
    for n, m in enumerate("qkv"):
        A["L2_W" + m] = I["L2_attn_W_qkv"][n * D:(n + 1) * D].T
        A["L2_b" + m] = I["L2_attn_b_qkv"][n * D:(n + 1) * D]
    A["wg2"] = A.pop("L2_ffn_Wg")
    A["L2_W1"] = A.pop("L2_ffn_W1").reshape(L2_E, D, 1, L2_H)
    A["L2_W2"] = A.pop("L2_ffn_W2").reshape(L2_E, L2_H // P, P, D).transpose(0, 2, 1, 3)
    for m in ("qw", "kw"):
        A[f"L3_{m}_swapped"] = A["L3_attn_" + m].reshape(D, D // 2, 2)[:, :, ::-1].reshape(D, D)
    A["wr3"] = A.pop("L3_ffn_Wr")
    A["L3_b1_cols"] = A.pop("L3_ffn_b1").reshape(L3_E, L3_F, P).transpose(2, 0, 1).reshape(P, L3_E * L3_F)
    A["w1_3"] = A.pop("L3_ffn_W1").transpose(1, 0, 2)
    A["w2_3"] = A.pop("L3_ffn_W2").reshape(L3_E, L3_F, P, D).transpose(2, 0, 1, 3)
    return A


def kernel(**inputs):
    import concourse.bacc as _bacc
    from concourse.bass_utils import run_bass_kernel_spmd as _run

    nc = _bacc.Bacc("TRN2", target_bir_lowering=False, num_devices=1)
    arrays, A = {}, {}
    laid_out = layouts({n: np.asarray(a) for n, a in inputs.items()})
    laid_out.update(constants())
    for name, a in laid_out.items():
        a = np.ascontiguousarray(a)
        arrays[f"in_{name}_dram"] = a
        A[name] = nc.dram_tensor(f"in_{name}_dram", a.shape, mybir.dt.from_np(a.dtype), kind="ExternalInput").ap()
    out = nc.dram_tensor("out_0_dram", (T, D), F32, kind="ExternalOutput").ap()
    recurrent_layers(nc, A, out)
    r = _run(nc, [arrays], core_ids=[0])
    return r.results[0]["out_0_dram"].reshape(1, T, D)
```

```python
from contextlib import ExitStack

import concourse.bass as bass
import numpy as np
from concourse import mybir

F32, BF16, I32 = mybir.dt.float32, mybir.dt.bfloat16, mybir.dt.int32
ALU, ACT, AX = mybir.AluOpType, mybir.ActivationFunctionType, mybir.AxisListType

T = 2048
D = 128
P = 128
NT = T // P
BLK = 512
NB = T // BLK
TPB = BLK // P
HEADS = 16
HD = D // HEADS
PARTS = 3
STK = PARTS * PARTS * HD
VW = 32
LN_EPS = 1e-5
NEG = -1e30
LOWEST = -3e38
WEIGHT_LOADS, L1_LOADS, L3_LOADS = 16 * 3, 16 * 3, 16 * 4
CLEAR = 2064
RSQRT_SEED = float(0x5F3759DF)


class Kept:
    pass


class Chain:

    def __init__(self, engine, sem):
        self.engine, self.sem, self.n = engine, sem, 0

    def __call__(self, ins):
        self.n += 1
        ins.then_inc(self.sem, 1)
        self.engine.wait_ge(self.sem, self.n)


class Stage:

    def __init__(self, nc, tag):
        self.nc, self.tag, self.ctx, self.sems = nc, tag, ExitStack(), []

    def __enter__(self):
        return self

    def __exit__(self, *said):
        done = self.ctx.__exit__(*said)
        self.nc.clear_and_free_semaphores(self.sems)
        self.nc.all_engine_barrier()
        return done

    def sb(self, name, shape, dt=F32):
        return self.ctx.enter_context(self.nc.sbuf_tensor(f"{self.tag}_{name}", list(shape), dt))

    def ps(self, name, shape, dt=F32):
        return self.ctx.enter_context(self.nc.psum_tensor(f"{self.tag}_{name}", list(shape), dt))

    def sem(self, name):
        sem = self.nc.alloc_semaphore(f"{self.tag}_{name}")
        self.sems.append(sem)
        return sem

    def block(self):
        return self.ctx.enter_context(self.nc.Block())


def rsqrt(dve, chain, y, v, t):
    chain(dve.tensor_scalar(t.bitcast(I32), v.bitcast(I32), 1, None, ALU.logical_shift_right))
    chain(dve.tensor_scalar(y.bitcast(I32), t.bitcast(I32), -1.0, RSQRT_SEED, ALU.mult, ALU.add))
    for _ in range(3):
        chain(dve.scalar_tensor_tensor(t, y, -0.5, y, ALU.mult, ALU.mult))
        chain(dve.tensor_tensor(t, t, v, ALU.mult))
        chain(dve.scalar_tensor_tensor(y, t, 1.5, y, ALU.add, ALU.mult))


def load_constants(nc, K, A):
    with Stage(nc, "load") as S:
        loaded, made = S.sem("loaded"), S.sem("made")
        masks = S.sb("masks", [P, 3, P])
        first = [(K.x[:, :, :], A["x"].rearrange("(t p) d -> p t d", p=P)), (K.ident[:, :], A["c_ident"]),
                 (masks[:, :, :], A["c_masks"])]
        block = S.block()

        @block.sync
        def _(sp):
            for dst, src in first:
                sp.dma_start(dst, src).then_inc(loaded, 16)
            for dst, n in ((K.squares, "squares"), (K.narrow, "narrow")):
                sp.dma_start(dst[:], A[n]).then_inc(K.weights_loaded, 16)
            sp.dma_start(K.rows_of[:, :], A["rows_of"].partition_broadcast(P)).then_inc(K.weights_loaded, 16)
            sp.wait_ge(loaded, 16 * len(first))

        @block.vector
        def _(dve):
            dve.memset(K.zeros[:, :], 0.0).then_inc(made, 1)
            dve.wait_ge(loaded, 16 * len(first))
            dve.tensor_copy(K.ident_b[:, :], K.ident[:, :]).then_inc(made, 1)
            dve.tensor_copy(K.above_b[:, :], masks[:, 0, :]).then_inc(made, 1)
            dve.tensor_copy(K.ones_b[:, :], masks[:, 2, :]).then_inc(made, 1)
            dve.tensor_scalar(K.neg_above[:, :], masks[:, 0, :], NEG, None, ALU.mult).then_inc(made, 1)
            dve.tensor_scalar(K.neg_below[:, :], masks[:, 1, :], NEG, None, ALU.mult).then_inc(made, 1)


def norm(nc, K, layer, loads=()):
    with Stage(nc, f"norm{layer}") as S:
        stats, mv = K.stats, S.sb("mv", [P, NT, 2])
        var, rstd, tmp = S.sb("var", [P, NT]), S.sb("rstd", [P, NT]), S.sb("tmp", [P, NT])
        pT = S.ps("pT", [P, 2, BLK])
        order, normed, turned, kept = (S.sem(n) for n in ("order", "normed", "turned", "kept"))
        block = S.block()

        @block.sync
        def _(sp):
            for dst, src, sem in loads:
                sp.dma_start(dst, src).then_inc(sem, 16)

        @block.scalar
        def _(act):
            for c in range(NB):
                act.wait_ge(turned, c + 1)
                act.activation(K.xnT[:, c * BLK:(c + 1) * BLK], pT[:, c % 2, :], ACT.Copy).then_inc(kept, 1)

        @block.vector
        def _(dve):
            chain = Chain(dve, order)
            if layer == 0:
                for t in range(NT):
                    last = dve.bn_stats(stats[:, t, :], K.x[:, t, :])
                chain(last)
            for t in range(NT):
                last = dve.bn_aggr(mv[:, t, :], stats[:, t, :])
            chain(last)
            chain(dve.tensor_scalar(var[:, :], mv[:, :, 1], LN_EPS, None, ALU.add))
            rsqrt(dve, chain, rstd[:, :], var[:, :], tmp[:, :])
            for t in range(NT):
                dve.tensor_scalar(K.xn[:, t, :], K.x[:, t, :], mv[:, t, 0:1], rstd[:, t:t + 1],
                                  ALU.subtract, ALU.mult).then_inc(normed, 1)

        @block.tensor
        def _(pe):
            for t in range(NT):
                if t % TPB == 0 and t >= 2 * TPB:
                    pe.wait_ge(kept, t // TPB - 1)
                pe.wait_ge(normed, t + 1)
                mm = pe.transpose(pT[:, t // TPB % 2, t % TPB * P:(t % TPB + 1) * P], K.xn[:, t, :], K.ident[:, :])
                if t % TPB == TPB - 1:
                    mm.then_inc(turned, 1)


class Top1Routing:

    def __init__(self, nc, K, S, logits_bank, places_bank):
        E, SH = L3_E, [P, NT, L3_E]
        self.K = K
        self.raw, self.shifted, self.gates, self.hit, self.cand, self.chosen, self.base, self.count, self.through = (
            S.sb(n, SH) for n in ("raw", "shifted", "gates", "hit", "cand", "chosen", "base", "count", "through"))
        self.ones_of = S.sb("ones_of", SH, BF16)
        self.none, self.total, self.idx, self.slot = (S.sb(n, [P, NT]) for n in ("none", "total", "idx", "slot"))
        self.fills, self.tiles_of, self.end, self.start = (
            S.sb("fills", [P, E, NT]), S.sb("tiles_of", [P, E]), S.sb("end", [P, E]), S.sb("start", [P, E]))
        self.behind, self.expert = S.sb("behind", [P, L3_TILES, E]), S.sb("expert", [P, L3_TILES])
        self.routed, self.exp_ready, self.exped, self.order, self.picked, self.located, self.counted = (
            S.sem(f"route_{n}") for n in ("routed", "exp_ready", "exped", "order", "picked", "located", "counted"))
        self.logits_bank, self.places_bank = logits_bank, places_bank
        self.logits = logits_bank[:, 0:NT * E].rearrange("p (t e) -> p t e", e=E)
        self.within, self.counts = (places_bank[:, n * NT * E:(n + 1) * NT * E].rearrange("p (t e) -> p t e", e=E)
                                    for n in range(2))

    def pe_logits(self, pe):
        for t in range(NT):
            mm = pe.matmul(self.logits_bank[:, t * L3_E:(t + 1) * L3_E], self.K.xnT[:, t * P:(t + 1) * P], self.K.wr3,
                           start=True, stop=True)
        mm.then_inc(self.routed, 1)

    def pe_places(self, pe):
        pe.wait_ge(self.picked, 1)
        ones = self.ones_of[:, :, :].rearrange("p t e -> p (t e)")
        n = NT * L3_E
        pe.matmul(self.places_bank[:, 0:n], self.K.above_b[:, :], ones, start=True, stop=True)
        pe.matmul(self.places_bank[:, n:2 * n], self.K.ones_b[:, :], ones, start=True, stop=True)\
          .then_inc(self.located, 1)

    def act_exp(self, act):
        act.wait_ge(self.exp_ready, 1)
        act.activation(self.gates[:, :, :], self.shifted[:, :, :], ACT.Exp).then_inc(self.exped, 1)

    def dve_step(self, dve, i):
        K, E, SH = self.K, L3_E, [P, NT, L3_E]
        gates, gate, total, hit, cand, chosen, base = (
            x[:] for x in (self.gates, K.gate, self.total, self.hit, self.cand, self.chosen, self.base))
        if i == 0:
            self.chain = Chain(dve, self.order)
        chain = self.chain

        def over_e(x):
            return x.unsqueeze(2).broadcast_to(SH)

        if i == 0:
            chain(dve.memset(self.none[:, :], 0.0))
            dve.wait_ge(self.routed, 1)
            chain(dve.tensor_tensor(self.raw[:, :, :], self.logits, K.row["L3_ffn_br"].unsqueeze(1).broadcast_to(SH),
                                    ALU.add))
            chain(dve.reduce_max(gate, self.raw[:, :, :], AX.X))
            dve.tensor_tensor(self.shifted[:, :, :], self.raw[:, :, :], over_e(gate), ALU.subtract)\
               .then_inc(self.exp_ready, 1)
        if i == 1:
            dve.wait_ge(self.exped, 1)
            chain(dve.reduce_sum(total, gates, AX.X))
            chain(dve.reciprocal(total, total))
            chain(dve.tensor_tensor(gates, gates, over_e(total), ALU.mult))
        if i == 2:
            iota = K.iota[:, 0:E].unsqueeze(1).broadcast_to(SH)
            chain(dve.reduce_max(gate, gates, AX.X))
            chain(dve.tensor_tensor(hit, gates, over_e(gate), ALU.is_lt))
            chain(dve.scalar_tensor_tensor(cand, hit, float(4 * E), iota, ALU.mult, ALU.add))
            chain(dve.tensor_reduce(self.idx[:, :], cand, AX.X, ALU.min))
            chain(dve.tensor_tensor(chosen, iota, over_e(self.idx[:, :]), ALU.is_equal))
            dve.tensor_copy(self.ones_of[:, :, :], chosen).then_inc(self.picked, 1)
        if i == 3:
            dve.wait_ge(self.located, 1)
            chain(dve.tensor_copy(self.count[:, :, :], self.counts))
            for e in range(E):
                last = dve.tensor_tensor_scan(self.through[:, :, e], self.count[:, :, e], self.none[:, :], 0.0,
                                              ALU.add, ALU.add)
            chain(last)
        if i == 4:
            chain(dve.scalar_tensor_tensor(self.fills[:, :, :],
                                           self.through[:, NT - 1, :].unsqueeze(2).broadcast_to([P, E, NT]),
                                           1.0 / P, K.iota[:, 0:NT].unsqueeze(1).broadcast_to([P, E, NT]),
                                           ALU.mult, ALU.is_gt))
            chain(dve.reduce_sum(self.tiles_of[:, :], self.fills[:, :, :], AX.X))
            chain(dve.tensor_tensor_scan(self.end[:, :], self.tiles_of[:, :], self.none[:, 0:E], 0.0, ALU.add, ALU.add))
            chain(dve.tensor_tensor(self.start[:, :], self.end[:, :], self.tiles_of[:, :], ALU.subtract))
        if i == 5:
            chain(dve.tensor_tensor(base, self.through[:, :, :], self.count[:, :, :], ALU.subtract))
            chain(dve.scalar_tensor_tensor(base, self.start[:, :].unsqueeze(1).broadcast_to(SH), float(P), base,
                                           ALU.mult, ALU.add))
            dve.tensor_tensor(base, base, self.within, ALU.add).then_inc(self.counted, 1)
            dve.wait_ge(self.counted, 1)
        if i == 6:
            chain(dve.tensor_tensor(base, base, chosen, ALU.mult))
            chain(dve.reduce_sum(self.slot[:, :], base, AX.X))
            dve.tensor_copy(K.slot3_i[:, :], self.slot[:, :])
        if i == 7:
            SB = [P, L3_TILES, E]
            chain(dve.tensor_tensor(self.behind[:, :, :], K.iota[:, 0:L3_TILES].unsqueeze(2).broadcast_to(SB),
                                    self.end[:, :].unsqueeze(1).broadcast_to(SB), ALU.is_ge))
            chain(dve.reduce_sum(self.expert[:, :], self.behind[:, :, :], AX.X))
            chain(dve.tensor_scalar(self.expert[:, :], self.expert[:, :], float(E - 1), None, ALU.min))
            dve.tensor_copy(K.tile_expert[:, :], self.expert[:, :])


def head_projections(nc, K, layer, wq, wk, wv, bq=None, bk=None, bv=None, rope=None, loads=()):
    with Stage(nc, f"proj{layer}") as S:
        scale = float(np.float32(HD) ** np.float32(-0.5))
        full = S.sb("full", [P, 4, BLK])
        rest = S.sb("rest", [P, 4, BLK])
        parts = [[S.sb(f"part{w}{a}", [P, T], BF16) for a in range(PARTS)] for w in range(2)]
        pq = S.ps("pq", [P, 4, BLK])
        pv = S.ps("pv", [P, 2, BLK])
        swp = S.sb("swp", [P, 2, BLK]) if rope else None
        ps_swap = S.ps("ps_swap", [P, 2, BLK]) if rope else None
        scaled = S.sb("scaled", [P, 2, D]) if rope else None
        bias = None if rope else S.sb("bias", [P, 1])
        (projected, vproj, taken, vkept, scaled_q, order, whole, hi, r1, mid, lo, stored) = (
            S.sem(n) for n in ("projected", "vproj", "taken", "vkept", "scaled_q", "order", "whole", "hi", "r1", "mid",
                               "lo", "stored"))
        routing = Top1Routing(nc, K, S, pv[:, 0, :], pv[:, 1, :]) if rope else None
        LOGITS_AT, ROUTE_AT, PLACES_AT = 1, (0, 1, 2, 5, 6, 6, 7, 8), 5
        block = S.block()
        N = 2 * NB
        whole = whole if rope else taken
        w_qk = (scaled[:, 0, :] if rope else wq, wk)
        w_swapped = (scaled[:, 1, :], rope[1]) if rope else None

        @block.sync
        def _(sp):
            if rope:
                sp.wait_ge(K.rope_loaded, 32)
            for dst, src, sem in loads:
                sp.dma_start(dst, src).then_inc(sem, 16)
            for w in range(2):
                for a, done in enumerate((hi, mid, lo)):
                    sp.wait_ge(done, NB * (w + 1))
                    sp.dma_start(K.parts[w][:, a, :, :], parts[w][a][:, :]).then_inc(stored, 16)
            sp.wait_ge(stored, 16 * 2 * PARTS)

        @block.tensor
        def _(pe):
            pe.wait_ge(K.weights_loaded, WEIGHT_LOADS)
            if rope:
                pe.wait_ge(scaled_q, 2)
            for n in range(N):
                w, b = divmod(n, NB)
                cols = slice(b * BLK, (b + 1) * BLK)
                if n >= 4:
                    pe.wait_ge(whole, n - 3)
                mm = pe.matmul(pq[:, n % 4, :], w_qk[w], K.xnT[:, cols], start=True, stop=True)
                if rope:
                    if n >= 2:
                        pe.wait_ge(whole, n - 1)
                    mm = pe.matmul(ps_swap[:, n % 2, :], w_swapped[w], K.xnT[:, cols], start=True, stop=True)
                mm.then_inc(projected, 1)
                if rope and n == LOGITS_AT:
                    routing.pe_logits(pe)
                if rope and n == PLACES_AT:
                    routing.pe_places(pe)
            if rope:
                pe.wait_ge(routing.counted, 1)
            for t in range(NT):
                if t % TPB == 0 and t >= 2 * TPB:
                    pe.wait_ge(vkept, t // TPB - 1)
                mm = pe.matmul(pv[:, t // TPB % 2, t % TPB * P:(t % TPB + 1) * P], K.xnT[:, t * P:(t + 1) * P],
                               wv, start=True, stop=True)
                if t % TPB == TPB - 1:
                    mm.then_inc(vproj, 1)

        def v_block(c):
            return K.v[:, c * TPB:(c + 1) * TPB, :], pv[:, c % 2, :].rearrange("p (t d) -> p t d", d=D)

        @block.scalar
        def _(act):
            act.wait_ge(K.weights_loaded, WEIGHT_LOADS)
            if rope:
                for i, w in enumerate((wq, rope[0])):
                    act.mul(scaled[:, i, :], w, scale).then_inc(scaled_q, 1)
            else:
                act.mul(bias[:, :], bq, scale).then_inc(scaled_q, 1)
                act.wait_ge(scaled_q, 1)
            for n in range(N + 1):
                w, b = divmod(n, NB)
                cols = slice(b * BLK, (b + 1) * BLK)
                if n < N and not rope:
                    act.wait_ge(projected, n + 1)
                    if n >= 4:
                        act.wait_ge(r1, n - 3)
                    act.activation(full[:, n % 4, :], pq[:, n % 4, :], ACT.Identity, bias=(bias[:, :], bk)[w],
                                   scale=scale if w == 0 else 1.0).then_inc(taken, 1)
                if n < N:
                    act.wait_ge(whole, n + 1)
                    act.activation(parts[w][0][:, cols], full[:, n % 4, :], ACT.Copy).then_inc(hi, 1)
                if n >= 1:
                    w, b = divmod(n - 1, NB)
                    act.wait_ge(r1, n)
                    act.activation(parts[w][1][:, b * BLK:(b + 1) * BLK], rest[:, (n - 1) % 4, :], ACT.Copy)\
                       .then_inc(mid, 1)
                if rope and n == ROUTE_AT[1]:
                    routing.act_exp(act)
            if rope:
                for c in range(NB):
                    act.wait_ge(vproj, c + 1)
                    act.activation(*v_block(c), ACT.Copy).then_inc(vkept, 1)

        @block.vector
        def _(dve):
            chain = Chain(dve, order)
            dve.wait_ge(K.weights_loaded, WEIGHT_LOADS)
            if rope:
                dve.wait_ge(K.rope_loaded, 32)

            def turn(n):
                w, b = divmod(n, NB)
                cols = slice(b * BLK, (b + 1) * BLK)
                dve.wait_ge(projected, n + 1)
                chain(dve.tensor_tensor(swp[:, n % 2, :], ps_swap[:, n % 2, :], rope[3][:, cols], ALU.mult))
                if n >= 4:
                    dve.wait_ge(hi, n - 3)
                chain(dve.tensor_tensor(full[:, n % 4, :], pq[:, n % 4, :], rope[2][:, cols], ALU.mult))
                dve.tensor_tensor(full[:, n % 4, :], full[:, n % 4, :], swp[:, n % 2, :], ALU.add).then_inc(whole, 1)

            if rope:
                turn(0)
            for n in range(N + 1):
                if rope and n + 1 < N:
                    turn(n + 1)
                if n < N:
                    w, b = divmod(n, NB)
                    dve.wait_ge(hi, n + 1)
                    if n >= 4:
                        dve.wait_ge(lo, n - 3)
                    dve.tensor_tensor(rest[:, n % 4, :], full[:, n % 4, :], parts[w][0][:, b * BLK:(b + 1) * BLK],
                                      ALU.subtract).then_inc(r1, 1)
                if n >= 1:
                    w, b = divmod(n - 1, NB)
                    cols = slice(b * BLK, (b + 1) * BLK)
                    dve.wait_ge(mid, n)
                    dve.tensor_tensor(parts[w][2][:, cols], rest[:, (n - 1) % 4, :], parts[w][1][:, cols],
                                      ALU.subtract).then_inc(lo, 1)
                if rope:
                    for i, at in enumerate(ROUTE_AT):
                        if at == n:
                            routing.dve_step(dve, i)
            if not rope:
                for c in range(NB):
                    dve.wait_ge(vproj, c + 1)
                    dst, src = v_block(c)
                    dve.tensor_tensor(dst, src, bv.unsqueeze(1).broadcast_to([P, TPB, D]), ALU.add).then_inc(vkept, 1)


def causal_plan(causal):
    units, runs = [], []
    for u in range(NT):
        lo = u * P if causal else 0
        halves = []
        for a in range(2):
            cols = [(b, max(b * BLK, lo), (b + 1) * BLK) for b in (2 * a, 2 * a + 1) if (b + 1) * BLK > lo]
            if cols:
                halves.append((a, cols))
        units.append(halves)
    for i in range(NT):
        hi = (i + 1) * P if causal else T
        runs += [(i, b, min(BLK, hi - b * BLK), causal and hi <= (b + 1) * BLK) for b in range(NB) if b * BLK < hi]
    return units, runs


def attention_heads(nc, K, layer, causal, scatter=None):
    units, runs = causal_plan(causal)
    NR = len(runs)
    chunks = [(u, a, cols) for u, halves in enumerate(units) for a, cols in halves]
    NC = len(chunks)
    first_chunk = [min(n for n, c in enumerate(chunks) if c[0] == u) for u in range(NT)] + [NC]
    ROUND = 3
    LOOPED = (HEADS - 2) // ROUND * ROUND
    TURN_AT = 12 if causal else 3
    ITEMS = NR + 1
    LEAD = TURN_AT + ITEMS // (3 if causal else 4)
    EVEN = 550
    FILLED = 3
    load = [EVEN + sum(c1 - c0 for _, cols in units[u] for _, c0, c1 in cols) for u in range(NT)]
    upto = [round(ITEMS * sum(load[:u]) / sum(load)) for u in range(NT + 1)]

    items = list(range(TURN_AT)) + [None] + list(range(TURN_AT, NR))
    first_items = [None] + list(range(NR))

    def ahead(u):
        return [(1, j) if j < ITEMS else (2, j - ITEMS) for j in range(upto[u] + LEAD, upto[u + 1] + LEAD)]

    with Stage(nc, f"heads{layer}") as S:
        qs = [S.sb(f"qs{i}", [P, T], BF16) for i in range(ROUND)]
        ks = [S.sb(f"ks{i}", [P, T], BF16) for i in range(ROUND)]
        vh = [S.sb(f"vh{i}", [P, NT, VW]) for i in range(ROUND)]
        ot = [S.sb(f"ot{i}", [P, BLK]) for i in range(ROUND)]
        probs = [S.sb(f"probs{i}", [P, T]) for i in range(2)]
        run_max = S.sb("run_max", [P, NT, NB])
        neg_max = S.sb("neg_max", [P, NT])
        left, warm = S.sb("left", [P, NT]), S.sb("warm", [P, 1])
        max_parts = S.sb("max_parts", [P, P // NT, NT], BF16)
        max_rows = S.sb("max_rows", [PARTS * NT, P], BF16)
        pS = S.ps("pS", [P, 2, 2 * BLK])
        pM = S.ps("pM", [P, FILLED, BLK])
        pO = S.ps("pO", [P, BLK])
        preset, scored, exped, filled, taken, splitting, split, rows_in, v_in, used, ot_kept, zeroed = (
            S.sem(n) for n in ("preset", "scored", "exped", "filled", "taken", "splitting", "split", "rows_in", "v_in",
                               "used", "ot_kept", "zeroed"))
        v_preset = S.sem("v_preset")
        ones_set = [S.sem(f"ones_set{i}") for i in range(ROUND)]
        stacked = [S.sem(f"stacked{i}") for i in range(ROUND)]
        ot_stored = [S.sem(f"ot_stored{i}") for i in range(ROUND)]
        block = S.block()
        LOADS = 6

        def every_head(engine, one_head, start=0):
            for h in range(start):
                one_head(h // ROUND, h % ROUND)
            with engine.Fori(start // ROUND, LOOPED // ROUND) as p:
                for c in range(ROUND):
                    one_head(p, c)
            for h in range(LOOPED, HEADS):
                one_head(h // ROUND, h % ROUND)

        def exists(p, c):
            return not isinstance(p, int) or ROUND * p + c < HEADS

        @block.sync
        def _(sp):
            def load_stacks(p, c):
                h = ROUND * p + c
                for r in range(PARTS):
                    rows = slice(r * PARTS * HD, (r + 1) * PARTS * HD)
                    sp.dma_start(qs[c % ROUND][rows, :], K.parts[0][h].rearrange("a d t -> (a d) t"))\
                      .then_inc(stacked[c % ROUND], 16)
                    sp.dma_start(ks[c % ROUND][rows, :], K.parts[1][h, r].unsqueeze(0).broadcast_to([PARTS, HD, T]))\
                      .then_inc(stacked[c % ROUND], 16)

            def load_max_rows(p, c):
                g = ROUND * p + c
                last = not exists(p, c + 1)
                sp.wait_ge(taken, ITEMS * (g + 1) + (0 if last else TURN_AT))
                for a in range(PARTS):
                    sp.dma_start(qs[c % ROUND][STK + a:STK + a + 1, :].rearrange("o (t c) -> o t c", c=P),
                                 max_rows[a * NT:(a + 1) * NT, :]).then_inc(rows_in, 16)

            def one_head(p, c):
                if exists(p, c + 2):
                    sp.wait_ge(scored, NC * (ROUND * p + c) + 1)
                    load_stacks(p, c + 2)
                if exists(p, c + 1):
                    load_max_rows(p, c + 1)

            for c in range(2):
                sp.wait_ge(ones_set[c], 1)
                load_stacks(0, c)
            load_max_rows(0, 0)
            sp.wait_ge(ones_set[2], 1)
            every_head(sp, one_head)

        @block.gpsimd
        def _(pool):
            def take_v(p, c):
                h = ROUND * p + c
                if not isinstance(h, int) or h >= ROUND:
                    pool.wait_ge(ot_stored[c % ROUND], 16 * NB * (p + c // ROUND))
                pool.tensor_copy(vh[c % ROUND][:, :, 0:HD], K.v[:, :, bass.ds(h * HD, HD)]).then_inc(v_in, 1)

            def one_head(p, c):
                h = ROUND * p + c
                if exists(p, c + 1):
                    pool.wait_ge(used, NT * h + 2)
                    take_v(p, c + 1)
                pool.wait_ge(ot_kept, h + 2)
                for b in range(NB):
                    pool.dma_start(K.head_out[h, :, b * BLK:(b + 1) * BLK], ot[c][b * 32:b * 32 + HD + 1, :])\
                        .then_inc(ot_stored[c], 16)

            for i in range(1, ROUND):
                pool.memset(ks[i][64:96, :], 1.0).then_inc(ones_set[i], 1)
                pool.wait_ge(ones_set[i], 1)
            for i in range(ROUND):
                pool.memset(vh[i][:, :, HD:VW], 0.0).then_inc(zeroed, 1)
            pool.wait_ge(zeroed, ROUND)
            for i in range(ROUND):
                pool.memset(vh[i][:, :, HD:HD + 1], 1.0).then_inc(v_preset, 1)
            pool.wait_ge(v_preset, ROUND)
            take_v(0, 0)
            if scatter:
                scatter.start(pool)
            every_head(pool, one_head, start=ROUND)
            if scatter:
                scatter.finish(pool)
            for c in range(ROUND):
                pool.wait_ge(ot_stored[c], 16 * NB * len(range(c, HEADS, ROUND)))

        @block.tensor
        def _(pe):
            def fill(p, c, j, run):
                g, n = ROUND * p + c, ITEMS * (ROUND * p + c) + j - 1
                slot = (ITEMS * c + j - 1) % FILLED
                if not isinstance(n, int) or n >= FILLED:
                    pe.wait_ge(taken, n - FILLED + 1)
                if run is None:
                    pe.wait_ge(split, g)
                    pe.transpose(pM[:, slot, :].bitcast(BF16)[:, 0:P],
                                 max_parts[:, :, :].rearrange("p a t -> p (a t)"), K.ident_b[:, :]).then_inc(filled, 1)
                else:
                    i, b, w, masked = runs[run]
                    if run == 0:
                        pe.wait_ge(stacked[c % ROUND], 16 * LOADS * (p + c // ROUND + 1))
                    mm = pe.matmul(pM[:, slot, 0:w], qs[c % ROUND][0:STK, i * P:(i + 1) * P],
                                   ks[c % ROUND][0:STK, b * BLK:b * BLK + w], start=True, stop=not masked)
                    if masked:
                        mm = pe.matmul(pM[:, slot, w - P:w], K.ident_b[:, :], K.neg_above[:, :], start=False, stop=True)
                    mm.then_inc(filled, 1)

            def score_chunk(p, c, n):
                h = ROUND * p + c
                u, _, cols = chunks[n]
                if n == 0:
                    pe.wait_ge(rows_in, 16 * PARTS * (h + 1))
                if not isinstance(h, int) or h > 0 or n >= 2:
                    pe.wait_ge(exped, NC * h + n - 1)
                for b, c0, c1 in cols:
                    o = c0 % (2 * BLK)
                    diag = causal and c0 == u * P
                    mm = pe.matmul(pS[:, (NC * c + n) % 2, o:o + c1 - c0],
                                   ks[c % ROUND][0:STK + PARTS, u * P:(u + 1) * P],
                                   qs[c % ROUND][0:STK + PARTS, c0:c1], start=True, stop=not diag)
                    if diag:
                        mm = pe.matmul(pS[:, (NC * c + n) % 2, o:o + P], K.ident_b[:, :], K.neg_below[:, :],
                                       start=False, stop=True)
                mm.then_inc(scored, 1)

            def sum_unit(p, c, u):
                h = ROUND * p + c
                if u == 0:
                    pe.wait_ge(v_in, h + 1)
                    pe.wait_ge(ot_kept, h + 1)
                pe.wait_ge(exped, NC * h + first_chunk[u + 1])
                for _, cols in units[u]:
                    for b, c0, c1 in cols:
                        mm = pe.matmul(pO[b * 32:b * 32 + VW, c0 - b * BLK:c1 - b * BLK], vh[c][:, u, :],
                                       probs[u % 2][:, c0:c1], start=(u == 0),
                                       stop=(u == (4 * b + 3 if causal else NT - 1)))
                mm.then_inc(used, 1)

            def one_head(p, c):
                for u in range(NT):
                    todo = [(c + d, j, items[j]) for d, j in ahead(u) if exists(p, c + d)]
                    if not exists(p, c + 2):
                        todo += [(c + d, 0, None) for d, j in ahead(u)
                                 if not exists(p, c + d) and exists(p, c + d - 1) and j == TURN_AT]
                    if u < NT - 1:
                        scores = [(c, n) for n in range(first_chunk[u + 1], first_chunk[u + 2])]
                    else:
                        scores = [(c + 1, n) for n in range(first_chunk[1])] if exists(p, c + 1) else []
                    places = len(scores) + 2
                    for k in range(places):
                        for item in todo[len(todo) * k // places:len(todo) * (k + 1) // places]:
                            fill(p, *item)
                        if k < len(scores):
                            score_chunk(p, *scores[k])
                        elif k == len(scores):
                            sum_unit(p, c, u)

            pe.wait_ge(preset, 1)
            for j in range(1, ITEMS):
                fill(0, 0, j, first_items[j])
            for j, run in enumerate(items[:LEAD]):
                fill(0, 1, j, run)
            for n in range(first_chunk[1]):
                score_chunk(0, 0, n)
            every_head(pe, one_head)

        @block.scalar
        def _(act):
            def one_head(p, c):
                h = ROUND * p + c
                for n, (u, _, cols) in enumerate(chunks):
                    act.wait_ge(scored, NC * h + n + 1)
                    act.wait_ge(used, NT * h + u + 1)
                    c0, c1 = cols[0][1], cols[-1][2]
                    o = c0 % (2 * BLK)
                    act.activation(probs[u % 2][:, c0:c1], pS[:, (NC * c + n) % 2, o:o + c1 - c0], ACT.Exp)\
                       .then_inc(exped, 1)

            act.activation(warm[:, :], K.x[:, 0, 0:1], ACT.Exp)
            every_head(act, one_head)

        @block.vector
        def _(dve):
            def take(p, c, j, run):
                g, n = ROUND * p + c, ITEMS * (ROUND * p + c) + j - 1
                slot = (ITEMS * c + j - 1) % FILLED
                dve.wait_ge(filled, n + 1)
                if run is not None:
                    i, b, w, _ = runs[run]
                    dve.reduce_max(run_max[:, i, b:b + 1], pM[:, slot, 0:w], AX.X).then_inc(taken, 1)
                else:
                    if not isinstance(g, int) or g > 1:
                        dve.wait_ge(rows_in, 16 * PARTS * (g - 1))
                    dve.tensor_copy(max_rows[:, :], pM[:, slot, :].bitcast(BF16)[0:PARTS * NT, 0:P]).then_inc(taken, 1)
                if j < ITEMS - 1 or not exists(p, c):
                    return
                dve.wait_ge(taken, ITEMS * (g + 1) - 1)
                dve.tensor_reduce(neg_max[:, :], run_max[:, :, :], AX.X, ALU.max, negate=True).then_inc(splitting, 1)
                dve.wait_ge(splitting, 4 * g + 1)
                dve.tensor_copy(max_parts[:, 0, :], neg_max[:, :]).then_inc(splitting, 1)
                dve.wait_ge(splitting, 4 * g + 2)
                dve.tensor_tensor(left[:, :], neg_max[:, :], max_parts[:, 0, :], ALU.subtract).then_inc(splitting, 1)
                dve.wait_ge(splitting, 4 * g + 3)
                dve.tensor_copy(max_parts[:, 1, :], left[:, :]).then_inc(splitting, 1)
                dve.wait_ge(splitting, 4 * g + 4)
                dve.tensor_tensor(max_parts[:, 2, :], left[:, :], max_parts[:, 1, :], ALU.subtract).then_inc(split, 1)

            def one_head(p, c):
                h = ROUND * p + c
                for u in range(NT):
                    for d, j in ahead(u):
                        if exists(p, c + d):
                            take(p, c + d, j, items[j])
                        elif exists(p, c + d - 1) and j == TURN_AT:
                            take(p, c + d, 0, None)
                dve.wait_ge(used, NT * (h + 1) + 2)
                dve.tensor_copy(ot[c][:, :], pO[:, :]).then_inc(ot_kept, 1)

            dve.memset(ks[0][64:96, :], 1.0).then_inc(ones_set[0], 1)
            dve.memset(max_parts[:, PARTS:, :], 0.0)
            dve.memset(run_max[:, :, :], LOWEST).then_inc(preset, 1)
            dve.engine_nop().then_inc(used, 2)
            dve.engine_nop().then_inc(ot_kept, 1)
            for j in range(1, ITEMS):
                take(0, 0, j, first_items[j])
            for j, run in enumerate(items[:LEAD]):
                take(0, 1, j, run)
            every_head(dve, one_head)


def finish_layer0(nc, K):
    with Stage(nc, "finish0") as S:
        sums, den = S.sb("sums", [P, T]), S.sb("den", [P, T])
        h1, h2 = S.sb("h1", [P, T]), S.sb("h2", [P, T])
        biased = S.sb("biased", [P, NB, TPB, D])
        pH, pR = S.ps("pH", [P, NB, BLK]), S.ps("pR", [P, NB, BLK])
        (loaded, inverted, scaled, ffn, ffn_kept, rows, b_kept, tanhed, gated, order) = (S.sem(n) for n in (
            "loaded", "inverted", "scaled", "ffn", "ffn_kept", "rows", "b_kept", "tanhed", "gated", "order"))
        block = S.block()
        tiles = [slice(c * TPB, (c + 1) * TPB) for c in range(NB)]

        @block.sync
        def _(sp):
            sp.dma_start(den[:, :], K.head_out[:, HD:HD + 1, :].broadcast_to([HEADS, HD, T])).then_inc(loaded, 16)
            sp.wait_ge(loaded, 16)
            sp.dma_start(sums[:, :], K.head_out[:, 0:HD, :]).then_inc(loaded, 16)
            sp.wait_ge(loaded, 32)

        @block.vector
        def _(dve):
            chain = Chain(dve, order)

            def row_of(name):
                return K.row[name][:, :].unsqueeze(1).broadcast_to([P, TPB, D])

            def rows_in(c):
                return pR[:, c, :].rearrange("p (t d) -> p t d", d=D)

            dve.wait_ge(loaded, 16)
            for c in range(NB):
                cols = slice(c * BLK, (c + 1) * BLK)
                dve.reciprocal(den[:, cols], den[:, cols]).then_inc(inverted, 1)
            for c in range(NB):
                dve.wait_ge(rows, c + 1)
                dve.tensor_tensor(biased[:, c], rows_in(c), row_of("L0_ffn_bias"), ALU.add).then_inc(b_kept, 1)
            for c in range(NB):
                cols = slice(c * BLK, (c + 1) * BLK)
                dve.wait_ge(inverted, c + 1)
                dve.wait_ge(loaded, 32)
                dve.tensor_tensor(sums[:, cols], sums[:, cols], den[:, cols], ALU.mult).then_inc(scaled, 1)
            for c in range(NB):
                dve.wait_ge(rows, NB + c + 1)
                chain(dve.tensor_tensor(K.s[:, tiles[c], :], rows_in(c), row_of("L0_attn_bo"), ALU.add))
                dve.wait_ge(gated, c + 1)
                chain(dve.tensor_tensor(K.g[:, tiles[c], :], K.g[:, tiles[c], :], K.s[:, tiles[c], :], ALU.mult))
                chain(dve.tensor_tensor(K.x[:, tiles[c], :], K.x[:, tiles[c], :], K.g[:, tiles[c], :], ALU.add))
                for t in range(c * TPB, (c + 1) * TPB):
                    dve.bn_stats(K.stats[:, t, :], K.x[:, t, :])

        @block.scalar
        def _(act):
            for n in range(2 * NB):
                b = n % NB
                act.wait_ge(ffn, n + 1)
                act.activation((h1, h2)[n // NB][:, b * BLK:(b + 1) * BLK], pH[:, b, :], ACT.Copy)\
                   .then_inc(ffn_kept, 1)
            for c in range(NB):
                act.wait_ge(b_kept, c + 1)
                act.activation(biased[:, c], biased[:, c], ACT.Tanh).then_inc(tanhed, 1)
            for c in range(NB):
                act.wait_ge(tanhed, c + 1)
                act.activation(K.g[:, tiles[c], :], biased[:, c], ACT.Silu).then_inc(gated, 1)

        @block.tensor
        def _(pe):
            def to_rows(c, feature_major, w):
                for t in range(TPB):
                    tok = slice(c * BLK + t * P, c * BLK + (t + 1) * P)
                    mm = pe.matmul(pR[:, c, t * P:(t + 1) * P], feature_major[:, tok], w, start=True, stop=True)
                mm.then_inc(rows, 1)

            for n in range(2 * NB):
                b = n % NB
                if n >= NB:
                    pe.wait_ge(ffn_kept, n - NB + 1)
                w = K.w[("L0_ffn_weight", "L0_ffn_aux_weight1")[n // NB]]
                pe.matmul(pH[:, b, :], w[:, :], (K.xnT, h1)[n // NB][:, b * BLK:(b + 1) * BLK],
                          start=True, stop=True).then_inc(ffn, 1)
            for c in range(NB):
                pe.wait_ge(ffn_kept, NB + c + 1)
                to_rows(c, h2, K.w["L0_ffn_aux_weight2"])
            for c in range(NB):
                pe.wait_ge(scaled, c + 1)
                pe.wait_ge(b_kept, c + 1)
                to_rows(c, sums, K.w["L0_attn_Wo"])


L1_E, L1_I, L1_TOP = 32, 64, 6
L1_J = L1_E * L1_I // P


class Top6Routing:

    def __init__(self, nc, K, A, S):
        E = L1_E
        self.K, self.A = K, A
        self.shifted, self.gates, self.score, self.mask, self.hit = (
            S.sb(n, [P, NT, E]) for n in ("shifted", "gates", "score", "mask", "hit"))
        self.mx, self.total = S.sb("mx", [P, NT]), S.sb("total", [P, NT])
        self.top, self.place = S.sb("top", [P, NT, 8]), S.sb("place", [P, NT, 8])
        self.place_u = S.sb("place_u", [P, NT, 8], mybir.dt.uint32)
        self.parts = S.sb("parts", [P, NT, PARTS, E], BF16)
        self.sel_f = S.sb("sel_f", [PARTS * E, L1_J * P])
        (self.sel_in, self.sel_made, self.routed, self.exp_ready, self.exped, self.order, self.split, self.turned,
         self.comb_kept) = (S.sem(f"route_{n}") for n in (
             "sel_in", "sel_made", "routed", "exp_ready", "exped", "order", "split", "turned", "comb_kept"))

    def load_selection(self, sp):
        sp.dma_start(self.sel_f[:, :], self.A["c_sel1"]).then_inc(self.sel_in, 16)

    def make_selection(self, act):
        act.wait_ge(self.sel_in, 16)
        act.activation(self.K.sel[:, :], self.sel_f[:, :], ACT.Copy).then_inc(self.sel_made, 1)

    def pe_logits(self, pe, bank):
        for t in range(NT):
            mm = pe.matmul(bank[:, t * L1_E:(t + 1) * L1_E], self.K.xnT[:, t * P:(t + 1) * P], self.K.wr1,
                           start=True, stop=True)
        mm.then_inc(self.routed, 1)

    def pe_turn(self, pe, banks):
        pe.wait_ge(self.split, 1)
        for t in range(NT):
            mm = pe.transpose(banks[t // 8].bitcast(BF16)[0:PARTS * L1_E, t % 8 * P:(t % 8 + 1) * P],
                              self.parts[:, t, :, :].rearrange("p a e -> p (a e)"), self.K.ident_b[:, :])
            if t % 8 == 7:
                mm.then_inc(self.turned, 1)

    def act_exp(self, act):
        act.wait_ge(self.exp_ready, 1)
        act.activation(self.gates[:, :, :], self.shifted[:, :, :], ACT.Exp).then_inc(self.exped, 1)

    def dve_keep(self, dve, banks):
        for c in range(2):
            dve.wait_ge(self.turned, c + 1)
            dve.tensor_copy(self.K.combT[:, c * 8 * P:(c + 1) * 8 * P], banks[c].bitcast(BF16)[0:PARTS * L1_E, :])\
               .then_inc(self.comb_kept, 1)

    def dve_step(self, dve, i, bank):
        K, E = self.K, L1_E
        shape = [P, NT, E]
        gates, total, mask, hit, parts = self.gates[:, :, :], self.total[:, :], self.mask[:, :, :], self.hit[:, :, :], \
            self.parts
        if i == 0:
            self.chain = Chain(dve, self.order)
            chain = self.chain
            logits = bank.rearrange("p (t e) -> p t e", e=E)
            dve.wait_ge(self.routed, 1)
            chain(dve.reduce_max(self.mx[:, :], logits, AX.X))
            dve.tensor_tensor(self.shifted[:, :, :], logits, self.mx[:, :].unsqueeze(2).broadcast_to(shape),
                              ALU.subtract).then_inc(self.exp_ready, 1)
        chain = self.chain
        if i == 1:
            dve.wait_ge(self.exped, 1)
            chain(dve.reduce_sum(total, gates, AX.X))
            chain(dve.reciprocal(total, total))
            chain(dve.tensor_tensor(gates, gates, total.unsqueeze(2).broadcast_to(shape), ALU.mult))
            chain(dve.tensor_tensor(self.score[:, :, :], gates,
                                    K.row["L1_ffn_e_score_bias"][:, :].unsqueeze(1).broadcast_to(shape), ALU.add))
        if i == 2:
            for t in range(NT):
                last = dve.max(self.top[:, t, :], self.score[:, t, :])
            chain(last)
        if i == 3:
            for t in range(NT):
                last = dve.max_index(self.place_u[:, t, :], self.top[:, t, :], self.score[:, t, :])
            chain(last)
            chain(dve.tensor_copy(self.place[:, :, :], self.place_u[:, :, :]))
        if 4 <= i < 4 + L1_TOP:
            k = i - 4
            iota = K.iota[:, 0:E].unsqueeze(1).broadcast_to(shape)
            chain(dve.tensor_tensor(hit if k else mask, iota, self.place[:, :, k:k + 1].broadcast_to(shape),
                                    ALU.is_equal))
            if k:
                chain(dve.tensor_tensor(mask, mask, hit, ALU.add))
        if i == 10:
            chain(dve.tensor_tensor(gates, gates, mask, ALU.mult))
            chain(dve.reduce_sum(total, gates, AX.X))
        if i == 11:
            chain(dve.tensor_scalar(total, total, 1e-12, None, ALU.max))
            chain(dve.reciprocal(total, total))
            chain(dve.tensor_tensor(gates, gates, total.unsqueeze(2).broadcast_to(shape), ALU.mult))
        if i == 12:
            chain(dve.tensor_copy(parts[:, :, 0, :], gates))
            chain(dve.tensor_tensor(hit, gates, parts[:, :, 0, :], ALU.subtract))
            chain(dve.tensor_copy(parts[:, :, 1, :], hit))
            dve.tensor_tensor(parts[:, :, 2, :], hit, parts[:, :, 1, :], ALU.subtract).then_inc(self.split, 1)


def attention_row_sums(nc, K, A, layer, wq, wk, wv, bq, bk, bv):
    scale = float(np.float32(1.0) / np.sqrt(np.float32(D)))
    with Stage(nc, f"rowsum{layer}") as S:
        qT, kT = S.sb("qT", [P, T]), S.sb("kT", [P, T])
        probs = S.sb("probs", [P, 2, T])
        row_max, neg, zero_neg = S.sb("row_max", [P, NT]), S.sb("neg", [P, NT]), S.sb("zero_neg", [P, NT])
        den, zero_p = K.row_den, K.row_zero
        pS = [S.ps(f"pS{n}", [P, T]) for n in range(2)]
        (projected, kept, vproj, vkept, scored, maxed, exped, order) = (
            S.sem(n) for n in ("projected", "kept", "vproj", "vkept", "scored", "maxed", "exped", "order"))
        routing = Top6Routing(nc, K, A, S)
        LOGITS = pS[0][:, (NB - 1) * BLK:]
        PARTS_T = [pS[0][:, c * BLK:(c + 1) * BLK] for c in range(2)]
        block = S.block()

        @block.sync
        def _(sp):
            routing.load_selection(sp)
            sp.wait_ge(routing.sel_in, 16)

        @block.tensor
        def _(pe):
            for n in range(2 * NB):
                w, b = divmod(n, NB)
                pe.matmul(pS[w][:, b * BLK:(b + 1) * BLK], (wq, wk)[w][:, :], K.xnT[:, b * BLK:(b + 1) * BLK],
                          start=True, stop=True).then_inc(projected, 1)
            pe.wait_ge(kept, NB)
            for t in range(NT):
                mm = pe.matmul(pS[0][:, t * P:(t + 1) * P], K.xnT[:, t * P:(t + 1) * P], wv[:, :],
                               start=True, stop=True)
                if t % TPB == TPB - 1:
                    mm.then_inc(vproj, 1)
            pe.wait_ge(kept, 2 * NB)
            pe.wait_ge(vkept, NB)
            routing.pe_logits(pe, LOGITS)
            for i in range(NT):
                if i >= 2:
                    pe.wait_ge(exped, i - 1)
                if i == (NB - 1) * TPB:
                    pe.wait_ge(routing.exp_ready, 1)
                hi = (i + 1) * P
                for b in range(-(-hi // BLK)):
                    c0, c1 = b * BLK, min((b + 1) * BLK, hi)
                    diag = c1 == hi
                    mm = pe.matmul(pS[i % 2][:, c0:c1], qT[:, i * P:(i + 1) * P], kT[:, c0:c1],
                                   start=True, stop=not diag)
                    if diag:
                        mm = pe.matmul(pS[i % 2][:, c1 - P:c1], K.ident_b[:, :], K.neg_above[:, :],
                                       start=False, stop=True)
                mm.then_inc(scored, 1)
            pe.wait_ge(exped, NT - 1)
            routing.pe_turn(pe, PARTS_T)

        @block.scalar
        def _(act):
            for n in range(2 * NB):
                w, b = divmod(n, NB)
                act.wait_ge(projected, n + 1)
                act.activation((qT, kT)[w][:, b * BLK:(b + 1) * BLK], pS[w][:, b * BLK:(b + 1) * BLK], ACT.Identity,
                               bias=(bq, bk)[w][:, :]).then_inc(kept, 1)
            for i in range(NT):
                if i == 1:
                    routing.act_exp(act)
                if i == NT // 2:
                    routing.make_selection(act)
                hi = (i + 1) * P
                act.wait_ge(maxed, i + 1)
                if i >= 2:
                    act.wait_ge(exped, i - 1)
                act.activation(probs[:, i % 2, 0:hi], pS[i % 2][:, 0:hi], ACT.Exp, bias=neg[:, i:i + 1], scale=scale,
                               accum_out=den[:, i:i + 1]).then_inc(exped, 1)
            act.activation(zero_p[:, :], zero_neg[:, :], ACT.Exp).then_inc(exped, 1)

        @block.vector
        def _(dve):
            chain = Chain(dve, order)
            for c in range(NB):
                dve.wait_ge(vproj, c + 1)
                dve.tensor_tensor(K.v[:, c * TPB:(c + 1) * TPB, :],
                                  pS[0][:, c * BLK:(c + 1) * BLK].rearrange("p (t d) -> p t d", d=D),
                                  bv[:, :].unsqueeze(1).broadcast_to([P, TPB, D]), ALU.add).then_inc(vkept, 1)
            for i in range(NT):
                col = slice(i, i + 1)
                dve.wait_ge(scored, i + 1)
                chain(dve.reduce_max(row_max[:, col], pS[i % 2][:, 0:(i + 1) * P], AX.X))
                chain(dve.tensor_tensor(row_max[:, col], row_max[:, col], K.floor[:, col], ALU.max))
                chain(dve.tensor_scalar(zero_neg[:, col], row_max[:, col], -scale, 0.0, ALU.mult, ALU.min))
                dve.tensor_scalar(neg[:, col], row_max[:, col], -scale, None, ALU.mult).then_inc(maxed, 1)
                routing.dve_step(dve, i, LOGITS)
            routing.dve_keep(dve, PARTS_T)


def finish_row_sums(dve, chain, K):
    den, zero_p, inv, weight = K.row_den[:, :], K.row_zero[:, :], K.row_inv[:, :], K.row_weight[:, :]
    chain(dve.tensor_tensor(zero_p, zero_p, K.after[:, :], ALU.mult))
    chain(dve.tensor_tensor(den, den, zero_p, ALU.add))
    chain(dve.reciprocal(inv, den))
    chain(dve.tensor_tensor(weight, den, inv, ALU.mult))
    chain(dve.tensor_tensor(K.s[:, :, :], K.v[:, :, :], weight.unsqueeze(2).broadcast_to([P, NT, D]), ALU.mult))


class SingleHeadAttention:

    def __init__(self, nc, K, S, wq, wk, wv, bq, bk, bv):
        self.nc, self.K = nc, K
        self.w_qk, self.wv, self.b_qk, self.bv = (wq, wk), wv, (bq, bk), bv
        self.scale = float(np.float32(1.0) / np.sqrt(np.float32(D)))
        self.qT, self.kT = S.sb("qT", [P, T]), S.sb("kT", [P, T])
        self.row_max, self.neg, self.den, self.inv = (S.sb(n, [P, NT]) for n in ("row_max", "neg", "den", "inv"))
        (self.projected, self.kept, self.vproj, self.vkept, self.scored, self.maxed, self.exped, self.turned,
         self.turn_kept, self.summed, self.order, self.finished) = (
            S.sem(n) for n in ("projected", "kept", "vproj", "vkept", "scored", "maxed", "exped", "turned",
                               "turn_kept", "summed", "order", "finished"))
        self.groups = [-(-(i + 1) // TPB) for i in range(NT)]
        self.before = [sum(self.groups[:i]) for i in range(NT + 1)]

    def room(self, S):
        self.probs = [S.sb(f"probs{n}", [P, T]) for n in range(2)]
        self.probsT = S.sb("probsT", [P, 2, NT, P])
        self.pS, self.pT, self.pO = S.ps("pS", [P, NB, BLK]), S.ps("pT", [P, 2, BLK]), S.ps("pO", [P, BLK])
        self.scores_row = self.pS[:, :, :].rearrange("p b c -> p (b c)")

    def pe_project_qk(self, pe, w):
        for b in range(NB):
            if w == 1:
                pe.wait_ge(self.kept, b + 1)
            pe.matmul(self.pS[:, b, :], self.w_qk[w], self.K.xnT[:, b * BLK:(b + 1) * BLK], start=True, stop=True)\
              .then_inc(self.projected, 1)

    def pe_project_v(self, pe):
        for t in range(NT):
            c = t // TPB
            if t % TPB == 0 and c >= 2:
                pe.wait_ge(self.vkept, c - 1)
            mm = pe.matmul(self.pT[:, c % 2, t % TPB * P:(t % TPB + 1) * P], self.K.xnT[:, t * P:(t + 1) * P], self.wv,
                           start=True, stop=True)
            if t % TPB == TPB - 1:
                mm.then_inc(self.vproj, 1)
        pe.wait_ge(self.kept, 2 * NB)
        pe.wait_ge(self.vkept, NB)

    def pe_step(self, pe, i, lo, hi):
        K = self.K

        def scores(i):
            if i >= 1:
                pe.wait_ge(self.exped, i)
            end = (i + 1) * P
            for b in range(-(-end // BLK)):
                w = min(BLK, end - b * BLK)
                diag = b == i // TPB
                mm = pe.matmul(self.pS[:, b, 0:w], self.qT[:, i * P:(i + 1) * P], self.kT[:, b * BLK:b * BLK + w],
                               start=True, stop=not diag)
                if diag:
                    mm = pe.matmul(self.pS[:, b, w - P:w], K.ident_b[:, :], K.neg_above[:, :], start=False, stop=True)
            mm.then_inc(self.scored, 1)

        def turn(i):
            pe.wait_ge(self.exped, i + 1)
            for c in range(self.groups[i]):
                n = self.before[i] + c
                if n >= 2:
                    pe.wait_ge(self.turn_kept, n - 1)
                for j in range(c * TPB, min(i + 1, (c + 1) * TPB)):
                    mm = pe.transpose(self.pT[:, n % 2, j % TPB * P:(j % TPB + 1) * P],
                                      self.probs[i % 2][:, j * P:(j + 1) * P], K.ident[:, :])
                mm.then_inc(self.turned, 1)

        def sums(i):
            if i >= 1:
                pe.wait_ge(self.finished, i)
            pe.wait_ge(self.turn_kept, self.before[i + 1])
            for j in range(i + 1):
                mm = pe.matmul(self.pO[:, 0:D], self.probsT[:, i % 2, j, :], K.v[:, j, :], start=(j == 0),
                               stop=(j == i))
            mm.then_inc(self.summed, 1)

        if i < hi:
            scores(i)
        if i > lo:
            turn(i - 1)
            sums(i - 1)

    def act_project(self, act):
        for n in range(2 * NB):
            w, b = divmod(n, NB)
            act.wait_ge(self.projected, n + 1)
            act.activation((self.qT, self.kT)[w][:, b * BLK:(b + 1) * BLK], self.pS[:, b, :], ACT.Identity,
                           bias=self.b_qk[w]).then_inc(self.kept, 1)

    def act_step(self, act, i, lo, hi):
        def keep_turned(i):
            for c in range(self.groups[i]):
                n = self.before[i] + c
                w = min(i + 1 - c * TPB, TPB) * P
                act.wait_ge(self.turned, n + 1)
                if i >= 2:
                    act.wait_ge(self.summed, i - 1)
                act.activation(self.probsT[:, i % 2, c * TPB:c * TPB + w // P, :],
                               self.pT[:, n % 2, 0:w].rearrange("p (j q) -> p j q", q=P), ACT.Copy)\
                   .then_inc(self.turn_kept, 1)

        if i < hi:
            act.wait_ge(self.maxed, i + 1)
            act.activation(self.probs[i % 2][:, 0:(i + 1) * P], self.scores_row[:, 0:(i + 1) * P], ACT.Exp,
                           bias=self.neg[:, i:i + 1], scale=self.scale, accum_out=self.den[:, i:i + 1])\
               .then_inc(self.exped, 1)
            keep_turned(i)

    def dve_project(self, dve):
        self.chain = Chain(dve, self.order)
        for c in range(NB):
            dve.wait_ge(self.vproj, c + 1)
            dve.tensor_tensor(self.K.v[:, c * TPB:(c + 1) * TPB, :],
                              self.pT[:, c % 2, :].rearrange("p (t d) -> p t d", d=D),
                              self.bv.unsqueeze(1).broadcast_to([P, TPB, D]), ALU.add).then_inc(self.vkept, 1)

    def dve_step(self, dve, i, lo, hi):
        def maximum(i):
            dve.wait_ge(self.scored, i + 1)
            self.chain(dve.reduce_max(self.row_max[:, i:i + 1], self.scores_row[:, 0:(i + 1) * P], AX.X))
            dve.tensor_scalar(self.neg[:, i:i + 1], self.row_max[:, i:i + 1], -self.scale, None, ALU.mult)\
               .then_inc(self.maxed, 1)

        def finish(i):
            dve.wait_ge(self.exped, i + 1)
            self.chain(dve.reciprocal(self.inv[:, i:i + 1], self.den[:, i:i + 1]))
            dve.wait_ge(self.summed, i + 1)
            dve.tensor_scalar(self.K.s[:, i, :], self.pO[:, 0:D], self.inv[:, i:i + 1], None, ALU.mult)\
               .then_inc(self.finished, 1)

        if i < hi:
            maximum(i)
        if i > lo:
            finish(i - 1)


def softmax_over(dve, act_done, chain, logits, n, mx, shifted, total, gates, exp_ready):
    chain(dve.reduce_max(mx, logits, AX.X))
    dve.tensor_tensor(shifted, logits, mx.unsqueeze(2).broadcast_to([P, NT, n]), ALU.subtract).then_inc(exp_ready, 1)
    dve.wait_ge(act_done, 1)
    chain(dve.reduce_sum(total, gates, AX.X))
    chain(dve.reciprocal(total, total))
    chain(dve.tensor_tensor(gates, gates, total.unsqueeze(2).broadcast_to([P, NT, n]), ALU.mult))


def ffn_top6(nc, K):
    with Stage(nc, "top6") as S:
        act_gate, hidden = S.sb("act_gate", [P, 2, BLK]), S.sb("hidden", [P, 2, BLK])
        yT = S.sb("yT", [P, BLK])
        pG, pU, pC = (S.ps(n, [P, 2, BLK]) for n in ("pG", "pU", "pC"))
        pY, pR = S.ps("pY", [P, BLK]), S.ps("pR", [P, BLK])
        order, opened, gated, mixed, downed, y_kept, y_turned, g_kept, mixing, summing = (S.sem(n) for n in (
            "order", "opened", "gated", "mixed", "downed", "y_kept", "y_turned", "g_kept", "mixing", "summing"))
        block = S.block()
        STEPS = L1_J + 1
        x_blocks, s_blocks, g_blocks = (a[:, :, :].rearrange("p (b t) d -> p b t d", t=TPB) for a in (K.x, K.s, K.g))
        stats_blocks = K.stats[:, :, :].rearrange("p (b t) k -> p b t k", t=TPB)

        @block.sync
        def _(sp):
            sp.wait_ge(K.cleared, K.clears)

        @block.tensor
        def _(pe):
            pe.wait_ge(K.l1_loaded, L1_LOADS)

            def open_step(b, n):
                if n >= 2:
                    pe.wait_ge(mixed, STEPS * b + n - 1)
                x = K.xnT[:, bass.ts(b, BLK)]
                gw, uw = (K.gate1[:, n * P:(n + 1) * P], K.up1[:, n * P:(n + 1) * P]) if n < L1_J else \
                    (K.sgate1[:, :], K.sup1[:, :])
                pe.matmul(pG[:, n % 2, :], gw, x, start=True, stop=True)
                mm = pe.matmul(pU[:, n % 2, :], uw, x, start=True, stop=True)
                if n < L1_J:
                    mm = pe.matmul(pC[:, n % 2, :], K.sel[:, n * P:(n + 1) * P], K.combT[:, bass.ts(b, BLK)],
                                   start=True, stop=True)
                mm.then_inc(opened, 1)

            def close_step(b, n):
                pe.wait_ge(mixed, STEPS * b + n + 1)
                w = K.down1[:, n, :] if n < L1_J else K.sdown1[:, :]
                pe.matmul(pY[:, :], w, hidden[:, n % 2, :], start=(n == 0), stop=(n == L1_J)).then_inc(downed, 1)

            with pe.Fori(0, NB) as b:
                for n in range(STEPS):
                    open_step(b, n)
                    if n >= 1:
                        close_step(b, n - 1)
                close_step(b, STEPS - 1)
                pe.wait_ge(y_kept, b + 1)
                for t in range(TPB):
                    mm = pe.transpose(pR[:, t * P:(t + 1) * P], yT[:, t * P:(t + 1) * P], K.ident[:, :])
                mm.then_inc(y_turned, 1)

        @block.scalar
        def _(act):
            with act.Fori(0, NB) as b:
                for n in range(STEPS):
                    act.wait_ge(opened, STEPS * b + n + 1)
                    if n >= 2:
                        act.wait_ge(mixed, STEPS * b + n - 1)
                    act.activation(act_gate[:, n % 2, :], pG[:, n % 2, :], ACT.Silu).then_inc(gated, 1)
                act.wait_ge(y_turned, b + 1)
                act.activation(g_blocks[:, b, :, :], pR[:, :].rearrange("p (t d) -> p t d", d=D), ACT.Silu)\
                   .then_inc(g_kept, 1)

        @block.vector
        def _(dve):
            chain = Chain(dve, order)
            finish_row_sums(dve, chain, K)

            def add_residual(b):
                dve.wait_ge(g_kept, b + 1)
                dve.tensor_tensor(g_blocks[:, b, :, :], g_blocks[:, b, :, :], s_blocks[:, b, :, :], ALU.mult)\
                   .then_inc(summing, 1)
                dve.wait_ge(summing, 2 * b + 1)
                dve.tensor_tensor(x_blocks[:, b, :, :], x_blocks[:, b, :, :], g_blocks[:, b, :, :], ALU.add)\
                   .then_inc(summing, 1)
                dve.wait_ge(summing, 2 * b + 2)
                for t in range(TPB):
                    dve.bn_stats(stats_blocks[:, b, t, :], x_blocks[:, b, t, :])

            def body(b, before):
                for n in range(STEPS):
                    dve.wait_ge(gated, STEPS * b + n + 1)
                    if n >= 2:
                        dve.wait_ge(downed, STEPS * b + n - 1)
                    mix = dve.tensor_tensor(hidden[:, n % 2, :], act_gate[:, n % 2, :], pU[:, n % 2, :], ALU.mult)
                    if n < L1_J:
                        mix.then_inc(mixing, 1)
                        dve.wait_ge(mixing, L1_J * b + n + 1)
                        mix = dve.tensor_tensor(hidden[:, n % 2, :], hidden[:, n % 2, :], pC[:, n % 2, :], ALU.mult)
                    mix.then_inc(mixed, 1)
                    if n == STEPS // 2:
                        for k in before:
                            add_residual(k)
                dve.wait_ge(downed, STEPS * (b + 1))
                dve.tensor_copy(yT[:, :], pY[:, :]).then_inc(y_kept, 1)

            body(0, [])
            with dve.Fori(1, NB) as b:
                body(b, [b - 1])
            add_residual(NB - 1)


L2_E, L2_H, L2_GROUPS = 24, 512, 4
L2_CAP = -(-2 * (T // L2_GROUPS) // L2_E)
L2_HALF = L2_CAP * L2_GROUPS // 2
L2_SLOTS = L2_E * 2 * L2_HALF
L2_LN_EPS = 1e-6
LOOP_EXPERTS = 4
LOOP_HALVES = 2 * LOOP_EXPERTS
LOOPS = L2_E // LOOP_EXPERTS


def route_top2(nc, K, A, attention, tiles, loads):
    lo, hi = tiles
    E, SH = L2_E, [P, NT, L2_E]
    with Stage(nc, "route2") as S:
        raw, shifted, gates = S.sb("raw", SH), S.sb("shifted", SH), S.sb("gates", SH)
        hit, cand, prod = S.sb("hit", SH), S.sb("cand", SH), S.sb("prod", SH)
        chosen, kept = [S.sb(f"chosen{c}", SH) for c in range(2)], [S.sb(f"kept{c}", SH) for c in range(2)]
        ones_of = [S.sb(f"ones_of{c}", SH, BF16) for c in range(2)]
        base, spare = S.sb("base", SH), S.sb("spare", [P, 2, NT])
        mx, total, idx = S.sb("mx", [P, NT]), S.sb("total", [P, NT]), S.sb("idx", [P, NT])
        weight, slot, held = S.sb("weight", [P, 2, NT]), S.sb("slot", [P, 2, NT]), S.sb("held", [P, 2, NT])
        place = S.sb("place", [P, 2, NT])
        attention.room(S)
        consts_in, routed, exp_ready, exped, order, picked, located, placed, combined, scattered = (
            S.sem(n) for n in ("consts_in", "routed", "exp_ready", "exped", "order", "picked", "located", "placed",
                               "combined", "scattered"))
        block = S.block()
        pL, pA = S.ps("pL", [P, BLK]), attention.pO
        pB = pL
        logits, loc = pL[:, 0:NT * E].rearrange("p (t e) -> p t e", e=E), [
            bank[:, 0:NT * E].rearrange("p (t e) -> p t e", e=E) for bank in (pA, pB)]

        @block.sync
        def _(sp):
            sp.dma_start(base[:, :, :], A["c_base2"]).then_inc(consts_in, 16)
            sp.dma_start(spare[:, :, :], A["c_spare2"]).then_inc(consts_in, 16)
            sp.wait_ge(consts_in, 32)
            for dst, src, sem in loads:
                sp.dma_start(dst, src).then_inc(sem, 16)

        @block.tensor
        def _(pe):
            for t in range(NT):
                mm = pe.matmul(pL[:, t * E:(t + 1) * E], K.xnT[:, t * P:(t + 1) * P], K.wg2[:, :],
                               start=True, stop=True)
            mm.then_inc(routed, 1)
            tiles = NT // L2_GROUPS
            for c in range(2):
                attention.pe_project_qk(pe, c)
                pe.wait_ge(picked, c + 1)
                for t in range(NT):
                    g0 = t // tiles * tiles
                    adds = [(ones_of[c], j) for j in range(g0, t)]
                    if c == 1:
                        adds += [(ones_of[0], j) for j in range(g0, g0 + tiles)]
                    out = (pA, pB)[c][:, t * E:(t + 1) * E]
                    mm = pe.matmul(out, K.above_b[:, :], ones_of[c][:, t, :], start=True, stop=not adds)
                    for n, (o, j) in enumerate(adds):
                        mm = pe.matmul(out, K.ones_b[:, :], o[:, j, :], start=False, stop=n == len(adds) - 1)
                mm.then_inc(located, 1)
            attention.pe_project_v(pe)
            pe.wait_ge(combined, 2)
            for i in range(lo, hi + 1):
                attention.pe_step(pe, i, lo, hi)

        @block.scalar
        def _(act):
            act.wait_ge(exp_ready, 1)
            act.activation(gates[:, :, :], shifted[:, :, :], ACT.Exp).then_inc(exped, 1)
            attention.act_project(act)
            for i in range(lo, hi + 1):
                attention.act_step(act, i, lo, hi)

        @block.vector
        def _(dve):
            chain = Chain(dve, order)
            iota = K.iota[:, 0:E].unsqueeze(1).broadcast_to(SH)

            def over_e(x):
                return x.unsqueeze(2).broadcast_to(SH)

            def choose(values, c):
                chain(dve.reduce_max(mx[:, :], values[:, :, :], AX.X))
                chain(dve.tensor_tensor(hit[:, :, :], values[:, :, :], over_e(mx[:, :]), ALU.is_lt))
                chain(dve.scalar_tensor_tensor(cand[:, :, :], hit[:, :, :], float(4 * E), iota, ALU.mult, ALU.add))
                chain(dve.tensor_reduce(idx[:, :], cand[:, :, :], AX.X, ALU.min))
                chain(dve.tensor_tensor(chosen[c][:, :, :], iota, over_e(idx[:, :]), ALU.is_equal))
                dve.tensor_copy(ones_of[c][:, :, :], chosen[c][:, :, :]).then_inc(picked, 1)

            dve.wait_ge(routed, 1)
            chain(dve.tensor_copy(raw[:, :, :], logits))
            softmax_over(dve, exped, chain, raw[:, :, :], E, mx[:, :], shifted[:, :, :], total[:, :],
                         gates[:, :, :], exp_ready)
            choose(gates, 0)
            chain(dve.scalar_tensor_tensor(raw[:, :, :], chosen[0][:, :, :], LOWEST, raw[:, :, :], ALU.mult, ALU.add))
            choose(raw, 1)
            dve.wait_ge(consts_in, 32)
            for c in range(2):
                dve.wait_ge(located, c + 1)
                chain(dve.scalar_tensor_tensor(kept[c][:, :, :], loc[c], float(L2_CAP), chosen[c][:, :, :],
                                               ALU.is_lt, ALU.mult))
                chain(dve.tensor_tensor(prod[:, :, :], gates[:, :, :], kept[c][:, :, :], ALU.mult))
                chain(dve.reduce_sum(weight[:, c, :], prod[:, :, :], AX.X))
                chain(dve.tensor_tensor(prod[:, :, :], loc[c], base[:, :, :], ALU.add))
                chain(dve.tensor_tensor(prod[:, :, :], prod[:, :, :], kept[c][:, :, :], ALU.mult))
                chain(dve.reduce_sum(slot[:, c, :], prod[:, :, :], AX.X))
                chain(dve.reduce_sum(held[:, c, :], kept[c][:, :, :], AX.X))
            chain(dve.tensor_tensor(place[:, :, :], held[:, :, :], spare[:, :, :], ALU.mult))
            chain(dve.tensor_tensor(place[:, :, :], spare[:, :, :], place[:, :, :], ALU.subtract))
            chain(dve.tensor_tensor(place[:, :, :], place[:, :, :], slot[:, :, :], ALU.add))
            dve.tensor_copy(K.place_i[:, :, :], place[:, :, :]).then_inc(placed, 1)
            chain(dve.tensor_copy(K.slot_i[:, :, :], slot[:, :, :]))
            chain(dve.tensor_tensor(total[:, :], weight[:, 0, :], weight[:, 1, :], ALU.add))
            chain(dve.tensor_scalar(total[:, :], total[:, :], 1e-9, None, ALU.max))
            chain(dve.reciprocal(total[:, :], total[:, :]))
            for c in range(2):
                dve.tensor_tensor(K.coef[:, c, :], weight[:, c, :], total[:, :], ALU.mult).then_inc(combined, 1)
            attention.dve_project(dve)
            for i in range(lo, hi + 1):
                attention.dve_step(dve, i, lo, hi)

        @block.gpsimd
        def _(pool):
            pool.wait_ge(K.cleared, K.clears)
            pool.wait_ge(placed, 1)
            for c in range(2):
                for t in range(NT):
                    pool.indirect_dma_start(
                        out=K.x_slots, out_offset=bass.IndirectOffsetOnAxis(ap=K.place_i[:, c, t:t + 1], axis=0),
                        in_=K.xn[:, t, :], in_offset=None).then_inc(scattered, 16)
            pool.wait_ge(scattered, 16 * 2 * NT)


def expert_pass(nc, K, tag, src, weights, bias, width_in, width_out, dst, resident=None):
    F = width_in // P
    R = L2_HALF
    with Stage(nc, tag) as S:
        rows = [S.sb(f"rows{j}", [R, 2, width_in]) for j in range(LOOP_EXPERTS)]
        rowsT = [S.sb(f"rowsT{n}", [P, F, R]) for n in range(2)]
        w = None if resident else [S.sb(f"w{j}", [P, F, width_out]) for j in range(LOOP_EXPERTS)]
        bias_rows = [S.sb(f"bias{j}", [R, width_out]) for j in range(LOOP_EXPERTS)]
        outs = [S.sb(f"outs{j}", [R, 2, width_out]) for j in range(LOOP_EXPERTS)]
        pT, pY = S.ps("pT", [P, 2, BLK]), S.ps("pY", [P, 2, BLK])
        turned, turn_kept, multiplied, kept = (S.sem(n) for n in ("turned", "turn_kept", "multiplied", "kept"))
        rows_in, w_in, bias_in, stored = ([S.sem(f"{n}{j}") for j in range(LOOP_EXPERTS)]
                                          for n in ("rows_in", "w_in", "bias_in", "stored"))
        block = S.block()
        w_loops = None if resident else weights.rearrange("(l j) p f d -> l j p f d", j=LOOP_EXPERTS)
        bias_loops = bias.rearrange("(l j) d -> l j d", j=LOOP_EXPERTS)
        src_loops = src[0:L2_SLOTS, :].rearrange("(l j k r) d -> l j r k d", j=LOOP_EXPERTS, k=2, r=R)
        dst_loops = dst.rearrange("(l j k r) d -> l j r k d", j=LOOP_EXPERTS, k=2, r=R)

        def every_loop(engine, body):
            body(0, True)
            with engine.Fori(1, LOOPS) as l:
                body(l, False)

        @block.sync
        def _(sp):
            def body(l, first):
                for j in range(LOOP_EXPERTS):
                    if not first:
                        sp.wait_ge(multiplied, LOOP_HALVES * (l - 1) + 2 * j + 2)
                    sp.dma_start(rows[j][:, :, :], src_loops[l, j]).then_inc(rows_in[j], 16)
                    if not resident:
                        sp.dma_start(w[j][:, :, :], w_loops[l, j]).then_inc(w_in[j], 16)

            every_loop(sp, body)

        @block.gpsimd
        def _(pool):
            def store(l, j):
                pool.wait_ge(kept, LOOP_HALVES * l + 2 * j + 2)
                pool.dma_start(dst_loops[l, j], outs[j][:, :, :]).then_inc(stored[j], 16)

            def body(l, first):
                for j in range(LOOP_EXPERTS):
                    if not first:
                        store(l - 1, j)
                    pool.dma_start(bias_rows[j][:, :], bias_loops[l, j].partition_broadcast(R)).then_inc(bias_in[j], 16)

            every_loop(pool, body)
            for j in range(LOOP_EXPERTS):
                store(LOOPS - 1, j)
            for j in range(LOOP_EXPERTS):
                pool.wait_ge(stored[j], 16 * LOOPS)

        @block.tensor
        def _(pe):
            def turn(l, first, k):
                n = LOOP_HALVES * l + k
                if k % 2 == 0:
                    pe.wait_ge(rows_in[k // 2], 16 * (l + 1))
                if not first or k >= 2:
                    pe.wait_ge(turn_kept, n - 1)
                for f in range(F):
                    mm = pe.transpose(pT[:, k % 2, f * R:(f + 1) * R], rows[k // 2][:, k % 2, f * P:(f + 1) * P],
                                      K.ident[0:R, 0:R])
                mm.then_inc(turned, 1)

            def multiply(l, first, k):
                n = LOOP_HALVES * l + k
                pe.wait_ge(turn_kept, n + 1)
                if k % 2 == 0 and not resident:
                    pe.wait_ge(w_in[k // 2], 16 * (l + 1))
                if not first or k >= 2:
                    pe.wait_ge(kept, n - 1)
                for f in range(F):
                    expert_w = resident[0][:, LOOP_EXPERTS * l + k // 2, f, :] if resident else w[k // 2][:, f, :]
                    mm = pe.matmul(pY[0:R, k % 2, 0:width_out], rowsT[k % 2][:, f, :], expert_w,
                                   start=(f == 0), stop=(f == F - 1))
                mm.then_inc(multiplied, 1)

            def body(l, first):
                for k in range(LOOP_HALVES):
                    turn(l, first, k)
                    if k >= 1:
                        multiply(l, first, k - 1)
                multiply(l, first, LOOP_HALVES - 1)

            if resident:
                pe.wait_ge(*resident[1])
            every_loop(pe, body)

        @block.scalar
        def _(act):
            def body(l, first):
                for k in range(LOOP_HALVES):
                    n = LOOP_HALVES * l + k
                    act.wait_ge(turned, n + 1)
                    if not first or k >= 2:
                        act.wait_ge(multiplied, n - 1)
                    act.activation(rowsT[k % 2][:, :, :], pT[:, k % 2, 0:F * R].rearrange("p (f r) -> p f r", r=R),
                                   ACT.Copy).then_inc(turn_kept, 1)

            every_loop(act, body)

        @block.vector
        def _(dve):
            def body(l, first):
                for k in range(LOOP_HALVES):
                    n, j = LOOP_HALVES * l + k, k // 2
                    if k % 2 == 0:
                        dve.wait_ge(bias_in[j], 16 * (l + 1))
                        if not first:
                            dve.wait_ge(stored[j], 16 * l)
                    dve.wait_ge(multiplied, n + 1)
                    dve.tensor_tensor(outs[j][:, k % 2, :], pY[0:R, k % 2, 0:width_out], bias_rows[j][:, :], ALU.add)\
                       .then_inc(kept, 1)

            every_loop(dve, body)

def combine_top2(nc, K, A, last, attention, tiles):
    W = D if last else L2_H
    G = 1 if last else L2_GROUPS
    src = K.y_slots if last else K.h_slots
    RING = 2 * TPB
    with Stage(nc, f"combine{int(last)}") as S:
        got = [S.sb(f"got{c}", [P, RING, W]) for c in range(2)]
        mixed = S.sb("mixed", [P, RING, W])
        ln_w, ln_b = S.sb("ln_w", [P, G, W]), S.sb("ln_b", [P, G, W])
        stats, mv = S.sb("stats", [P, NT, 6]), S.sb("mv", [P, NT, 2])
        var, rstd, tmp = S.sb("var", [P, NT]), S.sb("rstd", [P, NT]), S.sb("tmp", [P, NT])
        attention.room(S)
        gathered, scattered = ([S.sem(f"{n}{c}") for c in range(NB)] for n in ("gathered", "scattered"))
        loaded, weighed, taken, order, normed, rectified, gated = (S.sem(n) for n in (
            "loaded", "weighed", "taken", "order", "normed", "rectified", "gated"))
        block = S.block()
        names = ("L2_ffn_ln_out_w", "L2_ffn_ln_out_b") if last else ("L2_ffn_ln_hid_w", "L2_ffn_ln_hid_b")
        lo, hi = tiles
        steps = list(range(lo, hi + 1))
        places = [steps[len(steps) * k // (2 * NB):len(steps) * (k + 1) // (2 * NB)] for k in range(2 * NB)]

        @block.sync
        def _(sp):
            for dst, n in zip((ln_w, ln_b), names):
                row = A[n] if not last else A[n].unsqueeze(0)
                sp.dma_start(dst[:, :, :], row.partition_broadcast(P)).then_inc(loaded, 16)
            sp.wait_ge(loaded, 32)

        @block.gpsimd
        def _(pool):
            def gather(c):
                if c >= 2:
                    pool.wait_ge(taken, TPB * (c - 1))
                for t in range(TPB * c, TPB * (c + 1)):
                    for k in range(2):
                        pool.indirect_dma_start(
                            out=got[k][:, t % RING, :], out_offset=None, in_=src,
                            in_offset=bass.IndirectOffsetOnAxis(ap=K.slot_i[:, k, t:t + 1], axis=0))\
                            .then_inc(gathered[c], 16)

            def scatter(c):
                for t in range(TPB * c, TPB * (c + 1)):
                    pool.wait_ge(rectified, t + 1)
                    for k in range(2):
                        pool.indirect_dma_start(
                            out=K.hid_slots, out_offset=bass.IndirectOffsetOnAxis(ap=K.place_i[:, k, t:t + 1], axis=0),
                            in_=mixed[:, t % RING, :], in_offset=None).then_inc(scattered[c], 16)

            for c in range(NB + 2):
                if c < NB:
                    gather(c)
                if c >= 2 and not last:
                    scatter(c - 2)
            if not last:
                for c in range(NB):
                    pool.wait_ge(scattered[c], 32 * TPB)

        @block.tensor
        def _(pe):
            for i in steps:
                attention.pe_step(pe, i, lo, hi)

        @block.vector
        def _(dve):
            chain = Chain(dve, order)

            def add_residual(c):
                ts = slice(TPB * c, TPB * (c + 1))
                dve.wait_ge(gated, c + 1)
                if c == NB - 1:
                    dve.wait_ge(attention.finished, NT)
                chain(dve.tensor_tensor(K.g[:, ts, :], K.g[:, ts, :], K.s[:, ts, :], ALU.mult))
                chain(dve.tensor_tensor(K.x[:, ts, :], K.x[:, ts, :], K.g[:, ts, :], ALU.add))
                for t in range(TPB * c, TPB * (c + 1)):
                    dve.bn_stats(K.stats[:, t, :], K.x[:, t, :])

            dve.wait_ge(loaded, 32)
            for c in range(NB):
                group = range(TPB * c, TPB * (c + 1))
                if c >= 2 and not last:
                    dve.wait_ge(scattered[c - 2], 32 * TPB)
                for t in group:
                    m = mixed[:, t % RING, :]
                    dve.wait_ge(weighed, t + 1)
                    dve.scalar_tensor_tensor(m, got[1][:, t % RING, :], K.coef[:, 1, t:t + 1],
                                             got[0][:, t % RING, :], ALU.mult, ALU.add).then_inc(taken, 1)
                if last:
                    dve.wait_ge(taken, TPB * (c + 1))
                    m = mixed[:, TPB * c % RING:TPB * c % RING + TPB, :]
                    chain(dve.tensor_tensor(m, m, K.xn[:, TPB * c:TPB * (c + 1), :], ALU.add))
                for t in group:
                    dve.wait_ge(taken, t + 1)
                    end = dve.bn_stats(stats[:, t, :], mixed[:, t % RING, :])
                chain(end)
                for i in places[2 * c]:
                    attention.dve_step(dve, i, lo, hi)
                for t in group:
                    end = dve.bn_aggr(mv[:, t, :], stats[:, t, :])
                chain(end)
                ts = slice(TPB * c, TPB * (c + 1))
                chain(dve.tensor_scalar(var[:, ts], mv[:, ts, 1], L2_LN_EPS, None, ALU.add))
                rsqrt(dve, chain, rstd[:, ts], var[:, ts], tmp[:, ts])
                g = 0 if last else c
                for t in group:
                    m = mixed[:, t % RING, :]
                    end = dve.scalar_tensor_tensor(m, m, mv[:, t, 0:1], ln_w[:, g, :], ALU.subtract, ALU.mult)
                chain(end)
                for t in group:
                    m = mixed[:, t % RING, :]
                    dve.scalar_tensor_tensor(K.g[:, t, :] if last else m, m, rstd[:, t:t + 1], ln_b[:, g, :],
                                             ALU.mult, ALU.add).then_inc(normed, 1)
                for i in places[2 * c + 1]:
                    attention.dve_step(dve, i, lo, hi)
                if last and c >= 1:
                    add_residual(c - 1)
            if last:
                add_residual(NB - 1)

        @block.scalar
        def _(act):
            def weigh(c):
                act.wait_ge(gathered[c], 32 * TPB)
                for t in range(TPB * c, TPB * (c + 1)):
                    act.activation(got[0][:, t % RING, :], got[0][:, t % RING, :], ACT.Copy,
                                   scale=K.coef[:, 0, t:t + 1]).then_inc(weighed, 1)

            weigh(0)
            for c in range(NB):
                for i in places[2 * c]:
                    attention.act_step(act, i, lo, hi)
                if not last:
                    for t in range(TPB * c, TPB * (c + 1)):
                        act.wait_ge(normed, t + 1)
                        act.activation(mixed[:, t % RING, :], mixed[:, t % RING, :], ACT.Relu).then_inc(rectified, 1)
                if c + 1 < NB:
                    weigh(c + 1)
                if last:
                    act.wait_ge(normed, TPB * (c + 1))
                    act.activation(K.g[:, TPB * c:TPB * (c + 1), :], K.g[:, TPB * c:TPB * (c + 1), :], ACT.Silu)\
                       .then_inc(gated, 1)
                for i in places[2 * c + 1]:
                    attention.act_step(act, i, lo, hi)


def layer2(nc, K, A):
    with Stage(nc, "single") as S:
        attention = SingleHeadAttention(nc, K, S, K.w["L2_Wq"], K.w["L2_Wk"], K.w["L2_Wv"], K.col["L2_bq"],
                                        K.col["L2_bk"], K.row["L2_bv"])
        with Stage(nc, "first") as first:
            w1, w1_in = first.sb("w1", [D, L2_E, 1, L2_H]), first.sem("w1_in")
            loads = [(w1[:, e:e + LOOP_EXPERTS], A["L2_W1"][:, e:e + LOOP_EXPERTS], w1_in)
                     for e in range(0, L2_E, LOOP_EXPERTS)]
            route_top2(nc, K, A, attention, (0, 8), loads)
            expert_pass(nc, K, "experts2a", K.x_slots, None, A["L2_ffn_b1"], D, L2_H, K.h_slots,
                        resident=(w1, (w1_in, 16 * len(loads))))
        combine_top2(nc, K, A, False, attention, (8, 15))
        expert_pass(nc, K, "experts2b", K.hid_slots, A["L2_W2"], A["L2_ffn_b2"], L2_H, D, K.y_slots)
        combine_top2(nc, K, A, True, attention, (15, 16))


L3_E, L3_H = 8, 512
L3_F = L3_H // P
L3_TILES = NT + L3_E - 1


class Top1Scatter:

    def __init__(self, nc, K):
        self.K, self.scattered = K, nc.alloc_semaphore("scattered3")

    def start(self, pool):
        pool.wait_ge(self.K.cleared, self.K.clears)
        for t in range(NT):
            pool.indirect_dma_start(
                out=self.K.x3_slots, out_offset=bass.IndirectOffsetOnAxis(ap=self.K.slot3_i[:, t:t + 1], axis=0),
                in_=self.K.xn[:, t, :], in_offset=None).then_inc(self.scattered, 16)

    def finish(self, pool):
        pool.wait_ge(self.scattered, 16 * NT)


def experts_top1(nc, K, out):
    LAST = L3_TILES - 1
    with Stage(nc, "experts3") as S:
        rows, rowsT = [S.sb(f"rows{n}", [P, D]) for n in range(2)], S.sb("rowsT", [P, 2, P])
        inner, innerT, outs = S.sb("inner", [P, 2, L3_H]), S.sb("innerT", [P, 2, L3_H]), S.sb("outs", [P, 2, D])
        got, gate = S.sb("got", [P, NT, D]), S.sb("gate", [P, NT, D])
        sums, den = S.sb("sums", [P, T]), S.sb("den", [P, T])
        pT, pH, pI, pY = (S.ps(n, [P, 2, BLK]) for n in ("pT", "pH", "pI", "pY"))
        turned, turn_kept, opened, biased, inner_turned, rectified, closed, kept, weighed = (
            S.sem(n) for n in ("turned", "turn_kept", "opened", "biased", "inner_turned", "rectified", "closed", "kept",
                               "weighed"))
        heads_in, inverted, scaled, projected, s_kept, gated, order, summed, result_stored = (
            S.sem(n) for n in ("heads_in", "inverted", "scaled", "projected", "s_kept", "gated", "order", "summed",
                               "result_stored"))
        rows_in, stored = ([S.sem(f"{n}{k}") for k in range(2)] for n in ("rows_in", "stored"))
        gathered = [S.sem(f"gathered{c}") for c in range(NB)]
        block = S.block()
        slots = K.x3_slots.rearrange("(j p) d -> j p d", p=P)
        out_slots = K.y3_slots.rearrange("(j p) d -> j p d", p=P)
        out_rows = out.rearrange("(t p) d -> p t d", p=P)
        pS = [pT[:, 0, :], pT[:, 1, :], pH[:, 0, :], pH[:, 1, :]]

        def every_tile(engine, body):
            body(0, 0)
            body(0, 1)
            with engine.Fori(1, LAST // 2) as i:
                body(i, 0)
                body(i, 1)
            body(LAST // 2, 0)

        def reused(i):
            return not isinstance(i, int) or i > 0

        def following(i, n):
            i, n = (i, 1) if n == 0 else (i + 1, 0)
            return [(i, n)] if not isinstance(i, int) or 2 * i + n < L3_TILES else []

        def expert(engine, i, n):
            return engine.value_load(K.tile_expert[0:1, bass.ds(2 * i + n, 1)], min_val=0, max_val=L3_E - 1)

        @block.sync
        def _(sp):
            def load(i, n):
                if reused(i):
                    sp.wait_ge(turned, 2 * i + n - 1)
                sp.dma_start(rows[n][:, :], slots[2 * i + n]).then_inc(rows_in[n], 16)

            sp.dma_start(sums[:, :], K.head_out[:, 0:HD, :]).then_inc(heads_in, 16)
            sp.dma_start(den[:, :], K.head_out[:, HD:HD + 1, :].broadcast_to([HEADS, HD, T])).then_inc(heads_in, 16)
            every_tile(sp, load)
            for c in range(NB):
                ts = slice(c * TPB, (c + 1) * TPB)
                sp.wait_ge(summed, c + 1)
                sp.dma_start(out_rows[:, ts, :], K.x[:, ts, :]).then_inc(result_stored, 16)
            sp.wait_ge(result_stored, 16 * NB)

        @block.gpsimd
        def _(pool):
            def store(i, n):
                pool.wait_ge(kept, 2 * i + n + 1)
                pool.dma_start(out_slots[2 * i + n], outs[:, n, :]).then_inc(stored[n], 16)

            every_tile(pool, store)
            for n in range(2):
                pool.wait_ge(stored[n], 16 * len(range(n, L3_TILES, 2)))
            for t in range(NT):
                pool.indirect_dma_start(
                    out=got[:, t, :], out_offset=None, in_=K.y3_slots,
                    in_offset=bass.IndirectOffsetOnAxis(ap=K.slot3_i[:, t:t + 1], axis=0))\
                    .then_inc(gathered[t // TPB], 16)

        @block.tensor
        def _(pe):
            def turn(i, n):
                if reused(i):
                    pe.wait_ge(turn_kept, 2 * i + n - 1)
                pe.wait_ge(rows_in[n], 16 * (i + 1))
                pe.transpose(pT[:, n, 0:P], rows[n][:, :], K.ident[:, :]).then_inc(turned, 1)

            def open_tile(i, n):
                e = expert(pe, i, n)
                if reused(i):
                    pe.wait_ge(biased, 2 * i + n - 1)
                pe.wait_ge(turn_kept, 2 * i + n + 1)
                pe.matmul(pH[:, n, :], rowsT[:, n, :], K.w1_3[:, e, :], start=True, stop=True).then_inc(opened, 1)

            def turn_inner(i, n):
                if reused(i):
                    pe.wait_ge(rectified, 2 * i + n - 1)
                pe.wait_ge(biased, 2 * i + n + 1)
                for f in range(L3_F):
                    mm = pe.transpose(pI[:, n, f * P:(f + 1) * P], inner[:, n, f * P:(f + 1) * P], K.ident[:, :])
                mm.then_inc(inner_turned, 1)

            def close_tile(i, n):
                e = expert(pe, i, n)
                if reused(i):
                    pe.wait_ge(kept, 2 * i + n - 1)
                pe.wait_ge(rectified, 2 * i + n + 1)
                for f in range(L3_F):
                    mm = pe.matmul(pY[:, n, 0:D], innerT[:, n, f * P:(f + 1) * P], K.w2_3[:, e, f, :],
                                   start=(f == 0), stop=(f == L3_F - 1))
                mm.then_inc(closed, 1)

            def body(i, n):
                nxt = following(i, n)
                for k in nxt:
                    turn(*k)
                turn_inner(i, n)
                for k in nxt:
                    open_tile(*k)
                close_tile(i, n)

            pe.wait_ge(K.l3_loaded, L3_LOADS)
            turn(0, 0)
            open_tile(0, 0)
            every_tile(pe, body)
            pe.wait_ge(turn_kept, L3_TILES)
            pe.wait_ge(biased, L3_TILES)
            for b in range(NB):
                pe.wait_ge(scaled, b + 1)
                for t in range(TPB):
                    tok = slice(b * BLK + t * P, b * BLK + (t + 1) * P)
                    mm = pe.matmul(pS[b][:, t * P:(t + 1) * P], sums[:, tok], K.w["L3_attn_ow"][:, :],
                                   start=True, stop=True)
                mm.then_inc(projected, 1)

        @block.scalar
        def _(act):
            def keep_turned(i, n):
                if reused(i):
                    act.wait_ge(opened, 2 * i + n - 1)
                act.wait_ge(turned, 2 * i + n + 1)
                act.activation(rowsT[:, n, :], pT[:, n, 0:P], ACT.Copy).then_inc(turn_kept, 1)

            def body(i, n):
                for k in following(i, n):
                    keep_turned(*k)
                if reused(i):
                    act.wait_ge(closed, 2 * i + n - 1)
                act.wait_ge(inner_turned, 2 * i + n + 1)
                act.activation(innerT[:, n, :], pI[:, n, :], ACT.Relu).then_inc(rectified, 1)

            keep_turned(0, 0)
            every_tile(act, body)
            for b in range(NB):
                act.wait_ge(projected, b + 1)
                act.activation(K.s[:, b * TPB:(b + 1) * TPB, :], pS[b].rearrange("p (t d) -> p t d", d=D), ACT.Copy)\
                   .then_inc(s_kept, 1)
            for c in range(NB):
                act.wait_ge(weighed, (c + 1) * TPB)
                act.activation(gate[:, c * TPB:(c + 1) * TPB, :], K.g[:, c * TPB:(c + 1) * TPB, :], ACT.Silu)\
                   .then_inc(gated, 1)

        @block.vector
        def _(dve):
            def add_bias(i, n):
                e = expert(dve, i, n)
                if reused(i):
                    dve.wait_ge(inner_turned, 2 * i + n - 1)
                dve.wait_ge(opened, 2 * i + n + 1)
                dve.tensor_tensor(inner[:, n, :], pH[:, n, :], K.b1_3[:, e, :], ALU.add).then_inc(biased, 1)

            def body(i, n):
                for k in following(i, n):
                    add_bias(*k)
                e = expert(dve, i, n)
                if reused(i):
                    dve.wait_ge(stored[n], 16 * i)
                dve.wait_ge(closed, 2 * i + n + 1)
                dve.tensor_tensor(outs[:, n, :], pY[:, n, 0:D], K.b2_3[:, e, :], ALU.add).then_inc(kept, 1)

            dve.wait_ge(K.l3_loaded, L3_LOADS)
            add_bias(0, 0)
            every_tile(dve, body)
            chain = Chain(dve, order)
            dve.wait_ge(heads_in, 32)
            for b in range(NB):
                cols = slice(b * BLK, (b + 1) * BLK)
                dve.reciprocal(den[:, cols], den[:, cols]).then_inc(inverted, 1)
                dve.wait_ge(inverted, b + 1)
                dve.tensor_tensor(sums[:, cols], sums[:, cols], den[:, cols], ALU.mult).then_inc(scaled, 1)
            for c in range(NB):
                dve.wait_ge(gathered[c], 16 * TPB)
                for t in range(c * TPB, (c + 1) * TPB):
                    dve.tensor_scalar(K.g[:, t, :], got[:, t, :], K.gate[:, t:t + 1], None, ALU.mult)\
                       .then_inc(weighed, 1)
                ts = slice(c * TPB, (c + 1) * TPB)
                dve.wait_ge(s_kept, c + 1)
                dve.wait_ge(gated, c + 1)
                chain(dve.tensor_tensor(gate[:, ts, :], gate[:, ts, :], K.s[:, ts, :], ALU.mult))
                dve.tensor_tensor(K.x[:, ts, :], K.x[:, ts, :], gate[:, ts, :], ALU.add).then_inc(summed, 1)


SQUARES = ("L0_attn_Wq", "L0_attn_Wk", "L0_attn_Wv", "L0_attn_Wo", "L0_ffn_weight", "L0_ffn_aux_weight1",
           "L0_ffn_aux_weight2", "L1_attn_Wq", "L1_attn_Wk", "L1_attn_Wv", "L2_Wq", "L2_Wk", "L2_Wv", "L3_attn_qw",
           "L3_attn_kw", "L3_attn_vw", "L3_attn_ow", "L3_qw_swapped", "L3_kw_swapped", "sgate1", "sup1", "sdown1")
NARROW = {"L0_attn_bq": 1, "L0_attn_bk": 1, "L1_attn_bq": 1, "L1_attn_bk": 1, "L2_bq": 1, "L2_bk": 1,
          "c_iota": L1_E, "c_floor": NT, "c_after": NT, "wr1": L1_E, "wg2": L2_E, "wr3": L3_E}
ROWS = {"L0_attn_bv": D, "L0_attn_bo": D, "L0_ffn_bias": D, "L1_attn_bv": D, "L1_ffn_e_score_bias": L1_E, "L2_bv": D,
        "L3_ffn_br": L3_E}


def recurrent_layers(nc, A, out):
    with ExitStack() as ctx:
        def sb(name, shape, dt=F32):
            return ctx.enter_context(nc.sbuf_tensor(f"k_{name}", list(shape), dt))

        def dram(name, shape, dt=F32):
            return nc.dram_tensor(f"k_{name}_dram", tuple(shape), dt, kind="Internal").ap()

        K = Kept()
        K.x, K.xn, K.s, K.g, K.v = (sb(n, [P, NT, D]) for n in ("x", "xn", "s", "g", "v"))
        K.xnT = sb("xnT", [D, T])
        K.ident = sb("ident", [P, P])
        K.ident_b, K.above_b, K.ones_b, K.neg_above, K.neg_below = (
            sb(n, [P, P], BF16) for n in ("ident_b", "above_b", "ones_b", "neg_above", "neg_below"))
        K.squares = sb("squares", [D, len(SQUARES), D])
        K.w = {n: K.squares[:, i, :] for i, n in enumerate(SQUARES)}
        K.narrow = sb("narrow", [P, sum(NARROW.values())])
        K.col, at = {}, 0
        for n, width in NARROW.items():
            K.col[n] = K.narrow[:, at:at + width]
            at += width
        K.iota, K.floor, K.after = K.col["c_iota"], K.col["c_floor"], K.col["c_after"]
        K.wr1, K.wg2, K.wr3 = K.col["wr1"], K.col["wg2"], K.col["wr3"]
        K.sgate1, K.sup1, K.sdown1 = K.w["sgate1"], K.w["sup1"], K.w["sdown1"]
        K.rows_of = sb("rows_of", [P, sum(ROWS.values())])
        K.row, at = {}, 0
        for n, width in ROWS.items():
            K.row[n] = K.rows_of[:, at:at + width]
            at += width
        K.stats = sb("stats", [P, NT, 6])
        K.coef = sb("coef", [P, 2, NT])
        K.slot_i, K.place_i = sb("slot_i", [P, 2, NT], I32), sb("place_i", [P, 2, NT], I32)
        K.parts = [dram(f"parts{w}", (HEADS, PARTS, HD, T), BF16) for w in range(2)]
        K.head_out = dram("head_out", (HEADS, HD + 1, T))
        slots_x, slots_hid = (dram(n, ((L2_SLOTS + 2 * T) * w,)) for n, w in (("x_slots", D), ("hid_slots", L2_H)))
        K.x_slots, K.hid_slots = (a.rearrange("(n d) -> n d", d=w) for a, w in ((slots_x, D), (slots_hid, L2_H)))
        K.h_slots, K.y_slots = dram("h_slots", (L2_SLOTS, L2_H)), dram("y_slots", (L2_SLOTS, D))
        slots_x3 = dram("x3_slots", (L3_TILES * P * D,))
        K.x3_slots, K.y3_slots = slots_x3.rearrange("(n d) -> n d", d=D), dram("y3_slots", (L3_TILES * P, D))
        K.to_clear = [a[0:n * w].rearrange("(p c) -> p c", p=P) for a, n, w in (
            (slots_x, L2_SLOTS, D), (slots_hid, L2_SLOTS, L2_H), (slots_x3, L3_TILES * P, D))]
        K.slot3_i, K.gate = sb("slot3_i", [P, NT], I32), sb("gate", [P, NT])
        K.tile_expert = sb("tile_expert", [P, L3_TILES], I32)
        K.weights_loaded, K.l1_loaded, K.rope_loaded, K.l3_loaded, K.cleared = (
            nc.alloc_semaphore(n) for n in ("weights_loaded", "l1_loaded", "rope_loaded", "l3_loaded", "cleared"))
        K.clears = 16 * sum(-(-a.shape[1] // CLEAR) for a in K.to_clear)

        with ExitStack() as layer1:
            def sb1(name, shape, dt=F32):
                return layer1.enter_context(nc.sbuf_tensor(f"k_{name}", list(shape), dt))

            K.zeros = sb1("zeros", [P, CLEAR])
            K.combT, K.sel = sb1("combT", [PARTS * L1_E, T], BF16), sb1("sel", [PARTS * L1_E, L1_J * P], BF16)
            K.row_den, K.row_zero, K.row_inv, K.row_weight = (
                sb1(n, [P, NT]) for n in ("row_den", "row_zero", "row_inv", "row_weight"))
            K.gate1, K.up1, K.down1 = sb1("gate1", [D, L1_E * L1_I]), sb1("up1", [D, L1_E * L1_I]), sb1(
                "down1", [P, L1_J, D])
            load_constants(nc, K, A)
            norm(nc, K, 0)
            head_projections(nc, K, 0, K.w["L0_attn_Wq"], K.w["L0_attn_Wk"], K.w["L0_attn_Wv"], K.col["L0_attn_bq"],
                             K.col["L0_attn_bk"], K.row["L0_attn_bv"])
            attention_heads(nc, K, 0, causal=False)
            finish_layer0(nc, K)
            loads = [(dst[:], A[n], K.l1_loaded) for dst, n in ((K.gate1, "gate1"), (K.up1, "up1"), (K.down1, "down1"))]
            loads += [(a[:, c:min(c + CLEAR, a.shape[1])], K.zeros[:, 0:min(CLEAR, a.shape[1] - c)], K.cleared)
                      for a in K.to_clear for c in range(0, a.shape[1], CLEAR)]
            norm(nc, K, 1, loads)
            attention_row_sums(nc, K, A, 1, K.w["L1_attn_Wq"], K.w["L1_attn_Wk"], K.w["L1_attn_Wv"], K.col["L1_attn_bq"],
                               K.col["L1_attn_bk"], K.row["L1_attn_bv"])
            ffn_top6(nc, K)
        norm(nc, K, 2)
        layer2(nc, K, A)
        K.cos, K.sin = sb("cos", [D, T]), sb("sin", [D, T])
        K.w1_3, K.w2_3 = sb("w1_3", [D, L3_E, L3_H]), sb("w2_3", [P, L3_E, L3_F, D])
        K.b1_3, K.b2_3 = sb("b1_3", [P, L3_E, L3_H]), sb("b2_3", [P, L3_E, D])
        norm(nc, K, 3, [(K.cos[:], A["c_cos"], K.rope_loaded), (K.sin[:], A["c_sin"], K.rope_loaded)])
        head_projections(nc, K, 3, K.w["L3_attn_qw"], K.w["L3_attn_kw"], K.w["L3_attn_vw"],
                         rope=(K.w["L3_qw_swapped"], K.w["L3_kw_swapped"], K.cos, K.sin),
                         loads=[(dst[:], src, K.l3_loaded) for dst, src in (
                             (K.w1_3, A["w1_3"]), (K.w2_3, A["w2_3"]), (K.b1_3, A["L3_ffn_b1"].partition_broadcast(P)),
                             (K.b2_3, A["L3_ffn_b2"].partition_broadcast(P)))])
        attention_heads(nc, K, 3, causal=True, scatter=Top1Scatter(nc, K))
        experts_top1(nc, K, out)


def constants():
    i, tok = np.arange(P), np.arange(NT)[None, :] * P + np.arange(P)[:, None]
    masks = np.stack([i[None, :] > i[:, None], i[None, :] < i[:, None], np.ones((P, P), bool)], axis=1)
    c = {"c_ident": np.eye(P), "c_masks": masks, "c_iota": np.broadcast_to(np.arange(L1_E), (P, L1_E)),
         "c_floor": np.where(tok == T - 1, LOWEST, 0.0), "c_after": T - 1 - tok}
    sel1 = np.zeros((PARTS, L1_E, L1_E, L1_I))
    sel1[:, np.arange(L1_E), np.arange(L1_E)] = 1
    c["c_sel1"] = sel1.reshape(PARTS * L1_E, L1_E * L1_I)
    group = np.arange(NT) // (NT // L2_GROUPS)
    c["c_base2"] = np.broadcast_to(2 * L2_HALF * np.arange(L2_E) + L2_CAP * group[:, None], (P, NT, L2_E))
    c["c_spare2"] = L2_SLOTS + T * np.arange(2)[None, :, None] + tok[:, None, :]
    f32 = np.float32
    freq = np.arange(T, dtype=f32)[None, :] * (f32(1) / f32(10000) ** (np.arange(0, HD, 2, dtype=f32) / f32(HD)))[:, None]
    sign = np.where(np.arange(HD) % 2 == 0, -1, 1)[:, None]
    c["c_cos"] = np.tile(np.repeat(np.cos(freq), 2, axis=0), (HEADS, 1))
    c["c_sin"] = np.tile(np.repeat(np.sin(freq), 2, axis=0) * sign, (HEADS, 1))
    c = {n: np.ascontiguousarray(a, dtype=np.float32) for n, a in c.items()}
    return c


def layouts(I):
    A = {n: a for n, a in I.items() if n[:3] in ("L0_", "L1_", "L3_") or n.startswith("L2_ffn")}
    A["x"] = A.pop("L0_attn_x").reshape(T, D)
    gate_up = A.pop("L1_ffn_gate_up_proj")
    A["gate1"] = gate_up[:, :L1_I].reshape(L1_E * L1_I, D).T
    A["up1"] = gate_up[:, L1_I:].reshape(L1_E * L1_I, D).T
    A["down1"] = A.pop("L1_ffn_down_proj").transpose(0, 2, 1).reshape(L1_J, P, D).transpose(1, 0, 2)
    for n, m in (("sgate1", "shared_gate_w"), ("sup1", "shared_up_w"), ("sdown1", "shared_down_w"),
                 ("wr1", "router_weight")):
        A[n] = A.pop("L1_ffn_" + m).T
    for n, m in enumerate("qkv"):
        A["L2_W" + m] = I["L2_attn_W_qkv"][n * D:(n + 1) * D].T
        A["L2_b" + m] = I["L2_attn_b_qkv"][n * D:(n + 1) * D]
    A["wg2"] = A.pop("L2_ffn_Wg")
    A["L2_W1"] = A.pop("L2_ffn_W1").reshape(L2_E, D, 1, L2_H).transpose(1, 0, 2, 3)
    A["L2_W2"] = A.pop("L2_ffn_W2").reshape(L2_E, L2_H // P, P, D).transpose(0, 2, 1, 3)
    for m in ("qw", "kw"):
        A[f"L3_{m}_swapped"] = A["L3_attn_" + m].reshape(D, D // 2, 2)[:, :, ::-1].reshape(D, D)
    A["wr3"] = A.pop("L3_ffn_Wr")
    A["w1_3"] = A.pop("L3_ffn_W1").transpose(1, 0, 2)
    A["w2_3"] = A.pop("L3_ffn_W2").reshape(L3_E, L3_F, P, D).transpose(2, 0, 1, 3)
    A.update(constants())
    A["squares"] = np.stack([A.pop(n) for n in SQUARES], axis=1)
    A["narrow"] = np.concatenate([A.pop(n).reshape(P, width) for n, width in NARROW.items()], axis=1)
    A["rows_of"] = np.concatenate([A.pop(n) for n in ROWS])
    return A


def kernel(**inputs):
    import concourse.bacc as _bacc
    from concourse.bass_utils import run_bass_kernel_spmd as _run

    nc = _bacc.Bacc("TRN2", target_bir_lowering=False, num_devices=1)
    arrays, A = {}, {}
    laid_out = layouts({n: np.asarray(a) for n, a in inputs.items()})
    for name, a in laid_out.items():
        a = np.ascontiguousarray(a)
        arrays[f"in_{name}_dram"] = a
        A[name] = nc.dram_tensor(f"in_{name}_dram", a.shape, mybir.dt.from_np(a.dtype), kind="ExternalInput").ap()
    out = nc.dram_tensor("out_0_dram", (T, D), F32, kind="ExternalOutput").ap()
    recurrent_layers(nc, A, out)
    r = _run(nc, [arrays], core_ids=[0])
    return r.results[0]["out_0_dram"].reshape(1, T, D)
```
